# Optimizing a Trainium2 kernel written in Bass

```python
import numpy as np
import jax
import jax.numpy as jnp

def _softmax(x, axis=-1):
    return jax.nn.softmax(x, axis=axis)

def _gelu(x):
    return jax.nn.gelu(x, approximate=True)

def _silu(x):
    return jax.nn.silu(x)

def _sigmoid(x):
    return jax.nn.sigmoid(x)

def _layernorm(x, axis=-1, eps=1e-05):
    m = jnp.mean(x, axis=axis, keepdims=True)
    v = jnp.var(x, axis=axis, keepdims=True)
    return (x - m) / jnp.sqrt(v + eps)

def _scatter_add(tgt, idx, src, axis=0):
    return tgt.at[idx].add(src)

def _segment_sum(src, seg, n):
    return jax.ops.segment_sum(src, seg, n)
kernel_name = 'mk_gnn_resnorm_d2_gnn_r64_e38f36'

def setup_inputs(seed: int=0):
    np.random.seed(seed)
    _w = jnp.asarray

    def _rec_inputs():
        import jax
        import jax.numpy as jnp
        _gk = jax.random.key(seed)
        x = -0.0003713 + 1 * jax.random.normal(jax.random.fold_in(_gk, 1), (50000, 256), jnp.float32)
        src = jax.random.randint(jax.random.fold_in(_gk, 2), (25000,), 0, 50000, jnp.int32)
        dst = jnp.minimum((50000 * jax.random.uniform(jax.random.fold_in(_gk, 3), (25000,)) ** 2.0).astype(jnp.int32), 49999)
        _o = jnp.argsort(dst, stable=True)
        src = src[_o]
        dst = dst[_o]
        edge_weight = 3.40706e-05 + 0.0312496 * jax.random.normal(jax.random.fold_in(_gk, 13), (25000,), jnp.float32)
        return (x, src, dst, edge_weight)
    x, src, dst, edge_weight = _rec_inputs()

    def _L0_gnn_setup():
        import jax, jax.numpy as jnp
        import numpy as np
        N = 50000
        E = 12500
        F = 256
        H = 256
        EPS = 1e-05

        def _gcn_norm(edge_index):
            loop = jnp.arange(N, dtype=edge_index.dtype)
            src = jnp.concatenate([edge_index[0], loop])
            dst = jnp.concatenate([edge_index[1], loop])
            deg = jax.ops.segment_sum(jnp.ones_like(dst, dtype=jnp.float32), dst, num_segments=N)
            dinv = deg ** (-0.5)
            norm = dinv[src] * dinv[dst]
            return (src, dst, norm)

        def _gcn_conv(h, W, b, src, dst, norm):
            h = h @ W
            msg = h[src] * norm[:, None]
            out = jax.ops.segment_sum(msg, dst, num_segments=N)
            return out + b

        def _bn(h, gamma, beta):
            m = jnp.mean(h, axis=0)
            v = jnp.var(h, axis=0)
            return (h - m) * jax.lax.rsqrt(v + EPS) * gamma + beta
        key = jax.random.key(seed)
        ks = jax.random.split(key, 16)
        x = jax.random.normal(ks[0], (N, F), dtype=jnp.float32)
        edge_index = jax.random.randint(ks[1], (2, E), 0, N, dtype=jnp.int32)

        def glorot(k, fan_in, fan_out):
            lim = float(np.sqrt(6.0 / (fan_in + fan_out)))
            return jax.random.uniform(k, (fan_in, fan_out), jnp.float32, -lim, lim)
        inp = {'x': x, 'edge_index': edge_index, 'W1': glorot(ks[2], F, H), 'b1': jnp.zeros((H,), jnp.float32), 'g1': jnp.ones((H,), jnp.float32), 'be1': jnp.zeros((H,), jnp.float32), 'W2': glorot(ks[3], H, H), 'b2': jnp.zeros((H,), jnp.float32), 'g2': jnp.ones((H,), jnp.float32), 'be2': jnp.zeros((H,), jnp.float32), 'W3': glorot(ks[4], H, H), 'b3': jnp.zeros((H,), jnp.float32), 'g3': jnp.ones((H,), jnp.float32), 'be3': jnp.zeros((H,), jnp.float32)}
        return inp
    _L0_gnn_all = _L0_gnn_setup()
    _L0_gnn_in = {k: v for k, v in _L0_gnn_all.items() if k in ('W1', 'b1', 'g1', 'be1', 'W2', 'b2', 'g2', 'be2', 'W3', 'b3', 'g3', 'be3')}
    del _L0_gnn_all

    def _L1_gnn_setup():
        import jax, jax.numpy as jnp
        import numpy as np
        N = 100000
        E = 50000
        C_IN = 256
        C_OUT = 256
        CONV_ORDER = 3
        key = jax.random.key(seed)
        k1, k2, k3, k4, k5 = jax.random.split(key, 5)
        x = jax.random.normal(k1, (N, C_IN), dtype=jnp.float32)
        edge_row = jax.random.randint(k2, (E,), 0, N, dtype=jnp.int32)
        edge_col = jax.random.randint(k3, (E,), 0, N, dtype=jnp.int32)
        edge_val = jax.random.normal(k4, (E,), dtype=jnp.float32) * (1.0 / 32.0)
        fan_in, fan_out = (C_IN, C_OUT)
        bound = 1.414 * np.sqrt(6.0 / (fan_in + fan_out))
        weight = jax.random.uniform(k5, (C_IN, C_OUT, 1 + CONV_ORDER), dtype=jnp.float32, minval=-bound, maxval=bound)
        return {'x': x, 'edge_row': edge_row, 'edge_col': edge_col, 'edge_val': edge_val, 'weight': weight}
    _L1_gnn_all = _L1_gnn_setup()
    _L1_gnn_in = {k: v for k, v in _L1_gnn_all.items() if k in ('weight',)}
    del _L1_gnn_all
    return {'x': x, 'src': src, 'dst': dst, 'edge_weight': edge_weight, 'L0_gnn_W1': _L0_gnn_in['W1'], 'L0_gnn_b1': _L0_gnn_in['b1'], 'L0_gnn_g1': _L0_gnn_in['g1'], 'L0_gnn_be1': _L0_gnn_in['be1'], 'L0_gnn_W2': _L0_gnn_in['W2'], 'L0_gnn_b2': _L0_gnn_in['b2'], 'L0_gnn_g2': _L0_gnn_in['g2'], 'L0_gnn_be2': _L0_gnn_in['be2'], 'L0_gnn_W3': _L0_gnn_in['W3'], 'L0_gnn_b3': _L0_gnn_in['b3'], 'L0_gnn_g3': _L0_gnn_in['g3'], 'L0_gnn_be3': _L0_gnn_in['be3'], 'L1_gnn_weight': _L1_gnn_in['weight']}

def reference(x, src, dst, edge_weight, L0_gnn_W1, L0_gnn_b1, L0_gnn_g1, L0_gnn_be1, L0_gnn_W2, L0_gnn_b2, L0_gnn_g2, L0_gnn_be2, L0_gnn_W3, L0_gnn_b3, L0_gnn_g3, L0_gnn_be3, L1_gnn_weight):
    import jax
    import jax.numpy as jnp

    def _L0_gnn_ref(x, edge_index, W1, b1, g1, be1, W2, b2, g2, be2, W3, b3, g3, be3):
        import jax, jax.numpy as jnp
        import numpy as np
        N = 50000
        E = 12500
        F = 256
        H = 256
        EPS = 1e-05

        def _gcn_norm(edge_index):
            loop = jnp.arange(N, dtype=edge_index.dtype)
            src = jnp.concatenate([edge_index[0], loop])
            dst = jnp.concatenate([edge_index[1], loop])
            deg = jax.ops.segment_sum(jnp.ones_like(dst, dtype=jnp.float32), dst, num_segments=N)
            dinv = deg ** (-0.5)
            norm = dinv[src] * dinv[dst]
            return (src, dst, norm)

        def _gcn_conv(h, W, b, src, dst, norm):
            h = h @ W
            msg = h[src] * norm[:, None]
            out = jax.ops.segment_sum(msg, dst, num_segments=N)
            return out + b

        def _bn(h, gamma, beta):
            m = jnp.mean(h, axis=0)
            v = jnp.var(h, axis=0)
            return (h - m) * jax.lax.rsqrt(v + EPS) * gamma + beta
        src, dst, norm = _gcn_norm(edge_index)
        h = _bn(_gcn_conv(x, W1, b1, src, dst, norm), g1, be1)
        h = _bn(_gcn_conv(h, W2, b2, src, dst, norm), g2, be2)
        h = _bn(_gcn_conv(h, W3, b3, src, dst, norm), g3, be3)
        return h

    def _L1_gnn_ref(x, edge_row, edge_col, edge_val, weight):
        import jax, jax.numpy as jnp
        import numpy as np
        N = 100000
        E = 50000
        C_IN = 256
        C_OUT = 256
        CONV_ORDER = 3
        'GCNLayer.forward: Chebyshev hops of sparse Laplacian + weighted combine.\n\n            x: [N, C_in]; laplacian in COO (edge_row, edge_col, edge_val); weight: [C_in, C_out, 1+K].\n            Returns [N, C_out].\n            '
        n = x.shape[0]

        def spmm(v):
            return jax.ops.segment_sum(edge_val[:, None] * v[edge_col], edge_row, num_segments=n)
        hops = []
        h = x
        for _ in range(CONV_ORDER):
            h = spmm(h)
            hops.append(h)
        X = jnp.stack([x] + hops, axis=2)
        return jnp.einsum('nik,iok->no', X, weight)
    edge_index = jnp.stack([src, dst])
    x = _layernorm(x + _L0_gnn_ref(x, edge_index, L0_gnn_W1, L0_gnn_b1, L0_gnn_g1, L0_gnn_be1, L0_gnn_W2, L0_gnn_b2, L0_gnn_g2, L0_gnn_be2, L0_gnn_W3, L0_gnn_b3, L0_gnn_g3, L0_gnn_be3), axis=-1)
    x = _layernorm(x + _L1_gnn_ref(x, src, dst, edge_weight, L1_gnn_weight), axis=-1)
    return x

_drawn_inputs = setup_inputs


def setup_inputs(seed=0):
    import zlib

    import numpy as np

    out = dict(_drawn_inputs(seed))
    spreads = {'L0_gnn_b1': (0.0, 2.0),
     'L0_gnn_g1': (1.0, 0.2),
     'L0_gnn_be1': (0.0, 2.0),
     'L0_gnn_b2': (0.0, 2.0),
     'L0_gnn_g2': (1.0, 0.2),
     'L0_gnn_be2': (0.0, 0.616),
     'L0_gnn_b3': (0.0, 2.0),
     'L0_gnn_g3': (1.0, 0.2),
     'L0_gnn_be3': (0.0, 0.1)}
    factors = {'edge_weight': 3.098}
    for name, (base, spread) in spreads.items():
        noise = np.random.default_rng([zlib.crc32(name.encode()), seed]).standard_normal(out[name].shape)
        drawn = base * np.exp(spread * noise) if base else spread * noise
        out[name] = jnp.asarray(drawn.astype(out[name].dtype))
    for name, factor in factors.items():
        out[name] = (out[name] * factor).astype(out[name].dtype)
    return out
```

```python
from contextlib import ExitStack

import numpy as np

import concourse.bass as bass
from concourse import mybir

ALU = mybir.AluOpType
ACT = mybir.ActivationFunctionType
AX = mybir.AxisListType
F32 = mybir.dt.float32
BF16 = mybir.dt.bfloat16
I32 = mybir.dt.int32

P = 128
N = 50000
E = 25000
F = 256
XW = F + 4
RING = 4
ET = 196
NSLOT = ET * P
EI = ET // RING
GROUPS = 98
NPAD = GROUPS * 4 * P
GI = GROUPS // 2
FAR = 1000000.0
EPS = 1e-5
NT = GROUPS * 4


def build_program(nc, d):
    with ExitStack() as ctx:
        def sb(name, shape, dt=F32):
            return ctx.enter_context(nc.sbuf_tensor(name, shape, dt))

        in_use = []

        def sem(name):
            in_use.append(nc.alloc_semaphore(name=name))
            return in_use[-1]

        def end_of_block():
            nc.clear_and_free_semaphores(in_use)
            in_use.clear()
            nc.all_engine_barrier()

        def sems(name, n=RING):
            return [sem(f"{name}{k}") for k in range(n)]

        def copy(out, a):
            return nc.vector.tensor_scalar(out, a, 1.0, None, ALU.mult)

        def dram(name, shape, dt=F32):
            return nc.dram_tensor(name, shape, dt, kind="Internal").ap()
        table = dram("node_table", (NPAD, 2))
        hist = dram("l0_rows", (NPAD + 2 * NSLOT, XW))
        cube = dram("l0_cube", (NSLOT, XW))
        zrow = dram("z_rows", (NPAD, F))
        hop1 = dram("hop1", (NSLOT, F))
        hop2 = dram("hop2", (NSLOT, F))

        srows = dram("sorted_rows", (NSLOT, 4))
        flat = dram("key_rows", (ET, P))
        table2 = dram("hop_table", (NPAD, 2))

        ident = sb("ident", [P, P])
        identb = sb("identb", [P, P], BF16)
        onesf = sb("onesf", [P, P])
        same = sb("same", [P, ET, P], BF16)
        keyJ = sb("keyJ", [P, ET])
        keyK = sb("keyK", [P, ET])
        other = sb("other", [P, ET + RING], I32)
        dstJ = sb("dstJ", [P, ET + RING], I32)
        wK = sb("wK", [P, ET])
        w23 = sb("w23", [P, ET])
        edge = sb("edge", [P, ET, 2])
        idx2 = sb("idx2", [P, ET + RING], I32)
        idx3 = sb("idx3", [P, ET + RING], I32)
        idxh = sb("idxh", [P, ET + RING], I32)
        sidx = sb("sidx", [P, ET + RING], I32)
        rep = sb("rep", [P, ET])
        dinvrep = sb("dinvrep", [P, ET])
        dinv2rep = sb("dinv2rep", [P, ET])
        cflag = sb("cflag", [1, ET])
        side = sb("side", [P, ET, 3])
        nonU = sb("nonU", [P, NT])
        gram = sb("gram", [P, 3, XW])
        iring = sb("iring", [P, RING], I32)
        unsorted = sb("unsorted", [1, 1], I32)

        def loop(eng, step, peel=1):
            for i in range(peel):
                step(i, i)
            with eng.Fori(peel, EI - 1) as i:
                step(i, None)
            step(EI - 1, EI - 1)

        def linker(dve, chain):
            n = [0]

            def link(ins):
                n[0] += 1
                ins.then_inc(chain, 1)
                dve.wait_ge(chain, n[0])
            return link

        def load_block():
            with ExitStack() as c2:
                def tmp(name, shape, dt=F32):
                    return c2.enter_context(nc.sbuf_tensor(f"l_{name}", shape, dt))
                dK, dJ, dP = tmp("dK", [P, ET], I32), tmp("dJ", [P, ET], I32), tmp("dP", [P, ET], I32)
                dPf, t0, t1 = tmp("dPf", [P, ET]), tmp("t0", [P, ET]), tmp("t1", [P, 1])
                pf = c2.enter_context(nc.psum_tensor("l_pf", [1, 1], F32))
                loaded, chain, bad, summed = sem("l_loaded"), sem("l_chain"), sem("l_bad"), sem("l_sum")
                with nc.Block() as block:
                    @block.sync
                    def _(sp):
                        for t, name in ((ident, "ident"), (onesf, "ones"), (dK, "dstK"), (dJ, "dstJ"), (dP, "dprev")):
                            sp.dma_start(t[:], d[name]).then_inc(loaded, 16)
                        sp.dma_start(other[:, 0:ET], d["srcK"]).then_inc(loaded, 16)

                    @block.vector
                    def _(dve):
                        v = nc.vector
                        link = linker(dve, chain)
                        for t in (other, dstJ, idx2, idx3, idxh, sidx):
                            link(v.memset(t[:, ET:ET + RING], 0))
                        dve.wait_ge(loaded, 16 * 6)
                        link(v.tensor_copy(identb[:], ident[:]))
                        link(v.tensor_copy(keyK[:], dK[:]))
                        link(v.tensor_copy(keyJ[:], dJ[:]))
                        link(v.tensor_copy(dPf[:], dP[:]))
                        link(v.tensor_tensor(rep[:], keyJ[:], dPf[:], ALU.not_equal))
                        link(v.tensor_tensor(t0[:], dPf[:], keyJ[:], ALU.is_gt))
                        v.tensor_reduce(t1[:], t0[:], AX.X, ALU.add).then_inc(bad, 1)
                        dve.wait_ge(summed, 1)
                        link(v.tensor_copy(unsorted[:], pf[:]))

                    @block.tensor
                    def _(pe):
                        pe.wait_ge(bad, 1)
                        pe.matmul(pf[:], t1[:], onesf[:, 0:1], start=True, stop=True).then_inc(summed, 1)

        def sort_block(name, keys, key_rows, others, weights):
            LO = NPAD // P
            with ExitStack() as c2:
                def tmp(x, shape, dt=F32):
                    return c2.enter_context(nc.sbuf_tensor(f"{name}_{x}", shape, dt))
                key, oth, wt = tmp("key", [P, ET], I32), tmp("oth", [P, ET], I32), tmp("wt", [P, ET])
                hi, lo, ti = tmp("hi", [P, ET]), tmp("lo", [P, ET]), tmp("ti", [P, ET], I32)
                keyf, rank, pos = tmp("keyf", [P, ET]), tmp("rank", [P, ET]), tmp("pos", [P, ET])
                tf = tmp("tf", [P, ET])
                iota, tri, rev = tmp("iota", [P, LO]), tmp("tri", [P, P]), tmp("rev", [P, P])
                triu = tmp("triu", [P, P])
                rowb = tmp("rowb", [P, RING, P], I32)
                ohl, ohh = tmp("ohl", [P, RING, LO], BF16), tmp("ohh", [P, RING, P], BF16)
                ohT = tmp("ohT", [P, 2, P])
                state = tmp("state", [P, 2, LO])
                base, incl, zrow_ = tmp("base", [P, LO]), tmp("incl", [P, LO]), tmp("zrow", [P, LO])
                junk, junk2 = tmp("junk", [P, RING, LO], BF16), tmp("junk2", [P, RING, P], BF16)
                rec = tmp("rec", [P, ET, 4])
                vring = tmp("vring", [P, RING, 4])
                sj = tmp("sj", [P, ET, 4])
                ph = c2.enter_context(nc.psum_tensor(f"{name}_ph", [P, LO], F32))
                pl = [c2.enter_context(nc.psum_tensor(f"{name}_pl{x}", [P, LO], F32)) for x in range(2)]
                pt = [c2.enter_context(nc.psum_tensor(f"{name}_pt{x}", [P, P], BF16)) for x in range(2)]
                po = c2.enter_context(nc.psum_tensor(f"{name}_po", [P, 1], F32))
                pr = [c2.enter_context(nc.psum_tensor(f"{name}_pr{x}", [P, LO], F32)) for x in range(2)]
                s = lambda x: sem(f"{name}_{x}")
                loaded, chain, begun = s("loaded"), s("chain"), s("begun")
                hot1, counted, based, offset = s("hot1"), s("counted"), s("based"), s("offset")
                hot2, turned, turnedc, looked, kept, updated, chosen, inrank = [s(x) for x in ("hot2", "turn", "turnc", "look", "kept", "upd", "chosen", "inrank")]
                row_in, put, put_ready, back, reved, kdone = sems(f"{name}_row"), sems(f"{name}_put"), s("putr"), s("back"), s("rev"), s("kdone")
                placed = s("placed")
                with nc.Block() as block:
                    @block.sync
                    def _(sp):
                        for t, a in ((key, keys), (oth, others), (wt, weights), (iota, d["iota"]), (tri, d["tri"]), (rev, d["rev"]), (triu, d["triu"])):
                            sp.dma_start(t[:], a).then_inc(loaded, 16)

                        def step(i, first):
                            for r in range(RING):
                                if not first:
                                    sp.wait_ge(inrank, 4 * i + r - 3)
                                sp.dma_start(rowb[:, r, :], key_rows[bass.ds(i * RING + r, 1), :].to_broadcast((P, P))).then_inc(row_in[r], 16)
                        step(0, True)
                        with sp.Fori(1, EI) as i:
                            step(i, False)

                    @block.tensor
                    def _(pe):
                        pe.wait_ge(based, 1)
                        pe.matmul(ph[:], zrow_[:, 0:P], zrow_[:], start=True, stop=False)
                        with pe.Fori(0, EI) as i:
                            for r in range(RING):
                                pe.wait_ge(hot1, 8 * i + 2 * r + 2)
                                pe.matmul(ph[:], ohh[:, r, :], ohl[:, r, :], start=False, stop=False).then_inc(counted, 1)
                        pe.matmul(ph[:], zrow_[:, 0:P], zrow_[:], start=False, stop=True).then_inc(counted, 1)
                        pe.wait_ge(based, 2)
                        pe.matmul(po[:], triu[:], incl[:, LO - 1:LO], start=True, stop=True).then_inc(offset, 1)
                        pe.wait_ge(based, 3)
                        pe.matmul(ph[:], ident[:], base[:], start=True, stop=True).then_inc(updated, 1)

                        def step(i, first):
                            for r in range(RING):
                                u = 4 * i + r
                                pe.wait_ge(hot2, 2 * (u + 1))
                                if not (first and r < 2):
                                    pe.wait_ge(turnedc, u - 1)
                                pe.transpose(pt[r % 2][:], ohh[:, r, :], identb[:]).then_inc(turned, 1)
                                pe.wait_ge(turnedc, u + 1)
                                pe.wait_ge(kept, u + 1)
                                if not (first and r < 2):
                                    pe.wait_ge(chosen, u - 1)
                                pe.matmul(ph[:], ohh[:, r, :], ohl[:, r, :], start=False, stop=True, skip_group_check=True).then_inc(updated, 1)
                                pe.matmul(pl[r % 2][:], ohT[:, r % 2, :], state[:, r % 2, :], start=True, stop=True).then_inc(looked, 1)
                        step(0, True)
                        with pe.Fori(1, EI) as i:
                            step(i, False)
                        pe.wait_ge(back, 16)
                        sjf = sj[:].rearrange("p u c -> p (u c)")
                        for x in range(2):
                            last = pe.matmul(pr[x][:], rev[:], sjf[:, LO * x:LO * x + LO], start=True, stop=True)
                        last.then_inc(reved, 1)

                    @block.scalar
                    def _(act):
                        def step(i, first):
                            for r in range(RING):
                                u = 4 * i + r
                                act.wait_ge(updated, u + 1)
                                if not (first and r < 2):
                                    act.wait_ge(looked, u - 1)
                                nc.scalar.activation(state[:, r % 2, :], ph[:], ACT.Copy).then_inc(kept, 1)
                                act.wait_ge(turned, u + 1)
                                nc.scalar.activation(ohT[:, r % 2, :], pt[r % 2][:], ACT.Copy).then_inc(turnedc, 1)
                        step(0, True)
                        with act.Fori(1, EI) as i:
                            step(i, False)

                    @block.vector
                    def _(dve):
                        v = nc.vector
                        link = linker(dve, chain)
                        link(v.memset(zrow_[:], 0.0))
                        dve.wait_ge(loaded, 16 * 7)
                        link(v.tensor_copy(keyf[:], key[:]))
                        link(v.tensor_scalar(ti[:], key[:], 127, None, ALU.bitwise_and))
                        link(v.tensor_copy(hi[:], ti[:]))
                        link(v.tensor_scalar(ti[:], key[:], 7, None, ALU.arith_shift_right))
                        link(v.tensor_copy(lo[:], ti[:]))
                        dve.sem_inc(based, 1)

                        def hot(u, r, ready):
                            v.tensor_scalar(ohl[:, r, :], iota[:], lo[:, bass.ds(u, 1)], None, ALU.is_equal).then_inc(ready, 1)
                            v.tensor_scalar(ohh[:, r, :], iota[:, 0:P], hi[:, bass.ds(u, 1)], None, ALU.is_equal).then_inc(ready, 1)

                        def count(i, first):
                            for r in range(RING):
                                if not first:
                                    dve.wait_ge(counted, 4 * i + r - 3)
                                hot(4 * i + r, r, hot1)
                        count(0, True)
                        with dve.Fori(1, EI) as i:
                            count(i, False)
                        dve.wait_ge(counted, ET + 1)
                        link(v.tensor_copy(base[:], ph[:]))
                        link(v.tensor_tensor_scan(incl[:], zrow_[:], base[:], 0.0, ALU.add, ALU.add))
                        dve.sem_inc(based, 1)
                        link(v.tensor_tensor(base[:], incl[:], base[:], ALU.subtract))
                        dve.wait_ge(offset, 1)
                        link(v.tensor_scalar(base[:], base[:], po[:, 0:1], None, ALU.add))
                        dve.sem_inc(based, 1)

                        def select(u, r):
                            dve.wait_ge(looked, u + 1)
                            v.scalar_tensor_tensor(junk[:, r, :], pl[r % 2][:], 1.0, ohl[:, r, :], ALU.mult, ALU.mult, accum_out=pos[:, bass.ds(u, 1)]).then_inc(chosen, 1)

                        def step(i, at):
                            for r in range(RING):
                                u = 4 * i + r
                                if at != 0:
                                    dve.wait_ge(chosen, u - 3)
                                    dve.wait_ge(looked, u - 3)
                                    dve.wait_ge(inrank, u - 3)
                                hot(u, r, hot2)
                                dve.wait_ge(row_in[r], 16 * i + 16)
                                v.scalar_tensor_tensor(junk2[:, r, :], rowb[:, r, :], keyf[:, bass.ds(u, 1)], tri[:], ALU.is_equal, ALU.mult, accum_out=rank[:, bass.ds(u, 1)]).then_inc(inrank, 1)
                                if not (at == 0 and r == 0):
                                    select(u - 1, (r - 1) % 4)
                        loop(dve, step)
                        select(ET - 1, 3)
                        dve.wait_ge(inrank, ET)
                        dve.wait_ge(chosen, ET)
                        link(v.tensor_tensor(pos[:], pos[:], rank[:], ALU.add))
                        link(v.tensor_copy(ti[:], pos[:]))
                        link(v.tensor_scalar(ti[:], ti[:], 127, None, ALU.bitwise_and))
                        link(v.tensor_copy(rank[:], ti[:]))
                        link(v.tensor_tensor(tf[:], pos[:], rank[:], ALU.subtract))
                        link(v.tensor_scalar(tf[:], tf[:], -1.0 / P, ET - 1.0, ALU.mult, ALU.add))
                        link(v.scalar_tensor_tensor(pos[:], rank[:], float(ET), tf[:], ALU.mult, ALU.add))
                        link(v.tensor_copy(idx2[:, 0:ET], pos[:]))
                        link(v.tensor_copy(rec[:, :, 0], keyf[:]))
                        link(v.tensor_copy(rec[:, :, 1], oth[:]))
                        link(v.tensor_copy(rec[:, :, 2], wt[:]))
                        link(v.memset(rec[:, :, 3], 0.0))

                        def put_step(i, first):
                            for r in range(RING):
                                if not first:
                                    dve.wait_ge(put[r], 16 * i)
                                copy(vring[:, r, :], rec[:, bass.ds(i * RING + r, 1), :].rearrange("p a c -> p (a c)")).then_inc(put_ready, 1)
                                copy(iring[:, r:r + 1], idx2[:, bass.ds(i * RING + r, 1)]).then_inc(put_ready, 1)
                        put_step(0, True)
                        with dve.Fori(1, EI) as i:
                            put_step(i, False)
                        link(v.memset(tf[:], -1.0))
                        dve.wait_ge(back, 16)
                        link(v.tensor_copy(keyJ[:], sj[:, :, 0]))
                        dve.sem_inc(placed, 1)
                        dve.wait_ge(reved, 1)
                        H = ET // 2
                        for x in range(2):
                            g = pr[x][:].rearrange("p (u c) -> p u c", c=4)
                            link(v.tensor_copy(keyK[:, H * x:H * x + H], g[:, :, 0]))
                            link(v.tensor_copy(other[:, H * x:H * x + H], g[:, :, 1]))
                            link(v.tensor_copy(wK[:, H * x:H * x + H], g[:, :, 2]))
                        dve.wait_ge(kdone, 32)
                        link(v.tensor_tensor(rep[:], keyJ[:], tf[:], ALU.not_equal))

                    @block.gpsimd
                    def _(pool):
                        top = pool.to_reg(NSLOT - 1)
                        with pool.Fori(0, EI) as i:
                            for r in range(RING):
                                pool.wait_ge(put_ready, 8 * i + 2 * r + 2)
                                pool.sem_inc(begun, 1)
                                pool.indirect_dma_start(srows, bass.IndirectOffsetOnAxis(ap=iring[:, r:r + 1], axis=0), vring[:, r, :], None,
                                                        bounds_check=top, oob_is_err=False).then_inc(put[r], 16)
                        for r in range(RING):
                            pool.wait_ge(put[r], 16 * EI)
                        pool.dma_start(sj[:].rearrange("p u c -> p (u c)"), srows.rearrange("(p u) c -> p (u c)", p=P)).then_inc(back, 16)
                        pool.wait_ge(back, 16)
                        pool.wait_ge(placed, 1)
                        pool.dma_start(tf[1:P, :], keyJ[0:P - 1, :]).then_inc(kdone, 16)
                        pool.dma_start(tf[0:1, 0:ET - 1], keyJ[P - 1:P, 1:ET]).then_inc(kdone, 16)

        def structure_block(name, out_table, with_degree):
            with ExitStack() as c2:
                def tmp(x, shape, dt=F32):
                    return c2.enter_context(nc.sbuf_tensor(f"{name}_{x}", shape, dt))
                rowb = tmp("rowb", [P, RING, P])
                onesb = tmp("onesb", [P, 1], BF16)
                turned = tmp("turned", [ET // 2, 2, P])
                cnt, cont, t0 = tmp("cnt", [P, ET]), tmp("cont", [P, ET]), tmp("t0", [P, ET])
                srow, crow = tmp("srow", [1, ET]), tmp("crow", [1, ET])
                tabv, slots = tmp("tabv", [P, ET, 2]), tmp("slots", [P, ET])
                vring = tmp("vring", [P, RING, 2])
                tfull = tmp("tfull", [P, NT, 2])
                ptr = c2.enter_context(nc.psum_tensor(f"{name}_ptr", [ET // 2, 2, P], F32))
                pcnt = c2.enter_context(nc.psum_tensor(f"{name}_pcnt", [P, 512], F32))
                pbc = c2.enter_context(nc.psum_tensor(f"{name}_pbc", [P, 2, 256], F32))
                s = lambda x: sem(f"{name}_{x}")
                begun, loaded, tinit, chain, flat_out = s("begun"), s("loaded"), s("tinit"), s("chain"), s("flat")
                turn, turnc, row_free, cnt_done, rows_ready, bc_done = [s(x) for x in ("turn", "turnc", "built", "cnt", "rows", "bc")]
                sq_in, sq_out, put_ready, look_idx, looked, tfl = [s(x) for x in ("sqin", "sqout", "put", "lidx", "looked", "tfl")]
                row_in, put, look = sems(f"{name}_row"), sems(f"{name}_puts"), sems(f"{name}_look")
                H = ET // 2
                with nc.Block() as block:
                    @block.sync
                    def _(sp):
                        sp.dma_start(slots[:], d["slots"]).then_inc(loaded, 16)
                        sp.wait_ge(turnc, 1)
                        sp.dma_start(flat.rearrange("(x u) p -> u x p", x=2), turned[:]).then_inc(flat_out, 16)
                        sp.wait_ge(flat_out, 16)

                        def step(i, first):
                            for r in range(RING):
                                if not first:
                                    sp.wait_ge(row_free, 4 * i + r - 3)
                                sp.dma_start(rowb[:, r, :], flat[bass.ds(i * RING + r, 1), :].to_broadcast((P, P))).then_inc(row_in[r], 16)
                        step(0, True)
                        with sp.Fori(1, EI) as i:
                            step(i, False)

                    @block.tensor
                    def _(pe):
                        for x in range(2):
                            last = pe.transpose(ptr[:, x, :], keyJ[:, H * x:H * x + H], ident[:])
                        last.then_inc(turn, 1)
                        if with_degree:
                            with pe.Fori(0, EI) as i:
                                for r in range(RING):
                                    pe.wait_ge(row_free, 4 * i + r + 1)
                                    pe.matmul(pcnt[:, bass.ds(i * RING + r, 1)], same[:, bass.ds(i * RING + r, 1), :].rearrange("p a j -> p (a j)"),
                                              onesb[:], start=True, stop=True).then_inc(cnt_done, 1)
                            pe.wait_ge(rows_ready, 1)
                            pe.matmul(pbc[:, 0, 0:ET], onesf[0:1, :], crow[:], start=True, stop=True).then_inc(bc_done, 1)
                            pe.matmul(pbc[:, 1, 0:ET], onesf[0:1, :], keyJ[0:1, :], start=True, stop=True).then_inc(bc_done, 1)

                    @block.scalar
                    def _(act):
                        if with_degree:
                            act.wait_ge(sq_in, 1)
                            nc.scalar.activation(t0[:], cnt[:], ACT.Sqrt).then_inc(sq_out, 1)

                    @block.vector
                    def _(dve):
                        v = nc.vector
                        link = linker(dve, chain)
                        link(v.memset(onesb[:], 1.0))
                        dve.wait_ge(turn, 1)
                        v.tensor_copy(turned[:], ptr[:]).then_inc(turnc, 1)
                        link(v.tensor_scalar(t0[:], keyJ[:], float(N), None, ALU.is_lt))
                        link(v.tensor_tensor(rep[:], rep[:], t0[:], ALU.mult))
                        link(v.tensor_scalar(t0[:], rep[:], -FAR, FAR, ALU.mult, ALU.add))
                        link(v.tensor_tensor(t0[:], t0[:], keyJ[:], ALU.add))
                        link(v.tensor_copy(sidx[:, 0:ET], t0[:]))
                        link(v.tensor_copy(dstJ[:, 0:ET], keyJ[:]))
                        link(v.memset(cflag[:], 0.0))
                        link(v.tensor_tensor(cflag[:, 0:ET - 1], keyK[0:1, 1:ET], keyJ[0:1, 0:ET - 1], ALU.is_equal))
                        dve.wait_ge(loaded, 16)
                        link(v.tensor_copy(tabv[:, :, 0], slots[:]))
                        with dve.Fori(0, EI) as i:
                            for r in range(RING):
                                dve.wait_ge(row_in[r], 16 * i + 16)
                                v.tensor_scalar(same[:, bass.ds(i * RING + r, 1), :].rearrange("p a j -> p (a j)"), rowb[:, r, :],
                                                keyK[:, bass.ds(i * RING + r, 1)], None, ALU.is_equal).then_inc(row_free, 1)
                        if with_degree:
                            link(v.tensor_copy(side[:], rep[:, :, None].to_broadcast((P, ET, 3))))
                            link(v.memset(srow[:], 0.0))
                            link(v.tensor_tensor(srow[:, 1:ET], keyJ[0:1, 1:ET], keyJ[0:1, 0:ET - 1], ALU.is_equal))
                            dve.wait_ge(cnt_done, ET)
                            link(v.tensor_copy(cnt[:], pcnt[:, 0:ET]))
                            link(v.tensor_tensor_scan(crow[:], srow[:], cnt[0:1, :], 0.0, ALU.mult, ALU.add))
                            dve.sem_inc(rows_ready, 1)
                            dve.wait_ge(bc_done, 2)
                            link(v.tensor_tensor(cont[:, 1:ET], keyJ[:, 1:ET], pbc[:, 1, 0:ET - 1], ALU.is_equal))
                            link(v.tensor_tensor(cont[:, 1:ET], cont[:, 1:ET], pbc[:, 0, 0:ET - 1], ALU.mult))
                            link(v.tensor_tensor(cnt[:, 1:ET], cnt[:, 1:ET], cont[:, 1:ET], ALU.add))
                            link(v.tensor_scalar(cnt[:], cnt[:], 1.0, None, ALU.add))
                            dve.sem_inc(sq_in, 1)
                            dve.wait_ge(sq_out, 1)
                            link(v.reciprocal(tabv[:, :, 1], t0[:]))
                            link(v.tensor_tensor(dinvrep[:], tabv[:, :, 1], rep[:], ALU.mult))
                            link(v.tensor_tensor(dinv2rep[:], tabv[:, :, 1], dinvrep[:], ALU.mult))
                        else:
                            link(v.memset(tabv[:, :, 1], 0.0))

                        def put_step(i, first):
                            for r in range(RING):
                                if not first:
                                    dve.wait_ge(put[r], 16 * i)
                                copy(vring[:, r, :], tabv[:, bass.ds(i * RING + r, 1), :].rearrange("p a c -> p (a c)")).then_inc(put_ready, 1)
                                copy(iring[:, r:r + 1], sidx[:, bass.ds(i * RING + r, 1)]).then_inc(put_ready, 1)
                        put_step(0, True)
                        with dve.Fori(1, EI) as i:
                            put_step(i, False)
                        for r in range(RING):
                            dve.wait_ge(put[r], 16 * EI)

                        for r in range(RING):
                            copy(iring[:, r:r + 1], other[:, r:r + 1]).then_inc(look_idx, 1)
                        with dve.Fori(0, EI) as i:
                            for r in range(RING):
                                dve.wait_ge(look[r], 16 * i + 16)
                                copy(edge[:, bass.ds(i * RING + r, 1), :].rearrange("p a c -> p (a c)"), vring[:, r, :]).then_inc(looked, 1)
                                copy(iring[:, r:r + 1], other[:, bass.ds(i * RING + r + RING, 1)]).then_inc(look_idx, 1)
                        dve.wait_ge(looked, ET)
                        dve.wait_ge(look_idx, ET + RING)
                        link(v.tensor_scalar(t0[:], edge[:, :, 0], float(NPAD), None, ALU.is_ge))
                        if with_degree:
                            link(v.tensor_copy(idx2[:, 0:ET], edge[:, :, 0]))
                            link(v.tensor_scalar(cnt[:], t0[:], float(NSLOT), None, ALU.mult))
                            link(v.tensor_tensor(cnt[:], cnt[:], edge[:, :, 0], ALU.add))
                            link(v.tensor_copy(idx3[:, 0:ET], cnt[:]))
                            dve.wait_ge(tfl, 16)
                            link(v.tensor_scalar(nonU[:], tfull[:, :, 0], float(NPAD), None, ALU.is_lt))
                        else:
                            link(v.tensor_tensor(w23[:], wK[:], t0[:], ALU.mult))
                            link(v.tensor_scalar(t0[:], t0[:], -FAR, FAR - NPAD, ALU.mult, ALU.add))
                            link(v.tensor_tensor(t0[:], t0[:], edge[:, :, 0], ALU.add))
                            link(v.tensor_copy(idxh[:, 0:ET], t0[:]))

                    @block.gpsimd
                    def _(pool):
                        top = pool.to_reg(NPAD - 1)
                        pool.dma_start(out_table, d["table0"]).then_inc(tinit, 16)
                        pool.wait_ge(tinit, 16)
                        with pool.Fori(0, EI) as i:
                            for r in range(RING):
                                pool.wait_ge(put_ready, 8 * i + 2 * r + 2)
                                pool.sem_inc(begun, 1)
                                pool.indirect_dma_start(out_table, bass.IndirectOffsetOnAxis(ap=iring[:, r:r + 1], axis=0), vring[:, r, :], None,
                                                        bounds_check=top, oob_is_err=False).then_inc(put[r], 16)
                        for r in range(RING):
                            pool.wait_ge(put[r], 16 * EI)
                        if with_degree:
                            pool.dma_start(tfull[:].rearrange("p (s q) c -> p s (q c)", q=4),
                                           out_table.rearrange("(s p q) c -> p s (q c)", p=P, q=4)).then_inc(tfl, 16)

                        def look_step(i, first):
                            for r in range(RING):
                                if not first:
                                    pool.wait_ge(looked, 4 * i + r - 3)
                                pool.wait_ge(look_idx, 4 * i + r + 1)
                                pool.sem_inc(begun, 1)
                                pool.indirect_dma_start(vring[:, r, :], None, out_table, bass.IndirectOffsetOnAxis(ap=iring[:, r:r + 1], axis=0),
                                                        bounds_check=top, oob_is_err=False).then_inc(look[r], 16)
                        look_step(0, True)
                        with pool.Fori(1, EI) as i:
                            look_step(i, False)

        def node_gram_block():
            with ExitStack() as c2:
                xin = c2.enter_context(nc.sbuf_tensor("g_xin", [P, 2, 4, F], F32))
                xm = c2.enter_context(nc.sbuf_tensor("g_xm", [P, 2, 4, XW], F32))
                zero = c2.enter_context(nc.sbuf_tensor("g_zero", [P, XW], F32))
                pg = [c2.enter_context(nc.psum_tensor(f"g_p{k}", [P, XW], F32)) for k in range(3)]
                x_in = sems("g_in", 2)
                masked = sem("g_masked")
                sided = sem("g_side")
                used = sem("g_used")
                stored = sems("g_st", 2)
                zr = sem("g_zr")
                out = sem("g_out")
                xg = d["x"].rearrange("(s p q) f -> s p (q f)", p=P, q=4)
                hg = hist[0:NPAD, :].rearrange("(s p q) f -> s p (q f)", p=P, q=4)
                with nc.Block() as block:
                    @block.sync
                    def _(sp):
                        def step(i, first):
                            for b in range(2):
                                if not first:
                                    sp.wait_ge(masked, 4 * (2 * i + b - 1))
                                sp.dma_start(xin[:, b].rearrange("p q f -> p (q f)"), xg[bass.ds(2 * i + b, 1), :, :].rearrange("a p f -> (a p) f")).then_inc(x_in[b], 16)
                        step(0, True)
                        with sp.Fori(1, GI) as i:
                            step(i, False)

                    @block.gpsimd
                    def _(pool):
                        with pool.Fori(0, GI) as i:
                            for b in range(2):
                                pool.wait_ge(masked, 4 * (2 * i + b + 1))
                                pool.wait_ge(sided, 2 * i + b + 1)
                                pool.dma_start(hg[bass.ds(2 * i + b, 1), :, :].rearrange("a p f -> (a p) f"), xm[:, b].rearrange("p q f -> p (q f)")).then_inc(stored[b], 16)
                        for b in range(2):
                            pool.wait_ge(stored[b], 16 * GI)

                    @block.scalar
                    def _(act):
                        def step(i, first):
                            for b in range(2):
                                act.wait_ge(x_in[b], 16 * i + 16)
                                if not first:
                                    act.wait_ge(used, 2 * i + b - 1)
                                    act.wait_ge(stored[b], 16 * i)
                                for q in range(4):
                                    nc.scalar.activation(xm[:, b, q, 0:F], xin[:, b, q, :], ACT.Copy, scale=nonU[:, bass.ds((2 * i + b) * 4 + q, 1)]).then_inc(masked, 1)
                        step(0, True)
                        with act.Fori(1, GI) as i:
                            step(i, False)

                    @block.vector
                    def _(dve):
                        nc.vector.memset(zero[:], 0.0).then_inc(zr, 1)

                        def step(i, first):
                            for b in range(2):
                                if not first:
                                    dve.wait_ge(used, 2 * i + b - 1)
                                    dve.wait_ge(stored[b], 16 * i)
                                copy(xm[:, b, :, F:XW], nonU[:, bass.ds((2 * i + b) * 4, 4), None].to_broadcast((P, 4, 4))).then_inc(sided, 1)
                        step(0, True)
                        with dve.Fori(1, GI) as i:
                            step(i, False)
                        dve.wait_ge(used, GROUPS + 1)
                        for k in range(3):
                            nc.vector.tensor_copy(gram[0:P if k < 2 else 4, k, 128 * k:XW], pg[k][0:P if k < 2 else 4, 128 * k:XW]).then_inc(out, 1)

                    @block.tensor
                    def _(pe):
                        pe.wait_ge(zr, 1)
                        open_gram(pe, pg, zero)
                        with pe.Fori(0, GI) as i:
                            for b in range(2):
                                pe.wait_ge(masked, 4 * (2 * i + b + 1))
                                pe.wait_ge(sided, 2 * i + b + 1)
                                for q in range(4):
                                    last = add_gram(pe, pg, xm[:, b, q, :])
                                last.then_inc(used, 1)
                        close_gram(pe, pg, zero).then_inc(used, 1)

        def open_gram(pe, pg, zero):
            for k in range(3):
                m = P if k < 2 else 4
                pe.matmul(pg[k][0:m, 128 * k:XW], zero[:, 0:m], zero[:, 128 * k:XW], start=True, stop=False)

        def add_gram(pe, pg, y):
            for k in range(3):
                m = P if k < 2 else 4
                last = pe.matmul(pg[k][0:m, 128 * k:XW], y[:, 128 * k:128 * k + m], y[:, 128 * k:XW], start=False, stop=False)
            return last

        def close_gram(pe, pg, zero):
            for k in range(3):
                m = P if k < 2 else 4
                last = pe.matmul(pg[k][0:m, 128 * k:XW], zero[:, 0:m], zero[:, 128 * k:XW], start=False, stop=True)
            return last

        def a_pass(k, gout):
            table_of = d["x"] if k == 1 else hist[0:NPAD + (k - 1) * NSLOT, :]
            width = F if k == 1 else XW
            idx = {1: other, 2: idx2, 3: idx3}[k]
            rows = NPAD + (k - 1) * NSLOT
            prev = None if k == 1 else hist[NPAD + (k - 2) * NSLOT:NPAD + (k - 1) * NSLOT, :].rearrange("(u p) f -> u p f", p=P)
            dest = (hist[NPAD + (k - 1) * NSLOT:NPAD + k * NSLOT, :] if k < 3 else cube).rearrange("(u p) f -> u p f", p=P)
            with ExitStack() as c2:
                def tmp(name, shape, dt=F32):
                    return c2.enter_context(nc.sbuf_tensor(f"a{k}_{name}", shape, dt))
                xs = tmp("xs", [P, RING, XW])
                xd = tmp("xd", [P, RING, XW])
                mw = tmp("mw", [P, RING, P])
                urow = tmp("urow", [1, RING, P])
                carry = tmp("carry", [1, XW])
                yt = tmp("yt", [P, RING, F + 1])
                y = tmp("y", [P, RING, XW])
                jring = tmp("jring", [P, RING], I32)
                zero = tmp("zero", [P, XW])
                ps = [c2.enter_context(nc.psum_tensor(f"a{k}_ps{b}", [P, 512], F32)) for b in range(2)]
                pg = [c2.enter_context(nc.psum_tensor(f"a{k}_pg{b}", [P, XW], F32)) for b in range(3)]
                s = lambda x: sem(f"a{k}_{x}")
                begun = s("begun")
                init, idx_ready, mw_ready, ps_ready, carry_ready = s("init"), s("idx"), s("mw"), s("ps"), s("carry")
                yt_ready, y_ready, gram_done, out = s("yt"), s("y"), s("gram"), s("out")
                got, self_in, stored = sems(f"a{k}_got"), sems(f"a{k}_self"), sems(f"a{k}_st")
                W1 = F + 1
                with nc.Block() as block:
                    @block.gpsimd
                    def _(pool):
                        top = pool.to_reg(rows - 1)
                        pool.wait_ge(init, 4)

                        def step(i, first):
                            for r in range(RING):
                                u = 4 * i + r
                                if not first:
                                    pool.wait_ge(ps_ready, u - 3)
                                pool.wait_ge(idx_ready, (2 if k == 1 else 1) * (u + 1))
                                pool.sem_inc(begun, 1)
                                pool.indirect_dma_start(xs[:, r, 0:width], None, table_of, bass.IndirectOffsetOnAxis(ap=iring[:, r:r + 1], axis=0),
                                                        bounds_check=top, oob_is_err=False).then_inc(got[r], 16)
                                if k == 1:
                                    if not first:
                                        pool.wait_ge(y_ready, 2 * (u - 3))
                                    pool.sem_inc(begun, 1)
                                    pool.indirect_dma_start(xd[:, r, 0:F], None, table_of, bass.IndirectOffsetOnAxis(ap=jring[:, r:r + 1], axis=0),
                                                            bounds_check=top, oob_is_err=False).then_inc(self_in[r], 16)
                        step(0, True)
                        with pool.Fori(1, EI) as i:
                            step(i, False)

                    @block.sync
                    def _(sp):
                        sp.wait_ge(init, 4)
                        if k > 1:
                            def load(u, r):
                                sp.dma_start(xd[:, r, :], prev[bass.ds(u, 1), :, :].rearrange("a p f -> (a p) f")).then_inc(self_in[r], 16)
                            for r in range(RING):
                                load(r, r)

                        def step(i, last):
                            for r in range(RING):
                                u = 4 * i + r
                                sp.wait_ge(y_ready, 2 * (u + 1))
                                sp.dma_start(dest[bass.ds(u, 1), :, :].rearrange("a p f -> (a p) f"), y[:, r, :]).then_inc(stored[r], 16)
                                if k > 1 and not last:
                                    load(u + RING, r)
                        with sp.Fori(0, EI - 1) as i:
                            step(i, False)
                        step(EI - 1, True)
                        for r in range(RING):
                            sp.wait_ge(stored[r], 16 * EI)

                    @block.scalar
                    def _(act):
                        def step(i, first):
                            for r in range(RING):
                                u = 4 * i + r
                                act.wait_ge(ps_ready, u + 1)
                                nc.scalar.activation(carry[:, 0:W1], ps[r % 2][0:1, 0:W1], ACT.Copy, scale=cflag[:, bass.ds(u, 1)]).then_inc(carry_ready, 1)
                                if not first:
                                    act.wait_ge(y_ready, 2 * (u - 3))
                                nc.scalar.activation(yt[:, r, :], ps[r % 2][:, 0:W1], ACT.Copy, scale=dinvrep[:, bass.ds(u, 1)]).then_inc(yt_ready, 1)
                        step(0, True)
                        with act.Fori(1, EI) as i:
                            step(i, False)

                    @block.vector
                    def _(dve):
                        v = nc.vector
                        v.memset(zero[:], 0.0).then_inc(init, 1)
                        v.memset(carry[:], 0.0).then_inc(init, 1)
                        v.memset(xs[:], 1.0).then_inc(init, 1)
                        v.memset(xd[:], 1.0).then_inc(init, 1)

                        def idx_copy(u, r):
                            copy(iring[:, r:r + 1], idx[:, bass.ds(u, 1)]).then_inc(idx_ready, 1)
                            if k == 1:
                                copy(jring[:, r:r + 1], dstJ[:, bass.ds(u, 1)]).then_inc(idx_ready, 1)

                        def prepare(u, r, first):
                            if not first:
                                dve.wait_ge(ps_ready, u - 3)
                            sm = same[:, bass.ds(u, 1), :].rearrange("p a j -> p (a j)")
                            v.tensor_scalar(mw[:, r, :], sm, edge[:, bass.ds(u, 1), 1], None, ALU.mult).then_inc(mw_ready, 1)
                            v.tensor_copy(urow[:, r, :], same[0:1, bass.ds(u, 1), :].rearrange("p a j -> p (a j)")).then_inc(mw_ready, 1)

                        def finish(u, r, first, i):
                            dve.wait_ge(self_in[r], 16 * i + 16)
                            dve.wait_ge(yt_ready, u + 1)
                            if not first:
                                dve.wait_ge(gram_done, u - 3)
                                dve.wait_ge(stored[r], 16 * i)
                            v.scalar_tensor_tensor(y[:, r, 0:W1], xd[:, r, 0:W1], dinv2rep[:, bass.ds(u, 1)], yt[:, r, :], ALU.mult, ALU.add).then_inc(y_ready, 1)
                            copy(y[:, r, W1:XW], side[:, bass.ds(u, 1), :].rearrange("p a c -> p (a c)")).then_inc(y_ready, 1)
                            if k < 3:
                                dve.wait_ge(y_ready, 2 * (u + 1))
                                copy(side[:, bass.ds(u, 1), 2 - k], y[:, r, F:W1]).then_inc(out, 1)
                            idx_copy(u + RING, r)

                        for r in range(RING):
                            idx_copy(r, r)
                        for r in range(2):
                            prepare(r, r, True)

                        def step(i, first, last):
                            for r in range(RING):
                                u = 4 * i + r
                                if not (last and r >= 2):
                                    prepare(u + 2, (r + 2) % 4, first and r < 2)
                                finish(u, r, first, i)
                        step(0, True, False)
                        with dve.Fori(1, EI - 1) as i:
                            step(i, False, False)
                        step(EI - 1, False, True)
                        dve.wait_ge(gram_done, ET + 1)
                        for b in range(3):
                            m = P if b < 2 else 4
                            v.tensor_tensor(gout[0:m, b, 128 * b:XW], gram[0:m, b, 128 * b:XW], pg[b][0:m, 128 * b:XW], ALU.add).then_inc(out, 1)

                    @block.tensor
                    def _(pe):
                        pe.wait_ge(init, 4)
                        open_gram(pe, pg, zero)

                        def step(i, first):
                            for r in range(RING):
                                u = 4 * i + r
                                pe.wait_ge(got[r], 16 * i + 16)
                                pe.wait_ge(mw_ready, 2 * (u + 1))
                                if not (first and r < 2):
                                    pe.wait_ge(yt_ready, u - 1)
                                pe.matmul(ps[r % 2][:, 0:W1], mw[:, r, :], xs[:, r, 0:W1], start=True, stop=False)
                                if not (first and r == 0):
                                    pe.wait_ge(y_ready, 2 * u)
                                    add_gram(pe, pg, y[:, (r - 1) % 4, :]).then_inc(gram_done, 1)
                                    pe.wait_ge(carry_ready, u)
                                pe.matmul(ps[r % 2][:, 0:W1], urow[:, r, :], carry[:, 0:W1], start=False, stop=True).then_inc(ps_ready, 1)
                        step(0, True)
                        with pe.Fori(1, EI) as i:
                            step(i, False)
                        pe.wait_ge(y_ready, 2 * ET)
                        add_gram(pe, pg, y[:, 3, :]).then_inc(gram_done, 1)
                        close_gram(pe, pg, zero).then_inc(gram_done, 1)

        wa = [[sb(f"w_{k}_{c}", [P, F]) for c in range(2)] for k in (1, 2, 3)]
        hc = sb("hc", [4, F])
        hmap = [sb(f"hmap{c}", [P, F]) for c in range(2)]
        gk = [sb(f"gram{k}", [P, 3, XW]) for k in (1, 2, 3)]

        kept_w = [sb(f"l1w{k}", [P, 2, F]) for k in range(4)]
        hsplit = sb("hsplit", [68, F], BF16)
        oneb = sb("oneb", [68, P], BF16)
        epsc = sb("epsc", [P, 1])

        def norm_block():
            with ExitStack() as c2:
                def tmp(name, shape, dt=F32):
                    return c2.enter_context(nc.sbuf_tensor(f"n_{name}", shape, dt))
                gb = tmp("gb", [P, 3, 2, F])
                wl = tmp("wl", [P, 3, 2, F])
                b1 = tmp("b1", [4, F])
                brow = tmp("brow", [1, 3, F])
                e3 = tmp("e3", [1, 4])
                e3c = tmp("e3c", [4, 1])
                w = [tmp(f"w{c}", [P if c < 2 else 4, F]) for c in range(3)]
                cov = [tmp(f"cov{c}", [P if c < 2 else 4, XW]) for c in range(3)]
                mbc = tmp("mbc", [P, 3, P])
                mrow = tmp("mrow", [1, XW])
                prod = [tmp(f"prod{c}", [P if c < 2 else 4, F]) for c in range(3)]
                mean = tmp("mean", [P, F])
                var = tmp("var", [P, F])
                sd = tmp("sd", [P, F])
                sc = tmp("sc", [P, F])
                shift = tmp("shift", [P, F])
                hT = tmp("hT", [P, 2, XW])
                hTc = tmp("hTc", [P, 2, 4])
                t4 = tmp("t4", [4, F])
                pa, pb, pc, pd = [c2.enter_context(nc.psum_tensor(f"n_p{x}", [P, 512], F32)) for x in "abcd"]
                ld, dv, pt, sq = sem("n_loaded"), sem("n_dve"), sem("n_pe"), sem("n_sqrt")
                chain = sem("n_chain")
                halves = "(c p) f -> p c f"
                hs = (P, P, 4)
                with nc.Block() as block:
                    @block.sync
                    def _(sp):
                        for k in range(3):
                            sp.dma_start(gb[:, k, 0, :], d[f"g{k + 1}"].to_broadcast((P, F))).then_inc(ld, 16)
                            sp.dma_start(gb[:, k, 1, :], d[f"be{k + 1}"].to_broadcast((P, F))).then_inc(ld, 16)
                            sp.dma_start(wl[:, k, :, :], d[f"W{k + 1}"].rearrange(halves, p=P)).then_inc(ld, 16)
                            sp.dma_start(brow[:, k, :], d[f"b{k + 1}"]).then_inc(ld, 16)
                        sp.dma_start(b1[:], d["b1"].to_broadcast((4, F))).then_inc(ld, 16)
                        sp.dma_start(e3[:], d["e3"]).then_inc(ld, 16)
                        sp.dma_start(e3c[:], d["e3c"]).then_inc(ld, 16)
                        for k in range(4):
                            sp.dma_start(kept_w[k][:], d["L1W"][k].rearrange(halves, p=P)).then_inc(ld, 16)

                    @block.scalar
                    def _(act):
                        for k in range(3):
                            act.wait_ge(dv, 7 * k + 5)
                            nc.scalar.activation(sd[:], var[:], ACT.Sqrt).then_inc(sq, 1)

                    @block.tensor
                    def _(pe):
                        pe.wait_ge(ld, 16 * 19)
                        for k in range(3):
                            g = gk[k]
                            pe.wait_ge(dv, 7 * k + 1)
                            pe.transpose(pa[:, 0:P], g[:, 0, P:2 * P], ident[:])
                            pe.transpose(pa[0:4, P:2 * P], g[:, 0, 2 * P:XW], ident[:])
                            pe.transpose(pa[0:4, 2 * P:3 * P], g[:, 1, 2 * P:XW], ident[:])
                            pe.transpose(pb[0:1, 0:P], g[:, 0, XW - 1:XW], ident[:])
                            pe.transpose(pb[0:1, P:2 * P], g[:, 1, XW - 1:XW], ident[:])
                            pe.transpose(pb[0:1, 2 * P:XW], g[0:4, 2, XW - 1:XW], ident[0:4, 0:4]).then_inc(pt, 1)
                            pe.wait_ge(dv, 7 * k + 2)
                            for c, p in enumerate((pa, pb, pc)):
                                last = pe.matmul(p[0:hs[c], 0:XW], mrow[:, P * c:P * c + hs[c]], mrow[:], start=True, stop=True)
                            last.then_inc(pt, 1)
                            pe.wait_ge(dv, 7 * k + 3)
                            for m, p in enumerate((pa, pb, pc, pd)):
                                for c in range(3):
                                    lhsT = cov[c][:, P * m:P * m + hs[m]] if m < 3 else mbc[0:hs[c], c, :]
                                    last = pe.matmul(p[0:hs[m] if m < 3 else P, 0:F], lhsT, w[c][:], start=(c == 0), stop=(c == 2))
                            last.then_inc(pt, 1)
                            pe.wait_ge(dv, 7 * k + 4)
                            for c in range(3):
                                last = pe.matmul(pa[:, 0:F], onesf[0:hs[c], :], prod[c][:], start=(c == 0), stop=(c == 2))
                            last.then_inc(pt, 1)
                            if k < 2:
                                pe.wait_ge(dv, 7 * k + 6)
                                for c, p in enumerate((pa, pb)):
                                    for m in range(3):
                                        last = pe.transpose(p[:, P * m:P * m + hs[m]], w[m][:, P * c:P * c + P], ident[0:hs[m], 0:hs[m]])
                                last.then_inc(pt, 1)
                                pe.wait_ge(dv, 7 * k + 7)
                                for m, p in enumerate((pa, pb, pc)):
                                    for c in range(2):
                                        lhsT = hT[:, c, P * m:P * m + P] if m < 2 else hTc[:, c, :]
                                        last = pe.matmul(p[0:hs[m], 0:F], lhsT, wl[:, k + 1, c, :], start=(c == 0), stop=(c == 1 and m < 2))
                                last = pe.matmul(pc[0:4, 0:F], e3[:], brow[:, k + 1, :], start=False, stop=True)
                                last.then_inc(pt, 1)

                    @block.vector
                    def _(dve):
                        v = nc.vector
                        n = [0]

                        def link(ins):
                            n[0] += 1
                            ins.then_inc(chain, 1)
                            dve.wait_ge(chain, n[0])
                        dve.wait_ge(ld, 16 * 19)
                        for c in range(2):
                            link(v.tensor_copy(w[c][:], wl[:, 0, c, :]))
                        link(v.tensor_scalar(w[2][:], b1[:], e3c[:], None, ALU.mult))
                        for k in range(3):
                            g = gk[k]
                            dve.sem_inc(dv, 1)
                            dve.wait_ge(pt, 6 * k + 1)
                            link(v.tensor_scalar(cov[0][:], g[:, 0, :], 1.0 / N, None, ALU.mult))
                            link(v.tensor_scalar(cov[1][:, 0:P], pa[:, 0:P], 1.0 / N, None, ALU.mult))
                            link(v.tensor_scalar(cov[1][:, P:XW], g[:, 1, P:XW], 1.0 / N, None, ALU.mult))
                            link(v.tensor_scalar(cov[2][:, 0:2 * P], pa[0:4, P:3 * P], 1.0 / N, None, ALU.mult))
                            link(v.tensor_scalar(cov[2][:, 2 * P:XW], g[0:4, 2, 2 * P:XW], 1.0 / N, None, ALU.mult))
                            link(v.tensor_scalar(mrow[:], pb[0:1, 0:XW], 1.0 / N, None, ALU.mult))
                            for c in range(3):
                                link(v.tensor_copy(mbc[0:hs[c], c, :], cov[c][:, XW - 1:XW].to_broadcast((hs[c], P))))
                            dve.sem_inc(dv, 1)
                            dve.wait_ge(pt, 6 * k + 2)
                            for c, p in enumerate((pa, pb, pc)):
                                link(v.tensor_tensor(cov[c][:], cov[c][:], p[0:hs[c], 0:XW], ALU.subtract))
                            dve.sem_inc(dv, 1)
                            dve.wait_ge(pt, 6 * k + 3)
                            for c, p in enumerate((pa, pb, pc)):
                                link(v.tensor_tensor(prod[c][:], w[c][:], p[0:hs[c], 0:F], ALU.mult))
                            link(v.tensor_copy(mean[:], pd[:, 0:F]))
                            dve.sem_inc(dv, 1)
                            dve.wait_ge(pt, 6 * k + 4)
                            link(v.tensor_scalar(var[:], pa[:, 0:F], 0.0, EPS, ALU.max, ALU.add))
                            dve.sem_inc(dv, 1)
                            dve.wait_ge(sq, k + 1)
                            link(v.reciprocal(sc[:], sd[:]))
                            link(v.tensor_tensor(sc[:], sc[:], gb[:, k, 0, :], ALU.mult))
                            link(v.tensor_tensor(shift[:], mean[:], sc[:], ALU.mult))
                            link(v.tensor_tensor(shift[:], gb[:, k, 1, :], shift[:], ALU.subtract))
                            for c in range(3):
                                link(v.tensor_tensor(w[c][:], w[c][:], sc[0:hs[c], :], ALU.mult))
                            link(v.scalar_tensor_tensor(w[2][:], shift[0:4, :], e3c[:], w[2][:], ALU.mult, ALU.add))
                            dve.sem_inc(dv, 1)
                            if k < 2:
                                dve.wait_ge(pt, 6 * k + 5)
                                link(v.memset(hTc[:], 0.0))
                                for c, p in enumerate((pa, pb)):
                                    link(v.tensor_copy(hT[:, c, :], p[:, 0:XW]))
                                    link(v.tensor_copy(hTc[:, c, 0:3], p[:, F + 1:XW]))
                                dve.sem_inc(dv, 1)
                                dve.wait_ge(pt, 6 * k + 6)
                                for c, p in enumerate((pa, pb, pc)):
                                    link(v.tensor_copy(w[c][:], p[0:hs[c], 0:F]))
                            else:
                                for c in range(2):
                                    link(v.tensor_copy(hmap[c][:], w[c][:]))
                                link(v.tensor_copy(hc[:], w[2][:]))
                                link(v.memset(hsplit[:], 0.0))
                                link(v.memset(oneb[:], 1.0))
                                link(v.memset(epsc[:], EPS))
                                for part in range(3):
                                    link(v.tensor_copy(hsplit[32 * part:32 * part + 4, :], w[2][:]))
                                    if part < 2:
                                        link(v.tensor_copy(t4[:], hsplit[32 * part:32 * part + 4, :]))
                                        link(v.tensor_tensor(w[2][:], w[2][:], t4[:], ALU.subtract))

        def dense_block(name, rows, w, constant, dest):
            B = 4
            with ExitStack() as c2:
                def tmp(x, shape, dt=F32):
                    return c2.enter_context(nc.sbuf_tensor(f"{name}_{x}", shape, dt))
                xin, t, o = [tmp(x, [P, 2, 4, F]) for x in ("xin", "t", "o")]
                xT = tmp("xT", [P, B, 2, P])
                st, mv, pad = tmp("st", [P, 4, 6]), tmp("mv", [P, 4, 2]), tmp("pad", [P, 1])
                sd, rs, nm = tmp("sd", [P, 4]), tmp("rs", [P, 4]), tmp("nm", [P, 4])
                pT = [c2.enter_context(nc.psum_tensor(f"{name}_pT{x}", [P, 2, P], F32)) for x in range(B)]
                pz = [c2.enter_context(nc.psum_tensor(f"{name}_pz{x}", [P, F], F32)) for x in range(B)]
                s = lambda x: sem(f"{name}_{x}")
                t_done, xt_ready, mm_done, add_done, st_done, mv_done, sd_done, r_done, rs_done, ready = [
                    s(x) for x in ("T", "xT", "mm", "add", "stats", "mv", "sd", "r", "rs", "ready")]
                x_in, stored = sems(f"{name}_in", 2), sems(f"{name}_st", 2)
                xg = rows.rearrange("(s p q) f -> s p (q f)", p=P, q=4)
                og = dest.rearrange("(s p q) f -> s p (q f)", p=P, q=4)
                rows_of = "a p f -> (a p) f"
                free = "p q f -> p (q f)"

                def ends(eng, step):
                    step(0, True, False)
                    with eng.Fori(1, GI - 1) as i:
                        step(i, False, False)
                    step(GI - 1, False, True)

                with nc.Block() as block:
                    @block.sync
                    def _(sp):
                        def load(g, b):
                            sp.dma_start(xin[:, b].rearrange(free), xg[bass.ds(g, 1), :, :].rearrange(rows_of)).then_inc(x_in[b], 16)
                        load(0, 0)
                        load(1, 1)

                        def step(i, first, last):
                            for b in range(2):
                                g = 2 * i + b
                                if not last:
                                    sp.wait_ge(add_done, 4 * (g + 1))
                                    load(g + 2, b)
                                if not (first and b == 0):
                                    sp.wait_ge(ready, 4 * g)
                                    sp.dma_start(og[bass.ds(g - 1, 1), :, :].rearrange(rows_of), o[:, 1 - b].rearrange(free)).then_inc(stored[1 - b], 16)
                        ends(sp, step)
                        sp.wait_ge(ready, NT)
                        sp.dma_start(og[GROUPS - 1], o[:, 1].rearrange(free)).then_inc(stored[1], 16)
                        for b in range(2):
                            sp.wait_ge(stored[b], 16 * GI)

                    @block.tensor
                    def _(pe):
                        def product(n, un, waits):
                            pe.wait_ge(xt_ready, un + 1)
                            if waits:
                                pe.wait_ge(add_done, un - B + 1)
                            for c in range(2):
                                last = pe.matmul(pz[n][:], xT[:, n, c, :], w[c], start=(c == 0), stop=(c == 1 and not constant))
                            if constant:
                                last = pe.matmul(pz[n][:], oneb[:], hsplit[:], start=False, stop=True)
                            last.then_inc(mm_done, 1)

                        def step(i, first, last):
                            for b in range(2):
                                for q in range(4):
                                    un = 8 * i + 4 * b + q
                                    if q == 0:
                                        pe.wait_ge(x_in[b], 16 * i + 16)
                                    if not (first and b == 0):
                                        pe.wait_ge(xt_ready, un - B + 1)
                                    pe.transpose(pT[q][:, 0, :], xin[:, b, q, 0:P], ident[:])
                                    pe.transpose(pT[q][:, 1, :], xin[:, b, q, P:F], ident[:]).then_inc(t_done, 1)
                                    if not (first and b == 0 and q == 0):
                                        product((q - 1) % 4, un - 1, not (first and 4 * b + q <= B))
                        ends(pe, step)
                        product(3, NT - 1, True)

                    @block.scalar
                    def _(act):
                        a = nc.scalar

                        def norm(g, b, q):
                            if q == 0:
                                act.wait_ge(rs_done, g + 1)
                            a.activation(o[:, b, q, :], t[:, b, q, :], ACT.Identity, bias=nm[:, q:q + 1], scale=rs[:, q:q + 1]).then_inc(ready, 1)

                        def deviation(g):
                            act.wait_ge(mv_done, 4 * (g + 1))
                            a.activation(sd[:], mv[:, :, 1], ACT.Sqrt, bias=epsc[:]).then_inc(sd_done, 1)

                        def step(i, first, last):
                            for b in range(2):
                                g = 2 * i + b
                                lag = not (first and b == 0)
                                for q in range(4):
                                    un = 8 * i + 4 * b + q
                                    act.wait_ge(t_done, un + 1)
                                    if lag:
                                        act.wait_ge(mm_done, un - B + 1)
                                    a.activation(xT[:, q, :, :], pT[q][:], ACT.Copy).then_inc(xt_ready, 1)
                                    if lag and q == 1:
                                        deviation(g - 1)
                                    if lag and q >= 2:
                                        if q == 2 and not first:
                                            act.wait_ge(stored[1 - b], 16 * i if b == 1 else 16 * (i - 1))
                                        norm(g - 1, 1 - b, 2 * (q - 2))
                                        norm(g - 1, 1 - b, 2 * (q - 2) + 1)
                        ends(act, step)
                        deviation(GROUPS - 1)
                        act.wait_ge(stored[1], 16 * (GI - 1))
                        for q in range(4):
                            norm(GROUPS - 1, 1, q)

                    @block.vector
                    def _(dve):
                        v = nc.vector

                        def scales(g):
                            dve.wait_ge(sd_done, g + 1)
                            v.reciprocal(rs[:], sd[:]).then_inc(r_done, 1)
                            dve.wait_ge(r_done, g + 1)
                            v.scalar_tensor_tensor(nm[:], mv[:, :, 0], -1.0, rs[:], ALU.mult, ALU.mult).then_inc(rs_done, 1)

                        def step(i, first, last):
                            for b in range(2):
                                g = 2 * i + b
                                lag = not (first and b == 0)
                                for q in range(4):
                                    un = 8 * i + 4 * b + q
                                    dve.wait_ge(mm_done, un + 1)
                                    if q == 0 and lag:
                                        dve.wait_ge(ready, 4 * (g - 1))
                                    v.tensor_tensor(t[:, b, q, :], pz[q][:], xin[:, b, q, :], ALU.add).then_inc(add_done, 1)
                                    dve.wait_ge(add_done, un + 1)
                                    v.bn_stats(st[:, q, :], t[:, b, q, :]).then_inc(st_done, 1)
                                    if lag and q == 1:
                                        scales(g - 1)
                                dve.wait_ge(st_done, 4 * (g + 1))
                                if lag:
                                    dve.wait_ge(rs_done, g)
                                v.memset(pad[:], 0.0)
                                for q in range(4):
                                    v.bn_aggr(mv[:, q, :], st[:, q, :]).then_inc(mv_done, 1)
                        ends(dve, step)
                        scales(GROUPS - 1)

        class TileNorm:
            def __init__(self, c2, name):
                def tmp(x, shape):
                    return c2.enter_context(nc.sbuf_tensor(f"{name}_{x}", shape, F32))
                self.t, self.o = tmp("t", [P, RING, F]), tmp("o", [P, RING, F])
                self.st, self.mv = tmp("st", [P, RING, 6]), tmp("mv", [P, RING, 2])
                self.pad = tmp("pad", [P, 1])
                self.sd, self.rs, self.nm = tmp("sd", [P, RING]), tmp("rs", [P, RING]), tmp("nm", [P, RING])
                self.add_done, self.st_done, self.mv_done, self.sd_done, self.r_done, self.rs_done, self.ready = [
                    sem(f"{name}_{x}") for x in ("add", "stats", "mv", "sd", "r", "rs", "normed")]

            def moments(self, dve, u, r, a, b, waits):
                v = nc.vector
                if waits:
                    dve.wait_ge(self.ready, u - 3)
                v.tensor_tensor(self.t[:, r, :], a, b, ALU.add).then_inc(self.add_done, 1)
                dve.wait_ge(self.add_done, u + 1)
                v.bn_stats(self.st[:, r, :], self.t[:, r, :]).then_inc(self.st_done, 1)
                dve.wait_ge(self.st_done, u + 1)
                v.memset(self.pad[:], 0.0)
                v.bn_aggr(self.mv[:, r, :], self.st[:, r, :]).then_inc(self.mv_done, 1)

            def deviation(self, act, u, r):
                act.wait_ge(self.mv_done, u + 1)
                nc.scalar.activation(self.sd[:, r:r + 1], self.mv[:, r, 1:2], ACT.Sqrt, bias=epsc[:]).then_inc(self.sd_done, 1)

            def scales(self, dve, u, r):
                v = nc.vector
                dve.wait_ge(self.sd_done, u + 1)
                v.reciprocal(self.rs[:, r:r + 1], self.sd[:, r:r + 1]).then_inc(self.r_done, 1)
                dve.wait_ge(self.r_done, u + 1)
                v.scalar_tensor_tensor(self.nm[:, r:r + 1], self.mv[:, r, 0:1], -1.0, self.rs[:, r:r + 1], ALU.mult, ALU.mult).then_inc(self.rs_done, 1)

            def normed(self, act, u, r):
                act.wait_ge(self.rs_done, u + 1)
                nc.scalar.activation(self.o[:, r, :], self.t[:, r, :], ACT.Identity, bias=self.nm[:, r:r + 1], scale=self.rs[:, r:r + 1]).then_inc(self.ready, 1)

        def slots_block():
            with ExitStack() as c2:
                def tmp(name, shape, dt=F32):
                    return c2.enter_context(nc.sbuf_tensor(f"s_{name}", shape, dt))
                yin, xd = tmp("yin", [P, RING, XW]), tmp("xd", [P, RING, F])
                xT, xTc = tmp("xT", [P, 2, F]), tmp("xTc", [4, 2, P])
                jring, kring = tmp("jring", [P, RING], I32), tmp("kring", [P, RING], I32)
                k_ready = sem("s_k")
                ln = TileNorm(c2, "s_ln")
                begun = sem("s_begun")
                pT = [c2.enter_context(nc.psum_tensor(f"s_pT{x}", [P, 512], F32)) for x in range(2)]
                pz = [c2.enter_context(nc.psum_tensor(f"s_pz{x}", [P, F], F32)) for x in range(2)]
                idx_ready, t_done, xt_ready, mm_done = [sem(f"s_{x}") for x in ("idx", "T", "xT", "mm")]
                got, y_in, stored = sems("s_got"), sems("s_in"), sems("s_st")
                cv = cube.rearrange("(u p) f -> u p f", p=P)
                flat_ = "a p f -> (a p) f"
                with nc.Block() as block:
                    @block.sync
                    def _(sp):
                        def step(i, at):
                            for r in range(RING):
                                u = 4 * i + r
                                if at != 0:
                                    sp.wait_ge(t_done, u - 3)
                                sp.dma_start(yin[:, r, :], cv[bass.ds(u, 1), :, :].rearrange(flat_)).then_inc(y_in[r], 16)
                        loop(sp, step)

                    @block.gpsimd
                    def _(pool):
                        top = pool.to_reg(NPAD - 1)

                        def scatter(u, r):
                            pool.wait_ge(ln.ready, u + 1)
                            pool.wait_ge(k_ready, u + 1)
                            pool.sem_inc(begun, 1)
                            pool.indirect_dma_start(zrow, bass.IndirectOffsetOnAxis(ap=kring[:, r:r + 1], axis=0), ln.o[:, r, :], None,
                                                    bounds_check=top, oob_is_err=False).then_inc(stored[r], 16)

                        def step(i, at):
                            for r in range(RING):
                                u = 4 * i + r
                                pool.wait_ge(idx_ready, u + 1)
                                if at != 0:
                                    pool.wait_ge(ln.add_done, u - 3)
                                pool.sem_inc(begun, 1)
                                pool.indirect_dma_start(xd[:, r, :], None, d["x"], bass.IndirectOffsetOnAxis(ap=jring[:, r:r + 1], axis=0),
                                                        bounds_check=top, oob_is_err=False).then_inc(got[r], 16)
                                if not (at == 0 or (at == 1 and r < 3)):
                                    scatter(u - 7, (r - 7) % 4)
                        loop(pool, step, 2)
                        for u in range(ET - 7, ET):
                            scatter(u, u % 4)
                        for r in range(RING):
                            pool.wait_ge(stored[r], 16 * EI)

                    @block.tensor
                    def _(pe):
                        def product(u, r, waits):
                            pe.wait_ge(xt_ready, 2 * (u + 1))
                            if waits:
                                pe.wait_ge(ln.add_done, u - 1)
                            p = pz[r % 2]
                            for c in range(2):
                                pe.matmul(p[:], xT[:, r % 2, P * c:P * c + P], hmap[c][:], start=(c == 0), stop=False)
                            pe.matmul(p[:], xTc[:, r % 2, :], hc[:], start=False, stop=True).then_inc(mm_done, 1)

                        def step(i, at):
                            for r in range(RING):
                                u = 4 * i + r
                                pe.wait_ge(y_in[r], 16 * i + 16)
                                if not (at == 0 and r < 2):
                                    pe.wait_ge(xt_ready, 2 * (u - 1))
                                p = pT[r % 2]
                                pe.transpose(p[:, 0:P], yin[:, r, 0:P], ident[:])
                                pe.transpose(p[:, P:F], yin[:, r, P:F], ident[:])
                                pe.transpose(p[0:4, F:F + P], yin[:, r, F:XW], ident[:]).then_inc(t_done, 1)
                                if not (at == 0 and r == 0):
                                    product(u - 1, (r - 1) % 4, not (at == 0 and r < 3))
                        loop(pe, step)
                        product(ET - 1, 3, True)

                    @block.scalar
                    def _(act):
                        def norm(u, r, waits):
                            if waits is not None:
                                act.wait_ge(stored[r], waits)
                            ln.normed(act, u, r)

                        def step(i, at):
                            for r in range(RING):
                                u = 4 * i + r
                                act.wait_ge(t_done, u + 1)
                                if not (at == 0 and r < 2):
                                    act.wait_ge(mm_done, u - 1)
                                nc.scalar.activation(xT[:, r % 2, :], pT[r % 2][:, 0:F], ACT.Copy).then_inc(xt_ready, 1)
                                nc.scalar.activation(xTc[:, r % 2, :], pT[r % 2][0:4, F:F + P], ACT.Copy).then_inc(xt_ready, 1)
                                if not (at == 0 and r < 2):
                                    ln.deviation(act, u - 2, (r - 2) % 4)
                                if not (at == 0 and r < 3):
                                    norm(u - 3, (r - 3) % 4, None if at == 0 else (16 * i if r == 3 else 16 * (i - 1)))
                        loop(act, step)
                        for u in (ET - 2, ET - 1):
                            ln.deviation(act, u, u % 4)
                        for u in range(ET - 3, ET):
                            norm(u, u % 4, 16 * (EI - 1))

                    @block.vector
                    def _(dve):
                        v = nc.vector
                        for r in range(RING):
                            copy(jring[:, r:r + 1], dstJ[:, r:r + 1]).then_inc(idx_ready, 1)

                        def finish(i, r, waits):
                            u = 4 * i + r
                            dve.wait_ge(mm_done, u + 1)
                            dve.wait_ge(got[r], 16 * i + 16)
                            ln.moments(dve, u, r, pz[r % 2][:], xd[:, r, :], waits)
                            copy(jring[:, r:r + 1], dstJ[:, bass.ds(u + RING, 1)]).then_inc(idx_ready, 1)
                            if waits:
                                dve.wait_ge(stored[r], 16 * i)
                            copy(kring[:, r:r + 1], sidx[:, bass.ds(u, 1)]).then_inc(k_ready, 1)

                        def step(i, at):
                            for r in range(RING):
                                finish(i, r, at != 0)
                                if not (at == 0 and r < 2):
                                    ln.scales(dve, 4 * i + r - 2, (r - 2) % 4)
                        loop(dve, step)
                        for u in (ET - 2, ET - 1):
                            ln.scales(dve, u, u % 4)

        def hop_pass(k):
            table_of, rows = {1: (zrow, NPAD), 2: (hop1, NSLOT), 3: (hop2, NSLOT)}[k]
            idx, weight = (other, wK) if k == 1 else (idxh, w23)
            dest = None if k == 3 else (hop1, hop2)[k - 1].rearrange("(u p) f -> u p f", p=P)
            with ExitStack() as c2:
                def tmp(name, shape, dt=F32):
                    return c2.enter_context(nc.sbuf_tensor(f"h{k}_{name}", shape, dt))
                xs, h = tmp("xs", [P, RING, F]), tmp("h", [P, RING, F])
                mw, urow, carry = tmp("mw", [P, RING, P]), tmp("urow", [1, RING, P]), tmp("carry", [1, F])
                ps = [c2.enter_context(nc.psum_tensor(f"h{k}_ps{b}", [P, 512], F32)) for b in range(2)]
                s = lambda x: sem(f"h{k}_{x}")
                begun = s("begun")
                init, idx_ready, mw_ready, ps_ready, carry_ready, h_ready = s("init"), s("idx"), s("mw"), s("ps"), s("carry"), s("h")
                got, stored = sems(f"h{k}_got"), sems(f"h{k}_st")
                flat_ = "a p f -> (a p) f"
                if k == 3:
                    ins = tmp("ins", [P, RING, 3, F])
                    jring = tmp("jring", [P, RING], I32)
                    z_in, j_ready = sems("h3_zin"), s("j")
                    xT = tmp("xT", [P, 2, 8, P])
                    kring = tmp("kring", [P, RING], I32)
                    ln = TileNorm(c2, "o_ln")
                    pT = [c2.enter_context(nc.psum_tensor(f"h3_pT{b}", [P, 4, P], F32)) for b in range(2)]
                    pz = [c2.enter_context(nc.psum_tensor(f"h3_pz{b}", [P, F], F32)) for b in range(2)]
                    ta_done, tb_done, xa_ready, xb_ready, mm_done, k_ready = s("Ta"), s("Tb"), s("xa"), s("xb"), s("mm"), s("k")
                    in3 = sems("h3_in")
                    hops = [x.rearrange("(u p) f -> u p f", p=P) for x in (hop1, hop2)]
                with nc.Block() as block:
                    @block.gpsimd
                    def _(pool):
                        top = pool.to_reg(rows - 1)
                        out_top = pool.to_reg(NPAD - 1)
                        pool.wait_ge(init, 2)

                        def scatter(u, r):
                            pool.wait_ge(ln.ready, u + 1)
                            pool.wait_ge(k_ready, u + 1)
                            pool.sem_inc(begun, 1)
                            pool.indirect_dma_start(d["out"], bass.IndirectOffsetOnAxis(ap=kring[:, r:r + 1], axis=0), ln.o[:, r, :], None,
                                                    bounds_check=out_top, oob_is_err=False).then_inc(stored[r], 16)

                        def step(i, at):
                            for r in range(RING):
                                u = 4 * i + r
                                if at != 0:
                                    pool.wait_ge(ps_ready, u - 3)
                                pool.wait_ge(idx_ready, u + 1)
                                pool.sem_inc(begun, 1)
                                pool.indirect_dma_start(xs[:, r, :], None, table_of, bass.IndirectOffsetOnAxis(ap=iring[:, r:r + 1], axis=0),
                                                        bounds_check=top, oob_is_err=False).then_inc(got[r], 16)
                                if k == 3:
                                    if at != 0:
                                        pool.wait_ge(ln.add_done, u - 3)
                                    pool.wait_ge(j_ready, u + 1)
                                    pool.sem_inc(begun, 1)
                                    pool.indirect_dma_start(ins[:, r, 0, :], None, zrow, bass.IndirectOffsetOnAxis(ap=jring[:, r:r + 1], axis=0),
                                                            bounds_check=out_top, oob_is_err=False).then_inc(z_in[r], 16)
                                if k == 3 and not (at == 0 or (at == 1 and r < 3)):
                                    scatter(u - 7, (r - 7) % 4)
                        loop(pool, step, 2 if k == 3 else 1)
                        if k == 3:
                            for u in range(ET - 7, ET):
                                scatter(u, u % 4)
                            for r in range(RING):
                                pool.wait_ge(stored[r], 16 * EI)

                    @block.sync
                    def _(sp):
                        if k < 3:
                            with sp.Fori(0, EI) as i:
                                for r in range(RING):
                                    u = 4 * i + r
                                    sp.wait_ge(h_ready, u + 1)
                                    sp.dma_start(dest[bass.ds(u, 1), :, :].rearrange(flat_), h[:, r, :]).then_inc(stored[r], 16)
                            for r in range(RING):
                                sp.wait_ge(stored[r], 16 * EI)
                        else:
                            def step(i, at):
                                for r in range(RING):
                                    u = 4 * i + r
                                    if at != 0:
                                        sp.wait_ge(tb_done, u - 3)
                                    for x in range(2):
                                        sp.dma_start(ins[:, r, 1 + x, :], hops[x][bass.ds(u, 1), :, :].rearrange(flat_)).then_inc(in3[r], 16)
                            loop(sp, step)

                    @block.scalar
                    def _(act):
                        def norm(u, r, waits):
                            if waits is not None:
                                act.wait_ge(stored[r], waits)
                            ln.normed(act, u, r)

                        def step(i, at):
                            for r in range(RING):
                                u = 4 * i + r
                                act.wait_ge(ps_ready, u + 1)
                                nc.scalar.activation(carry[:], ps[r % 2][0:1, 0:F], ACT.Copy, scale=cflag[:, bass.ds(u, 1)]).then_inc(carry_ready, 1)
                                if at != 0:
                                    if k == 3:
                                        act.wait_ge(tb_done, u - 3)
                                    else:
                                        act.wait_ge(stored[r], 16 * i)
                                nc.scalar.activation(h[:, r, :], ps[r % 2][:, 0:F], ACT.Copy).then_inc(h_ready, 1)
                                if k == 3:
                                    act.wait_ge(tb_done, u + 1)
                                    if not (at == 0 and r < 2):
                                        act.wait_ge(mm_done, u - 1)
                                    nc.scalar.activation(xT[:, r % 2, 4:8, :], pT[1][:], ACT.Copy).then_inc(xb_ready, 1)
                                    if not (at == 0 and r < 2):
                                        ln.deviation(act, u - 2, (r - 2) % 4)
                                    if not (at == 0 and r < 3):
                                        norm(u - 3, (r - 3) % 4, None if at == 0 else (16 * i if r == 3 else 16 * (i - 1)))
                        loop(act, step)
                        if k == 3:
                            for u in (ET - 2, ET - 1):
                                ln.deviation(act, u, u % 4)
                            for u in range(ET - 3, ET):
                                norm(u, u % 4, 16 * (EI - 1))

                    @block.tensor
                    def _(pe):
                        pe.wait_ge(init, 2)

                        def product(u, r, waits):
                            pe.wait_ge(xa_ready, u + 1)
                            pe.wait_ge(xb_ready, u + 1)
                            if waits:
                                pe.wait_ge(ln.add_done, u - 1)
                            for c in range(8):
                                last = pe.matmul(pz[r % 2][:], xT[:, r % 2, c, :], kept_w[c // 2][:, c % 2, :], start=(c == 0), stop=(c == 7))
                            last.then_inc(mm_done, 1)

                        def step(i, at):
                            for r in range(RING):
                                u = 4 * i + r
                                pe.wait_ge(got[r], 16 * i + 16)
                                pe.wait_ge(mw_ready, 2 * (u + 1))
                                if not (at == 0 and r < 2):
                                    pe.wait_ge(h_ready, u - 1)
                                pe.matmul(ps[r % 2][:, 0:F], mw[:, r, :], xs[:, r, :], start=True, stop=False)
                                if not (at == 0 and r == 0):
                                    pe.wait_ge(carry_ready, u)
                                pe.matmul(ps[r % 2][:, 0:F], urow[:, r, :], carry[:], start=False, stop=True).then_inc(ps_ready, 1)
                                if k == 3:
                                    pe.wait_ge(in3[r], 32 * i + 32)
                                    pe.wait_ge(z_in[r], 16 * i + 16)
                                    if not (at == 0 and r == 0):
                                        pe.wait_ge(xa_ready, u)
                                    for c in range(4):
                                        last = pe.transpose(pT[0][:, c, :], ins[:, r, c // 2, P * (c % 2):P * (c % 2) + P], ident[:])
                                    last.then_inc(ta_done, 1)
                                    if not (at == 0 and r == 0):
                                        product(u - 1, (r - 1) % 4, not (at == 0 and r < 3))
                                    if not (at == 0 and r == 0):
                                        pe.wait_ge(xb_ready, u)
                                    for c in range(2):
                                        pe.transpose(pT[1][:, c, :], ins[:, r, 2, P * c:P * c + P], ident[:])
                                    pe.wait_ge(h_ready, u + 1)
                                    for c in range(2):
                                        last = pe.transpose(pT[1][:, 2 + c, :], h[:, r, P * c:P * c + P], ident[:])
                                    last.then_inc(tb_done, 1)
                        loop(pe, step)
                        if k == 3:
                            product(ET - 1, 3, True)

                    @block.vector
                    def _(dve):
                        v = nc.vector
                        v.memset(carry[:], 0.0).then_inc(init, 1)
                        v.memset(xs[:], 0.0).then_inc(init, 1)

                        def prepare(u, r, first):
                            if not first:
                                dve.wait_ge(ps_ready, u - 3)
                            v.tensor_scalar(mw[:, r, :], same[:, bass.ds(u, 1), :].rearrange("p a j -> p (a j)"), weight[:, bass.ds(u, 1)], None, ALU.mult).then_inc(mw_ready, 1)
                            v.tensor_copy(urow[:, r, :], same[0:1, bass.ds(u, 1), :].rearrange("p a j -> p (a j)")).then_inc(mw_ready, 1)

                        def sums(u, r, waits, stored_at):
                            dve.wait_ge(mm_done, u + 1)
                            ln.moments(dve, u, r, pz[r % 2][:], ins[:, r, 0, :], waits)
                            if stored_at is not None:
                                dve.wait_ge(stored[r], stored_at)
                            copy(kring[:, r:r + 1], sidx[:, bass.ds(u, 1)]).then_inc(k_ready, 1)

                        for r in range(RING):
                            copy(iring[:, r:r + 1], idx[:, r:r + 1]).then_inc(idx_ready, 1)
                            if k == 3:
                                copy(jring[:, r:r + 1], dstJ[:, r:r + 1]).then_inc(j_ready, 1)
                        for r in range(2):
                            prepare(r, r, True)

                        def step(i, at):
                            for r in range(RING):
                                u = 4 * i + r
                                if not (at == EI - 1 and r >= 2):
                                    prepare(u + 2, (r + 2) % 4, at == 0 and r < 2)
                                dve.wait_ge(got[r], 16 * i + 16)
                                copy(iring[:, r:r + 1], idx[:, bass.ds(u + RING, 1)]).then_inc(idx_ready, 1)
                                if k == 3:
                                    dve.wait_ge(z_in[r], 16 * i + 16)
                                    copy(jring[:, r:r + 1], dstJ[:, bass.ds(u + RING, 1)]).then_inc(j_ready, 1)
                                    dve.wait_ge(ta_done, u + 1)
                                    if not (at == 0 and r < 2):
                                        dve.wait_ge(mm_done, u - 1)
                                    v.tensor_copy(xT[:, r % 2, 0:4, :], pT[0][:]).then_inc(xa_ready, 1)
                                    if not (at == 0 and r == 0):
                                        sums(u - 1, (r - 1) % 4, not (at == 0 or (at == 1 and r == 0)),
                                             None if at == 0 or (at == 1 and r == 0) else (16 * (i - 1) if r == 0 else 16 * i))
                                    if not (at == 0 and r < 3):
                                        ln.scales(dve, u - 3, (r - 3) % 4)
                        loop(dve, step, 2 if k == 3 else 1)
                        if k == 3:
                            sums(ET - 1, 3, True, 16 * (EI - 1))
                            for u in range(ET - 3, ET):
                                ln.scales(dve, u, u % 4)

        load_block()
        end_of_block()
        out_of_order = nc.values_load(unsorted[0:1, 0:1], min_val=0, max_val=NSLOT)
        with nc.If(out_of_order > 0):
            sort_block("ds", d["dstK"], d["dstrow"], d["srcK"], d["wK"])
            end_of_block()
        structure_block("dt", table, True)
        end_of_block()
        node_gram_block()
        end_of_block()
        for k in (1, 2, 3):
            a_pass(k, gk[k - 1])
            end_of_block()
        norm_block()
        end_of_block()
        dense_block("z", d["x"], [hmap[0][:], hmap[1][:]], True, zrow)
        end_of_block()
        slots_block()
        end_of_block()
        sort_block("ss", d["skey"], d["skeyrow"], d["sother"], d["wK"])
        end_of_block()
        structure_block("st", table2, False)
        end_of_block()
        dense_block("o", zrow, [kept_w[0][:, 0, :], kept_w[0][:, 1, :]], False, d["out"])
        end_of_block()
        for k in (1, 2, 3):
            hop_pass(k)
            end_of_block()


def kernel(x, src, dst, edge_weight, L0_gnn_W1, L0_gnn_b1, L0_gnn_g1, L0_gnn_be1, L0_gnn_W2, L0_gnn_b2, L0_gnn_g2, L0_gnn_be2,
           L0_gnn_W3, L0_gnn_b3, L0_gnn_g3, L0_gnn_be3, L1_gnn_weight):
    import concourse.bacc as bacc
    from concourse.bass_utils import run_bass_kernel_spmd

    def padded(a, n, fill):
        return np.concatenate([a, np.full((n - a.shape[0],) + a.shape[1:], fill, a.dtype)])

    def tiles(a):
        return np.ascontiguousarray(a.reshape(ET, P)[::-1])

    x, src, dst, edge_weight = (np.asarray(a) for a in (x, src, dst, edge_weight))
    s, t, w = padded(src, NSLOT, 0), padded(dst, NSLOT, N), padded(edge_weight, NSLOT, 0)
    skey, sother = padded(src, NSLOT, N), padded(dst, NSLOT, 0)
    before = np.concatenate([np.full((1,), -1, t.dtype), t[:-1]])
    table0 = np.zeros((NPAD, 2), np.float32)
    table0[:, 0] = np.where(np.arange(NPAD) < N, np.arange(NPAD), 2 * NPAD)
    table0[:, 1] = 1.0

    def rows(a):
        return np.ascontiguousarray(tiles(a)[:, ::-1])

    def columns(a):
        return np.ascontiguousarray(rows(a).T)

    k, m = np.arange(P)[:, None], np.arange(P)[None, :]
    arrays = {
        "x": padded(x, NPAD, 0),
        "srcK": columns(s), "dstK": columns(t), "wK": columns(w), "dstrow": rows(t),
        "skey": columns(skey), "skeyrow": rows(skey), "sother": columns(sother),
        "dstJ": np.ascontiguousarray(tiles(t).T), "dprev": np.ascontiguousarray(tiles(before).T),
        "iota": np.ascontiguousarray(np.broadcast_to(np.arange(NPAD // P, dtype=np.float32), (P, NPAD // P))),
        "tri": (m < k).astype(np.float32), "triu": (k < m).astype(np.float32), "rev": (k + m == P - 1).astype(np.float32),
        "slots": np.ascontiguousarray((NPAD + np.arange(NSLOT, dtype=np.float32)).reshape(ET, P).T),
        "table0": table0, "ident": np.eye(P, dtype=np.float32), "ones": np.ones((P, P), np.float32),
        "e3": np.array([[0, 0, 0, 1]], np.float32), "e3c": np.array([[0], [0], [0], [1]], np.float32),
        "L1W": np.ascontiguousarray(np.asarray(L1_gnn_weight).transpose(2, 0, 1)),
    }
    for k, (W, b, g, be) in enumerate(((L0_gnn_W1, L0_gnn_b1, L0_gnn_g1, L0_gnn_be1), (L0_gnn_W2, L0_gnn_b2, L0_gnn_g2, L0_gnn_be2),
                                       (L0_gnn_W3, L0_gnn_b3, L0_gnn_g3, L0_gnn_be3)), 1):
        arrays[f"W{k}"] = np.asarray(W)
        for n, a in (("b", b), ("g", g), ("be", be)):
            arrays[f"{n}{k}"] = np.asarray(a)[None]
    nc = bacc.Bacc("TRN2", target_bir_lowering=False, num_devices=1)
    d = {n: nc.dram_tensor(f"in_{n}", a.shape, mybir.dt.from_np(a.dtype), kind="ExternalInput").ap() for n, a in arrays.items()}
    d["out"] = nc.dram_tensor("out_rows", (NPAD, F), F32, kind="ExternalOutput").ap()
    build_program(nc, d)
    r = run_bass_kernel_spmd(nc, [{f"in_{n}": a for n, a in arrays.items()}], core_ids=[0])
    return r.results[0]["out_rows"][:N]
```

```python
from contextlib import ExitStack

import numpy as np

import concourse.bass as bass
from concourse import mybir

ALU = mybir.AluOpType
ACT = mybir.ActivationFunctionType
AX = mybir.AxisListType
F32 = mybir.dt.float32
BF16 = mybir.dt.bfloat16
I32 = mybir.dt.int32

P = 128
N = 50000
E = 25000
F = 256
XW = F + 4
RING = 4
ET = 196
NSLOT = ET * P
EI = ET // RING
GROUPS = 98
NPAD = GROUPS * 4 * P
GI = GROUPS // 2
FAR = 1000000.0
EPS = 1e-5
NT = GROUPS * 4


def build_program(nc, d):
    with ExitStack() as ctx:
        def sb(name, shape, dt=F32):
            return ctx.enter_context(nc.sbuf_tensor(name, shape, dt))

        in_use = []

        def sem(name):
            in_use.append(nc.alloc_semaphore(name=name))
            return in_use[-1]

        def end_of_block():
            nc.clear_and_free_semaphores(in_use)
            in_use.clear()
            nc.all_engine_barrier()

        def sems(name, n=RING):
            return [sem(f"{name}{k}") for k in range(n)]

        def copy(out, a):
            return nc.vector.tensor_scalar(out, a, 1.0, None, ALU.mult)

        def dram(name, shape, dt=F32):
            return nc.dram_tensor(name, shape, dt, kind="Internal").ap()
        table = dram("node_table", (NPAD, 2))
        hist = dram("l0_rows", (NPAD + 2 * NSLOT, XW))
        cube = dram("l0_cube", (NSLOT, XW))
        zrow = dram("z_rows", (NPAD, F))
        xown = dram("own_rows", (NSLOT, F))
        hop1 = dram("hop1", (NSLOT, F))
        hop2 = dram("hop2", (NSLOT, F))

        srows = dram("sorted_rows", (NSLOT, 4))
        flat = dram("key_rows", (ET, P))
        table2 = dram("hop_table", (NPAD, 2))

        ident = sb("ident", [P, P])
        identb = sb("identb", [P, P], BF16)
        onesf = sb("onesf", [P, P])
        same = sb("same", [P, ET, P], BF16)
        keyJ = sb("keyJ", [P, ET])
        keyK = sb("keyK", [P, ET])
        other = sb("other", [P, ET + RING], I32)
        dstJ = sb("dstJ", [P, ET + RING], I32)
        wK = sb("wK", [P, ET])
        w23 = sb("w23", [P, ET])
        edge = sb("edge", [P, ET, 2])
        idx2 = sb("idx2", [P, ET + RING], I32)
        idx3 = sb("idx3", [P, ET + RING], I32)
        idxh = sb("idxh", [P, ET + RING], I32)
        sidx = sb("sidx", [P, ET + RING], I32)
        rep = sb("rep", [P, ET])
        dinvrep = sb("dinvrep", [P, ET])
        dinv2rep = sb("dinv2rep", [P, ET])
        cflag = sb("cflag", [1, ET])
        side = sb("side", [P, ET, 3])
        nonU = sb("nonU", [P, NT])
        gram = sb("gram", [P, 3, XW])
        iring = sb("iring", [P, RING], I32)
        unsorted = sb("unsorted", [1, 1], I32)

        def loop(eng, step, peel=1):
            for i in range(peel):
                step(i, i)
            with eng.Fori(peel, EI - 1) as i:
                step(i, None)
            step(EI - 1, EI - 1)

        def linker(dve, chain):
            n = [0]

            def link(ins):
                n[0] += 1
                ins.then_inc(chain, 1)
                dve.wait_ge(chain, n[0])
            return link

        def load_block():
            with ExitStack() as c2:
                def tmp(name, shape, dt=F32):
                    return c2.enter_context(nc.sbuf_tensor(f"l_{name}", shape, dt))
                dK, dJ, dP = tmp("dK", [P, ET], I32), tmp("dJ", [P, ET], I32), tmp("dP", [P, ET], I32)
                dPf, t0, t1 = tmp("dPf", [P, ET]), tmp("t0", [P, ET]), tmp("t1", [P, 1])
                pf = c2.enter_context(nc.psum_tensor("l_pf", [1, 1], F32))
                loaded, chain, bad, summed = sem("l_loaded"), sem("l_chain"), sem("l_bad"), sem("l_sum")
                with nc.Block() as block:
                    @block.sync
                    def _(sp):
                        for t, name in ((ident, "ident"), (onesf, "ones"), (dK, "dstK"), (dJ, "dstJ"), (dP, "dprev")):
                            sp.dma_start(t[:], d[name]).then_inc(loaded, 16)
                        sp.dma_start(other[:, 0:ET], d["srcK"]).then_inc(loaded, 16)

                    @block.vector
                    def _(dve):
                        v = nc.vector
                        link = linker(dve, chain)
                        for t in (other, dstJ, idx2, idx3, idxh, sidx):
                            link(v.memset(t[:, ET:ET + RING], 0))
                        dve.wait_ge(loaded, 16 * 6)
                        link(v.tensor_copy(identb[:], ident[:]))
                        link(v.tensor_copy(keyK[:], dK[:]))
                        link(v.tensor_copy(keyJ[:], dJ[:]))
                        link(v.tensor_copy(dPf[:], dP[:]))
                        link(v.tensor_tensor(rep[:], keyJ[:], dPf[:], ALU.not_equal))
                        link(v.tensor_tensor(t0[:], dPf[:], keyJ[:], ALU.is_gt))
                        v.tensor_reduce(t1[:], t0[:], AX.X, ALU.add).then_inc(bad, 1)
                        dve.wait_ge(summed, 1)
                        link(v.tensor_copy(unsorted[:], pf[:]))

                    @block.tensor
                    def _(pe):
                        pe.wait_ge(bad, 1)
                        pe.matmul(pf[:], t1[:], onesf[:, 0:1], start=True, stop=True).then_inc(summed, 1)

        def sort_block(name, keys, key_rows, others, weights):
            LO = NPAD // P
            with ExitStack() as c2:
                def tmp(x, shape, dt=F32):
                    return c2.enter_context(nc.sbuf_tensor(f"{name}_{x}", shape, dt))
                key, oth, wt = tmp("key", [P, ET], I32), tmp("oth", [P, ET], I32), tmp("wt", [P, ET])
                hi, lo, ti = tmp("hi", [P, ET]), tmp("lo", [P, ET]), tmp("ti", [P, ET], I32)
                keyf, rank, pos = tmp("keyf", [P, ET]), tmp("rank", [P, ET]), tmp("pos", [P, ET])
                tf = tmp("tf", [P, ET])
                iota, tri, rev = tmp("iota", [P, LO]), tmp("tri", [P, P]), tmp("rev", [P, P])
                triu = tmp("triu", [P, P])
                rowb = tmp("rowb", [P, RING, P], I32)
                ohl, ohh = tmp("ohl", [P, RING, LO], BF16), tmp("ohh", [P, RING, P], BF16)
                ohT = tmp("ohT", [P, 2, P])
                state = tmp("state", [P, 2, LO])
                base, incl, zrow_ = tmp("base", [P, LO]), tmp("incl", [P, LO]), tmp("zrow", [P, LO])
                junk, junk2 = tmp("junk", [P, RING, LO], BF16), tmp("junk2", [P, RING, P], BF16)
                rec = tmp("rec", [P, ET, 4])
                vring = tmp("vring", [P, RING, 4])
                sj = tmp("sj", [P, ET, 4])
                ph = c2.enter_context(nc.psum_tensor(f"{name}_ph", [P, LO], F32))
                pl = [c2.enter_context(nc.psum_tensor(f"{name}_pl{x}", [P, LO], F32)) for x in range(2)]
                pt = [c2.enter_context(nc.psum_tensor(f"{name}_pt{x}", [P, P], BF16)) for x in range(2)]
                po = c2.enter_context(nc.psum_tensor(f"{name}_po", [P, 1], F32))
                pr = [c2.enter_context(nc.psum_tensor(f"{name}_pr{x}", [P, LO], F32)) for x in range(2)]
                s = lambda x: sem(f"{name}_{x}")
                loaded, chain, begun = s("loaded"), s("chain"), s("begun")
                hot1, counted, based, offset = s("hot1"), s("counted"), s("based"), s("offset")
                hot2, turned, turnedc, looked, kept, updated, chosen, inrank = [s(x) for x in ("hot2", "turn", "turnc", "look", "kept", "upd", "chosen", "inrank")]
                row_in, put, put_ready, back, reved, kdone = sems(f"{name}_row"), sems(f"{name}_put"), s("putr"), s("back"), s("rev"), s("kdone")
                placed = s("placed")
                with nc.Block() as block:
                    @block.sync
                    def _(sp):
                        for t, a in ((key, keys), (oth, others), (wt, weights), (iota, d["iota"]), (tri, d["tri"]), (rev, d["rev"]), (triu, d["triu"])):
                            sp.dma_start(t[:], a).then_inc(loaded, 16)

                        def step(i, first):
                            for r in range(RING):
                                if not first:
                                    sp.wait_ge(inrank, 4 * i + r - 3)
                                sp.dma_start(rowb[:, r, :], key_rows[bass.ds(i * RING + r, 1), :].to_broadcast((P, P))).then_inc(row_in[r], 16)
                        step(0, True)
                        with sp.Fori(1, EI) as i:
                            step(i, False)

                    @block.tensor
                    def _(pe):
                        pe.wait_ge(based, 1)
                        pe.matmul(ph[:], zrow_[:, 0:P], zrow_[:], start=True, stop=False)
                        with pe.Fori(0, EI) as i:
                            for r in range(RING):
                                pe.wait_ge(hot1, 8 * i + 2 * r + 2)
                                pe.matmul(ph[:], ohh[:, r, :], ohl[:, r, :], start=False, stop=False).then_inc(counted, 1)
                        pe.matmul(ph[:], zrow_[:, 0:P], zrow_[:], start=False, stop=True).then_inc(counted, 1)
                        pe.wait_ge(based, 2)
                        pe.matmul(po[:], triu[:], incl[:, LO - 1:LO], start=True, stop=True).then_inc(offset, 1)
                        pe.wait_ge(based, 3)
                        pe.matmul(ph[:], ident[:], base[:], start=True, stop=True).then_inc(updated, 1)

                        def step(i, first):
                            for r in range(RING):
                                u = 4 * i + r
                                pe.wait_ge(hot2, 2 * (u + 1))
                                if not (first and r < 2):
                                    pe.wait_ge(turnedc, u - 1)
                                pe.transpose(pt[r % 2][:], ohh[:, r, :], identb[:]).then_inc(turned, 1)
                                pe.wait_ge(turnedc, u + 1)
                                pe.wait_ge(kept, u + 1)
                                if not (first and r < 2):
                                    pe.wait_ge(chosen, u - 1)
                                pe.matmul(ph[:], ohh[:, r, :], ohl[:, r, :], start=False, stop=True, skip_group_check=True).then_inc(updated, 1)
                                pe.matmul(pl[r % 2][:], ohT[:, r % 2, :], state[:, r % 2, :], start=True, stop=True).then_inc(looked, 1)
                        step(0, True)
                        with pe.Fori(1, EI) as i:
                            step(i, False)
                        pe.wait_ge(back, 16)
                        sjf = sj[:].rearrange("p u c -> p (u c)")
                        for x in range(2):
                            last = pe.matmul(pr[x][:], rev[:], sjf[:, LO * x:LO * x + LO], start=True, stop=True)
                        last.then_inc(reved, 1)

                    @block.scalar
                    def _(act):
                        def step(i, first):
                            for r in range(RING):
                                u = 4 * i + r
                                act.wait_ge(updated, u + 1)
                                if not (first and r < 2):
                                    act.wait_ge(looked, u - 1)
                                nc.scalar.activation(state[:, r % 2, :], ph[:], ACT.Copy).then_inc(kept, 1)
                                act.wait_ge(turned, u + 1)
                                nc.scalar.activation(ohT[:, r % 2, :], pt[r % 2][:], ACT.Copy).then_inc(turnedc, 1)
                        step(0, True)
                        with act.Fori(1, EI) as i:
                            step(i, False)

                    @block.vector
                    def _(dve):
                        v = nc.vector
                        link = linker(dve, chain)
                        link(v.memset(zrow_[:], 0.0))
                        dve.wait_ge(loaded, 16 * 7)
                        link(v.tensor_copy(keyf[:], key[:]))
                        link(v.tensor_scalar(ti[:], key[:], 127, None, ALU.bitwise_and))
                        link(v.tensor_copy(hi[:], ti[:]))
                        link(v.tensor_scalar(ti[:], key[:], 7, None, ALU.arith_shift_right))
                        link(v.tensor_copy(lo[:], ti[:]))
                        dve.sem_inc(based, 1)

                        def hot(u, r, ready):
                            v.tensor_scalar(ohl[:, r, :], iota[:], lo[:, bass.ds(u, 1)], None, ALU.is_equal).then_inc(ready, 1)
                            v.tensor_scalar(ohh[:, r, :], iota[:, 0:P], hi[:, bass.ds(u, 1)], None, ALU.is_equal).then_inc(ready, 1)

                        def count(i, first):
                            for r in range(RING):
                                if not first:
                                    dve.wait_ge(counted, 4 * i + r - 3)
                                hot(4 * i + r, r, hot1)
                        count(0, True)
                        with dve.Fori(1, EI) as i:
                            count(i, False)
                        dve.wait_ge(counted, ET + 1)
                        link(v.tensor_copy(base[:], ph[:]))
                        link(v.tensor_tensor_scan(incl[:], zrow_[:], base[:], 0.0, ALU.add, ALU.add))
                        dve.sem_inc(based, 1)
                        link(v.tensor_tensor(base[:], incl[:], base[:], ALU.subtract))
                        dve.wait_ge(offset, 1)
                        link(v.tensor_scalar(base[:], base[:], po[:, 0:1], None, ALU.add))
                        dve.sem_inc(based, 1)

                        def select(u, r):
                            dve.wait_ge(looked, u + 1)
                            v.scalar_tensor_tensor(junk[:, r, :], pl[r % 2][:], 1.0, ohl[:, r, :], ALU.mult, ALU.mult, accum_out=pos[:, bass.ds(u, 1)]).then_inc(chosen, 1)

                        def step(i, at):
                            for r in range(RING):
                                u = 4 * i + r
                                if at != 0:
                                    dve.wait_ge(chosen, u - 3)
                                    dve.wait_ge(looked, u - 3)
                                    dve.wait_ge(inrank, u - 3)
                                hot(u, r, hot2)
                                dve.wait_ge(row_in[r], 16 * i + 16)
                                v.scalar_tensor_tensor(junk2[:, r, :], rowb[:, r, :], keyf[:, bass.ds(u, 1)], tri[:], ALU.is_equal, ALU.mult, accum_out=rank[:, bass.ds(u, 1)]).then_inc(inrank, 1)
                                if not (at == 0 and r == 0):
                                    select(u - 1, (r - 1) % 4)
                        loop(dve, step)
                        select(ET - 1, 3)
                        dve.wait_ge(inrank, ET)
                        dve.wait_ge(chosen, ET)
                        link(v.tensor_tensor(pos[:], pos[:], rank[:], ALU.add))
                        link(v.tensor_copy(ti[:], pos[:]))
                        link(v.tensor_scalar(ti[:], ti[:], 127, None, ALU.bitwise_and))
                        link(v.tensor_copy(rank[:], ti[:]))
                        link(v.tensor_tensor(tf[:], pos[:], rank[:], ALU.subtract))
                        link(v.tensor_scalar(tf[:], tf[:], -1.0 / P, ET - 1.0, ALU.mult, ALU.add))
                        link(v.scalar_tensor_tensor(pos[:], rank[:], float(ET), tf[:], ALU.mult, ALU.add))
                        link(v.tensor_copy(idx2[:, 0:ET], pos[:]))
                        link(v.tensor_copy(rec[:, :, 0], keyf[:]))
                        link(v.tensor_copy(rec[:, :, 1], oth[:]))
                        link(v.tensor_copy(rec[:, :, 2], wt[:]))
                        link(v.memset(rec[:, :, 3], 0.0))

                        def put_step(i, first):
                            for r in range(RING):
                                if not first:
                                    dve.wait_ge(put[r], 16 * i)
                                copy(vring[:, r, :], rec[:, bass.ds(i * RING + r, 1), :].rearrange("p a c -> p (a c)")).then_inc(put_ready, 1)
                                copy(iring[:, r:r + 1], idx2[:, bass.ds(i * RING + r, 1)]).then_inc(put_ready, 1)
                        put_step(0, True)
                        with dve.Fori(1, EI) as i:
                            put_step(i, False)
                        link(v.memset(tf[:], -1.0))
                        dve.wait_ge(back, 16)
                        link(v.tensor_copy(keyJ[:], sj[:, :, 0]))
                        dve.sem_inc(placed, 1)
                        dve.wait_ge(reved, 1)
                        H = ET // 2
                        for x in range(2):
                            g = pr[x][:].rearrange("p (u c) -> p u c", c=4)
                            link(v.tensor_copy(keyK[:, H * x:H * x + H], g[:, :, 0]))
                            link(v.tensor_copy(other[:, H * x:H * x + H], g[:, :, 1]))
                            link(v.tensor_copy(wK[:, H * x:H * x + H], g[:, :, 2]))
                        dve.wait_ge(kdone, 32)
                        link(v.tensor_tensor(rep[:], keyJ[:], tf[:], ALU.not_equal))

                    @block.gpsimd
                    def _(pool):
                        top = pool.to_reg(NSLOT - 1)
                        with pool.Fori(0, EI) as i:
                            for r in range(RING):
                                pool.wait_ge(put_ready, 8 * i + 2 * r + 2)
                                pool.sem_inc(begun, 1)
                                pool.indirect_dma_start(srows, bass.IndirectOffsetOnAxis(ap=iring[:, r:r + 1], axis=0), vring[:, r, :], None,
                                                        bounds_check=top, oob_is_err=False).then_inc(put[r], 16)
                        for r in range(RING):
                            pool.wait_ge(put[r], 16 * EI)
                        pool.dma_start(sj[:].rearrange("p u c -> p (u c)"), srows.rearrange("(p u) c -> p (u c)", p=P)).then_inc(back, 16)
                        pool.wait_ge(back, 16)
                        pool.wait_ge(placed, 1)
                        pool.dma_start(tf[1:P, :], keyJ[0:P - 1, :]).then_inc(kdone, 16)
                        pool.dma_start(tf[0:1, 0:ET - 1], keyJ[P - 1:P, 1:ET]).then_inc(kdone, 16)

        def structure_block(name, out_table, with_degree):
            with ExitStack() as c2:
                def tmp(x, shape, dt=F32):
                    return c2.enter_context(nc.sbuf_tensor(f"{name}_{x}", shape, dt))
                rowb = tmp("rowb", [P, RING, P])
                onesb = tmp("onesb", [P, 1], BF16)
                turned = tmp("turned", [ET // 2, 2, P])
                cnt, cont, t0 = tmp("cnt", [P, ET]), tmp("cont", [P, ET]), tmp("t0", [P, ET])
                srow, crow = tmp("srow", [1, ET]), tmp("crow", [1, ET])
                tabv, slots = tmp("tabv", [P, ET, 2]), tmp("slots", [P, ET])
                vring = tmp("vring", [P, RING, 2])
                tfull = tmp("tfull", [P, NT, 2])
                ptr = c2.enter_context(nc.psum_tensor(f"{name}_ptr", [ET // 2, 2, P], F32))
                pcnt = c2.enter_context(nc.psum_tensor(f"{name}_pcnt", [P, 512], F32))
                pbc = c2.enter_context(nc.psum_tensor(f"{name}_pbc", [P, 2, 256], F32))
                s = lambda x: sem(f"{name}_{x}")
                begun, loaded, tinit, chain, flat_out = s("begun"), s("loaded"), s("tinit"), s("chain"), s("flat")
                turn, turnc, row_free, cnt_done, rows_ready, bc_done = [s(x) for x in ("turn", "turnc", "built", "cnt", "rows", "bc")]
                sq_in, sq_out, put_ready, look_idx, looked, tfl = [s(x) for x in ("sqin", "sqout", "put", "lidx", "looked", "tfl")]
                row_in, put, look = sems(f"{name}_row"), sems(f"{name}_puts"), sems(f"{name}_look")
                H = ET // 2
                with nc.Block() as block:
                    @block.sync
                    def _(sp):
                        sp.dma_start(slots[:], d["slots"]).then_inc(loaded, 16)
                        sp.wait_ge(turnc, 1)
                        sp.dma_start(flat.rearrange("(x u) p -> u x p", x=2), turned[:]).then_inc(flat_out, 16)
                        sp.wait_ge(flat_out, 16)

                        def step(i, first):
                            for r in range(RING):
                                if not first:
                                    sp.wait_ge(row_free, 4 * i + r - 3)
                                sp.dma_start(rowb[:, r, :], flat[bass.ds(i * RING + r, 1), :].to_broadcast((P, P))).then_inc(row_in[r], 16)
                        step(0, True)
                        with sp.Fori(1, EI) as i:
                            step(i, False)

                    @block.tensor
                    def _(pe):
                        for x in range(2):
                            last = pe.transpose(ptr[:, x, :], keyJ[:, H * x:H * x + H], ident[:])
                        last.then_inc(turn, 1)
                        if with_degree:
                            with pe.Fori(0, EI) as i:
                                for r in range(RING):
                                    pe.wait_ge(row_free, 4 * i + r + 1)
                                    pe.matmul(pcnt[:, bass.ds(i * RING + r, 1)], same[:, bass.ds(i * RING + r, 1), :].rearrange("p a j -> p (a j)"),
                                              onesb[:], start=True, stop=True).then_inc(cnt_done, 1)
                            pe.wait_ge(rows_ready, 1)
                            pe.matmul(pbc[:, 0, 0:ET], onesf[0:1, :], crow[:], start=True, stop=True).then_inc(bc_done, 1)
                            pe.matmul(pbc[:, 1, 0:ET], onesf[0:1, :], keyJ[0:1, :], start=True, stop=True).then_inc(bc_done, 1)

                    @block.scalar
                    def _(act):
                        if with_degree:
                            act.wait_ge(sq_in, 1)
                            nc.scalar.activation(t0[:], cnt[:], ACT.Sqrt).then_inc(sq_out, 1)

                    @block.vector
                    def _(dve):
                        v = nc.vector
                        link = linker(dve, chain)
                        link(v.memset(onesb[:], 1.0))
                        dve.wait_ge(turn, 1)
                        v.tensor_copy(turned[:], ptr[:]).then_inc(turnc, 1)
                        link(v.tensor_scalar(t0[:], keyJ[:], float(N), None, ALU.is_lt))
                        link(v.tensor_tensor(rep[:], rep[:], t0[:], ALU.mult))
                        link(v.tensor_scalar(t0[:], rep[:], -FAR, FAR, ALU.mult, ALU.add))
                        link(v.tensor_tensor(t0[:], t0[:], keyJ[:], ALU.add))
                        link(v.tensor_copy(sidx[:, 0:ET], t0[:]))
                        link(v.tensor_copy(dstJ[:, 0:ET], keyJ[:]))
                        link(v.memset(cflag[:], 0.0))
                        link(v.tensor_tensor(cflag[:, 0:ET - 1], keyK[0:1, 1:ET], keyJ[0:1, 0:ET - 1], ALU.is_equal))
                        dve.wait_ge(loaded, 16)
                        link(v.tensor_copy(tabv[:, :, 0], slots[:]))
                        with dve.Fori(0, EI) as i:
                            for r in range(RING):
                                dve.wait_ge(row_in[r], 16 * i + 16)
                                v.tensor_scalar(same[:, bass.ds(i * RING + r, 1), :].rearrange("p a j -> p (a j)"), rowb[:, r, :],
                                                keyK[:, bass.ds(i * RING + r, 1)], None, ALU.is_equal).then_inc(row_free, 1)
                        if with_degree:
                            link(v.tensor_copy(side[:], rep[:, :, None].to_broadcast((P, ET, 3))))
                            link(v.memset(srow[:], 0.0))
                            link(v.tensor_tensor(srow[:, 1:ET], keyJ[0:1, 1:ET], keyJ[0:1, 0:ET - 1], ALU.is_equal))
                            dve.wait_ge(cnt_done, ET)
                            link(v.tensor_copy(cnt[:], pcnt[:, 0:ET]))
                            link(v.tensor_tensor_scan(crow[:], srow[:], cnt[0:1, :], 0.0, ALU.mult, ALU.add))
                            dve.sem_inc(rows_ready, 1)
                            dve.wait_ge(bc_done, 2)
                            link(v.tensor_tensor(cont[:, 1:ET], keyJ[:, 1:ET], pbc[:, 1, 0:ET - 1], ALU.is_equal))
                            link(v.tensor_tensor(cont[:, 1:ET], cont[:, 1:ET], pbc[:, 0, 0:ET - 1], ALU.mult))
                            link(v.tensor_tensor(cnt[:, 1:ET], cnt[:, 1:ET], cont[:, 1:ET], ALU.add))
                            link(v.tensor_scalar(cnt[:], cnt[:], 1.0, None, ALU.add))
                            dve.sem_inc(sq_in, 1)
                            dve.wait_ge(sq_out, 1)
                            link(v.reciprocal(tabv[:, :, 1], t0[:]))
                            link(v.tensor_tensor(dinvrep[:], tabv[:, :, 1], rep[:], ALU.mult))
                            link(v.tensor_tensor(dinv2rep[:], tabv[:, :, 1], dinvrep[:], ALU.mult))
                        else:
                            link(v.memset(tabv[:, :, 1], 0.0))

                        def put_step(i, first):
                            for r in range(RING):
                                if not first:
                                    dve.wait_ge(put[r], 16 * i)
                                copy(vring[:, r, :], tabv[:, bass.ds(i * RING + r, 1), :].rearrange("p a c -> p (a c)")).then_inc(put_ready, 1)
                                copy(iring[:, r:r + 1], sidx[:, bass.ds(i * RING + r, 1)]).then_inc(put_ready, 1)
                        put_step(0, True)
                        with dve.Fori(1, EI) as i:
                            put_step(i, False)
                        for r in range(RING):
                            dve.wait_ge(put[r], 16 * EI)

                        for r in range(RING):
                            copy(iring[:, r:r + 1], other[:, r:r + 1]).then_inc(look_idx, 1)
                        with dve.Fori(0, EI) as i:
                            for r in range(RING):
                                dve.wait_ge(look[r], 16 * i + 16)
                                copy(edge[:, bass.ds(i * RING + r, 1), :].rearrange("p a c -> p (a c)"), vring[:, r, :]).then_inc(looked, 1)
                                copy(iring[:, r:r + 1], other[:, bass.ds(i * RING + r + RING, 1)]).then_inc(look_idx, 1)
                        dve.wait_ge(looked, ET)
                        dve.wait_ge(look_idx, ET + RING)
                        link(v.tensor_scalar(t0[:], edge[:, :, 0], float(NPAD), None, ALU.is_ge))
                        if with_degree:
                            link(v.tensor_copy(idx2[:, 0:ET], edge[:, :, 0]))
                            link(v.tensor_scalar(cnt[:], t0[:], float(NSLOT), None, ALU.mult))
                            link(v.tensor_tensor(cnt[:], cnt[:], edge[:, :, 0], ALU.add))
                            link(v.tensor_copy(idx3[:, 0:ET], cnt[:]))
                            dve.wait_ge(tfl, 16)
                            link(v.tensor_scalar(nonU[:], tfull[:, :, 0], float(NPAD), None, ALU.is_lt))
                        else:
                            link(v.tensor_tensor(w23[:], wK[:], t0[:], ALU.mult))
                            link(v.tensor_scalar(t0[:], t0[:], -FAR, FAR - NPAD, ALU.mult, ALU.add))
                            link(v.tensor_tensor(t0[:], t0[:], edge[:, :, 0], ALU.add))
                            link(v.tensor_copy(idxh[:, 0:ET], t0[:]))

                    @block.gpsimd
                    def _(pool):
                        top = pool.to_reg(NPAD - 1)
                        pool.dma_start(out_table, d["table0"]).then_inc(tinit, 16)
                        pool.wait_ge(tinit, 16)
                        with pool.Fori(0, EI) as i:
                            for r in range(RING):
                                pool.wait_ge(put_ready, 8 * i + 2 * r + 2)
                                pool.sem_inc(begun, 1)
                                pool.indirect_dma_start(out_table, bass.IndirectOffsetOnAxis(ap=iring[:, r:r + 1], axis=0), vring[:, r, :], None,
                                                        bounds_check=top, oob_is_err=False).then_inc(put[r], 16)
                        for r in range(RING):
                            pool.wait_ge(put[r], 16 * EI)
                        if with_degree:
                            pool.dma_start(tfull[:].rearrange("p (s q) c -> p s (q c)", q=4),
                                           out_table.rearrange("(s p q) c -> p s (q c)", p=P, q=4)).then_inc(tfl, 16)

                        def look_step(i, first):
                            for r in range(RING):
                                if not first:
                                    pool.wait_ge(looked, 4 * i + r - 3)
                                pool.wait_ge(look_idx, 4 * i + r + 1)
                                pool.sem_inc(begun, 1)
                                pool.indirect_dma_start(vring[:, r, :], None, out_table, bass.IndirectOffsetOnAxis(ap=iring[:, r:r + 1], axis=0),
                                                        bounds_check=top, oob_is_err=False).then_inc(look[r], 16)
                        look_step(0, True)
                        with pool.Fori(1, EI) as i:
                            look_step(i, False)

        def node_gram_block():
            with ExitStack() as c2:
                xin = c2.enter_context(nc.sbuf_tensor("g_xin", [P, 2, 4, F], F32))
                xm = c2.enter_context(nc.sbuf_tensor("g_xm", [P, 2, 4, XW], F32))
                zero = c2.enter_context(nc.sbuf_tensor("g_zero", [P, XW], F32))
                pg = [c2.enter_context(nc.psum_tensor(f"g_p{k}", [P, XW], F32)) for k in range(3)]
                x_in = sems("g_in", 2)
                masked = sem("g_masked")
                sided = sem("g_side")
                used = sem("g_used")
                stored = sems("g_st", 2)
                zr = sem("g_zr")
                out = sem("g_out")
                xg = d["x"].rearrange("(s p q) f -> s p (q f)", p=P, q=4)
                hg = hist[0:NPAD, :].rearrange("(s p q) f -> s p (q f)", p=P, q=4)
                with nc.Block() as block:
                    @block.sync
                    def _(sp):
                        def step(i, first):
                            for b in range(2):
                                if not first:
                                    sp.wait_ge(masked, 4 * (2 * i + b - 1))
                                sp.dma_start(xin[:, b].rearrange("p q f -> p (q f)"), xg[bass.ds(2 * i + b, 1), :, :].rearrange("a p f -> (a p) f")).then_inc(x_in[b], 16)
                        step(0, True)
                        with sp.Fori(1, GI) as i:
                            step(i, False)

                    @block.gpsimd
                    def _(pool):
                        with pool.Fori(0, GI) as i:
                            for b in range(2):
                                pool.wait_ge(masked, 4 * (2 * i + b + 1))
                                pool.wait_ge(sided, 2 * i + b + 1)
                                pool.dma_start(hg[bass.ds(2 * i + b, 1), :, :].rearrange("a p f -> (a p) f"), xm[:, b].rearrange("p q f -> p (q f)")).then_inc(stored[b], 16)
                        for b in range(2):
                            pool.wait_ge(stored[b], 16 * GI)

                    @block.scalar
                    def _(act):
                        def step(i, first):
                            for b in range(2):
                                act.wait_ge(x_in[b], 16 * i + 16)
                                if not first:
                                    act.wait_ge(used, 2 * i + b - 1)
                                    act.wait_ge(stored[b], 16 * i)
                                for q in range(4):
                                    nc.scalar.activation(xm[:, b, q, 0:F], xin[:, b, q, :], ACT.Copy, scale=nonU[:, bass.ds((2 * i + b) * 4 + q, 1)]).then_inc(masked, 1)
                        step(0, True)
                        with act.Fori(1, GI) as i:
                            step(i, False)

                    @block.vector
                    def _(dve):
                        nc.vector.memset(zero[:], 0.0).then_inc(zr, 1)

                        def step(i, first):
                            for b in range(2):
                                if not first:
                                    dve.wait_ge(used, 2 * i + b - 1)
                                    dve.wait_ge(stored[b], 16 * i)
                                copy(xm[:, b, :, F:XW], nonU[:, bass.ds((2 * i + b) * 4, 4), None].to_broadcast((P, 4, 4))).then_inc(sided, 1)
                        step(0, True)
                        with dve.Fori(1, GI) as i:
                            step(i, False)
                        dve.wait_ge(used, GROUPS + 1)
                        for k in range(3):
                            nc.vector.tensor_copy(gram[0:P if k < 2 else 4, k, 128 * k:XW], pg[k][0:P if k < 2 else 4, 128 * k:XW]).then_inc(out, 1)

                    @block.tensor
                    def _(pe):
                        pe.wait_ge(zr, 1)
                        open_gram(pe, pg, zero)
                        with pe.Fori(0, GI) as i:
                            for b in range(2):
                                pe.wait_ge(masked, 4 * (2 * i + b + 1))
                                pe.wait_ge(sided, 2 * i + b + 1)
                                for q in range(4):
                                    last = add_gram(pe, pg, xm[:, b, q, :])
                                last.then_inc(used, 1)
                        close_gram(pe, pg, zero).then_inc(used, 1)

        def open_gram(pe, pg, zero):
            for k in range(3):
                m = P if k < 2 else 4
                pe.matmul(pg[k][0:m, 128 * k:XW], zero[:, 0:m], zero[:, 128 * k:XW], start=True, stop=False)

        def add_gram(pe, pg, y):
            for k in range(3):
                m = P if k < 2 else 4
                last = pe.matmul(pg[k][0:m, 128 * k:XW], y[:, 128 * k:128 * k + m], y[:, 128 * k:XW], start=False, stop=False)
            return last

        def close_gram(pe, pg, zero):
            for k in range(3):
                m = P if k < 2 else 4
                last = pe.matmul(pg[k][0:m, 128 * k:XW], zero[:, 0:m], zero[:, 128 * k:XW], start=False, stop=True)
            return last

        def carrying_weights(v, link, wcol, weight):
            link(v.tensor_copy(wcol[:], weight))
            link(v.memset(wcol[0:1, :], 1.0))

        def a_pass(k, gout):
            table_of = d["x"] if k == 1 else hist[0:NPAD + (k - 1) * NSLOT, :]
            width = F if k == 1 else XW
            idx = {1: other, 2: idx2, 3: idx3}[k]
            rows = NPAD + (k - 1) * NSLOT
            prev = None if k == 1 else hist[NPAD + (k - 2) * NSLOT:NPAD + (k - 1) * NSLOT, :].rearrange("(u p) f -> u p f", p=P)
            dest = (hist[NPAD + (k - 1) * NSLOT:NPAD + k * NSLOT, :] if k < 3 else cube).rearrange("(u p) f -> u p f", p=P)
            own = xown.rearrange("(u p) f -> u p f", p=P)
            W1 = F + 1
            heads = 2 if k == 1 else 1
            with ExitStack() as c2:
                def tmp(name, shape, dt=F32):
                    return c2.enter_context(nc.sbuf_tensor(f"a{k}_{name}", shape, dt))
                xs = tmp("xs", [P, RING, XW])
                xd = tmp("xd", [P, RING, XW])
                mw = tmp("mw", [P, RING, P])
                yt = tmp("yt", [P, RING, W1])
                y = tmp("y", [P, RING, XW])
                jring = tmp("jring", [P, RING], I32)
                zero = tmp("zero", [P, XW])
                wcol = tmp("wcol", [P, ET])
                ps = [c2.enter_context(nc.psum_tensor(f"a{k}_ps{b}", [P, 512], F32)) for b in range(RING)]
                pg = [c2.enter_context(nc.psum_tensor(f"a{k}_pg{b}", [P, XW], F32)) for b in range(3)]
                s = lambda x: sem(f"a{k}_{x}")
                begun = s("begun")
                chain = s("chain")
                init, idx_ready, mw_ready, head_ready, carried, ps_ready = s("init"), s("idx"), s("mw"), s("head"), s("carried"), s("ps")
                yt_ready, y_ready, gram_done, out = s("yt"), s("y"), s("gram"), s("out")
                got, self_in, stored = sems(f"a{k}_got"), sems(f"a{k}_self"), sems(f"a{k}_st")
                kept = sems(f"a{k}_kept")
                rows_of = "a p f -> (a p) f"
                with nc.Block() as block:
                    @block.gpsimd
                    def _(pool):
                        top = pool.to_reg(rows - 1)
                        pool.wait_ge(init, 3)

                        def step(i, at):
                            for r in range(RING):
                                u = 4 * i + r
                                if at != 0:
                                    pool.wait_ge(ps_ready, u - 3)
                                pool.wait_ge(idx_ready, (2 if k == 1 else 1) * (u + 1))
                                pool.sem_inc(begun, 1)
                                pool.indirect_dma_start(xs[:, r, 0:width], None, table_of, bass.IndirectOffsetOnAxis(ap=iring[:, r:r + 1], axis=0),
                                                        bounds_check=top, oob_is_err=False).then_inc(got[r], 16)
                                if k == 1:
                                    if at != 0:
                                        pool.wait_ge(y_ready, 2 * (u - 3))
                                        pool.wait_ge(kept[r], 16 * i)
                                    pool.sem_inc(begun, 1)
                                    pool.indirect_dma_start(xd[:, r, 0:F], None, table_of, bass.IndirectOffsetOnAxis(ap=jring[:, r:r + 1], axis=0),
                                                            bounds_check=top, oob_is_err=False).then_inc(self_in[r], 16)
                        loop(pool, step)

                    @block.sync
                    def _(sp):
                        sp.wait_ge(init, 3)

                        def step(i, at):
                            for r in range(RING):
                                u = 4 * i + r
                                if k > 1:
                                    if at != 0:
                                        sp.wait_ge(y_ready, 2 * (u - 3))
                                    sp.dma_start(xd[:, r, :], prev[bass.ds(u, 1), :, :].rearrange(rows_of)).then_inc(self_in[r], 16)
                                else:
                                    sp.wait_ge(self_in[r], 16 * i + 16)
                                    sp.dma_start(own[bass.ds(u, 1), :, :].rearrange(rows_of), xd[:, r, 0:F]).then_inc(kept[r], 16)
                        loop(sp, step)
                        if k == 1:
                            for r in range(RING):
                                sp.wait_ge(kept[r], 16 * EI)

                    @block.scalar
                    def _(act):
                        def head(u, r, i):
                            act.wait_ge(got[r], 16 * i + 16)
                            nc.scalar.activation(xs[0:1, r, 0:width], xs[0:1, r, 0:width], ACT.Copy, scale=edge[0:1, bass.ds(u, 1), 1]).then_inc(head_ready, 1)
                            if k == 1:
                                nc.scalar.activation(xs[0:1, r, F:W1], edge[0:1, bass.ds(u, 1), 1], ACT.Copy).then_inc(head_ready, 1)

                        def scaled(u, r, waits):
                            act.wait_ge(ps_ready, u + 1)
                            if waits:
                                act.wait_ge(y_ready, 2 * (u - 3))
                            nc.scalar.activation(yt[:, r, :], ps[r][:, 0:W1], ACT.Copy, scale=dinvrep[:, bass.ds(u, 1)]).then_inc(yt_ready, 1)

                        def store(u, r):
                            act.wait_ge(y_ready, 2 * (u + 1))
                            act.dma_start(dest[bass.ds(u, 1), :, :].rearrange(rows_of), y[:, r, :]).then_inc(stored[r], 16)

                        act.wait_ge(init, 3)
                        head(0, 0, 0)

                        def step(i, at):
                            for r in range(RING):
                                u = 4 * i + r
                                if not (at == EI - 1 and r == 3):
                                    head(u + 1, (r + 1) % 4, i + (1 if r == 3 else 0))
                                if not (at == 0 and r == 0):
                                    act.wait_ge(carried, u)
                                    scaled(u - 1, (r - 1) % 4, not (at == 0 or (at == 1 and r == 0)))
                                if not (at == 0 and r < 3):
                                    store(u - 3, (r - 3) % 4)
                        loop(act, step, 2)
                        scaled(ET - 1, 3, True)
                        for u in range(ET - 3, ET):
                            store(u, u % 4)
                        for r in range(RING):
                            act.wait_ge(stored[r], 16 * EI)

                    @block.vector
                    def _(dve):
                        v = nc.vector
                        v.memset(zero[:], 0.0).then_inc(init, 1)
                        v.memset(xs[:], 1.0).then_inc(init, 1)
                        v.memset(xd[:], 1.0).then_inc(init, 1)
                        carrying_weights(v, linker(dve, chain), wcol, edge[:, :, 1])

                        def idx_copy(u, r):
                            copy(iring[:, r:r + 1], idx[:, bass.ds(u, 1)]).then_inc(idx_ready, 1)
                            if k == 1:
                                copy(jring[:, r:r + 1], dstJ[:, bass.ds(u, 1)]).then_inc(idx_ready, 1)

                        def prepare(u, r, waits):
                            if waits:
                                dve.wait_ge(ps_ready, u - 3)
                            v.tensor_scalar(mw[:, r, :], same[:, bass.ds(u, 1), :].rearrange("p a j -> p (a j)"), wcol[:, bass.ds(u, 1)], None, ALU.mult).then_inc(mw_ready, 1)

                        def carry(u, r):
                            dve.wait_ge(head_ready, heads * (u + 1))
                            dve.wait_ge(ps_ready, u)
                            v.scalar_tensor_tensor(xs[0:1, r, 0:W1], ps[(r - 1) % 4][0:1, 0:W1], cflag[:, bass.ds(u - 1, 1)], xs[0:1, r, 0:W1],
                                                   ALU.mult, ALU.add).then_inc(carried, 1)

                        def finish(u, r, waits, i):
                            dve.wait_ge(self_in[r], 16 * i + 16)
                            dve.wait_ge(yt_ready, u + 1)
                            if waits:
                                dve.wait_ge(gram_done, u - 3)
                                dve.wait_ge(stored[r], 16 * i)
                            v.scalar_tensor_tensor(y[:, r, 0:W1], xd[:, r, 0:W1], dinv2rep[:, bass.ds(u, 1)], yt[:, r, :], ALU.mult, ALU.add).then_inc(y_ready, 1)
                            copy(y[:, r, W1:XW], side[:, bass.ds(u, 1), :].rearrange("p a c -> p (a c)")).then_inc(y_ready, 1)
                            if k < 3:
                                dve.wait_ge(y_ready, 2 * (u + 1))
                                copy(side[:, bass.ds(u, 1), 2 - k], y[:, r, F:W1]).then_inc(out, 1)

                        for r in range(RING):
                            idx_copy(r, r)
                        for r in range(2):
                            prepare(r, r, False)

                        def step(i, at):
                            for r in range(RING):
                                u = 4 * i + r
                                if not (at == 0 and r == 0):
                                    carry(u, r)
                                if not (at == EI - 1 and r >= 2):
                                    prepare(u + 2, (r + 2) % 4, not (at == 0 and r < 2))
                                if not (at == 0 and r < 2):
                                    finish(u - 2, (r - 2) % 4, not (at == 0 or (at == 1 and r < 2)), i - (1 if r < 2 else 0))
                                dve.wait_ge(got[r], 16 * i + 16)
                                if k == 1:
                                    dve.wait_ge(self_in[r], 16 * i + 16)
                                idx_copy(u + RING, r)
                        loop(dve, step, 2)
                        for r in (2, 3):
                            finish(ET - 4 + r, r, True, EI - 1)
                        dve.wait_ge(gram_done, ET + 1)
                        for b in range(3):
                            m = P if b < 2 else 4
                            v.tensor_tensor(gout[0:m, b, 128 * b:XW], gram[0:m, b, 128 * b:XW], pg[b][0:m, 128 * b:XW], ALU.add).then_inc(out, 1)

                    @block.tensor
                    def _(pe):
                        pe.wait_ge(init, 3)
                        open_gram(pe, pg, zero)

                        def step(i, at):
                            for r in range(RING):
                                u = 4 * i + r
                                pe.wait_ge(mw_ready, u + 1)
                                if at != 0:
                                    pe.wait_ge(yt_ready, u - 3)
                                if at == 0 and r == 0:
                                    pe.wait_ge(head_ready, heads)
                                else:
                                    pe.wait_ge(carried, u)
                                pe.matmul(ps[r][:, 0:W1], mw[:, r, :], xs[:, r, 0:W1], start=True, stop=True).then_inc(ps_ready, 1)
                                if not (at == 0 and r < 3):
                                    pe.wait_ge(y_ready, 2 * (u - 2))
                                    add_gram(pe, pg, y[:, (r - 3) % 4, :]).then_inc(gram_done, 1)
                        loop(pe, step)
                        for u in range(ET - 3, ET):
                            pe.wait_ge(y_ready, 2 * (u + 1))
                            add_gram(pe, pg, y[:, u % 4, :]).then_inc(gram_done, 1)
                        close_gram(pe, pg, zero).then_inc(gram_done, 1)

        wa = [[sb(f"w_{k}_{c}", [P, F]) for c in range(2)] for k in (1, 2, 3)]
        hc = sb("hc", [4, F])
        hmap = [sb(f"hmap{c}", [P, F]) for c in range(2)]
        gk = [sb(f"gram{k}", [P, 3, XW]) for k in (1, 2, 3)]

        kept_w = [sb(f"l1w{k}", [P, 2, F]) for k in range(4)]
        hsplit = sb("hsplit", [68, F], BF16)
        oneb = sb("oneb", [68, P], BF16)
        epsc = sb("epsc", [P, 1])

        def norm_block():
            with ExitStack() as c2:
                def tmp(name, shape, dt=F32):
                    return c2.enter_context(nc.sbuf_tensor(f"n_{name}", shape, dt))
                gb = tmp("gb", [P, 3, 2, F])
                wl = tmp("wl", [P, 3, 2, F])
                b1 = tmp("b1", [4, F])
                brow = tmp("brow", [1, 3, F])
                e3 = tmp("e3", [1, 4])
                e3c = tmp("e3c", [4, 1])
                w = [tmp(f"w{c}", [P if c < 2 else 4, F]) for c in range(3)]
                cov = [tmp(f"cov{c}", [P if c < 2 else 4, XW]) for c in range(3)]
                mbc = tmp("mbc", [P, 3, P])
                mrow = tmp("mrow", [1, XW])
                prod = [tmp(f"prod{c}", [P if c < 2 else 4, F]) for c in range(3)]
                mean = tmp("mean", [P, F])
                var = tmp("var", [P, F])
                sd = tmp("sd", [P, F])
                sc = tmp("sc", [P, F])
                shift = tmp("shift", [P, F])
                hT = tmp("hT", [P, 2, XW])
                hTc = tmp("hTc", [P, 2, 4])
                t4 = tmp("t4", [4, F])
                pa, pb, pc, pd = [c2.enter_context(nc.psum_tensor(f"n_p{x}", [P, 512], F32)) for x in "abcd"]
                ld, dv, pt, sq = sem("n_loaded"), sem("n_dve"), sem("n_pe"), sem("n_sqrt")
                chain = sem("n_chain")
                halves = "(c p) f -> p c f"
                hs = (P, P, 4)
                with nc.Block() as block:
                    @block.sync
                    def _(sp):
                        for k in range(3):
                            sp.dma_start(gb[:, k, 0, :], d[f"g{k + 1}"].to_broadcast((P, F))).then_inc(ld, 16)
                            sp.dma_start(gb[:, k, 1, :], d[f"be{k + 1}"].to_broadcast((P, F))).then_inc(ld, 16)
                            sp.dma_start(wl[:, k, :, :], d[f"W{k + 1}"].rearrange(halves, p=P)).then_inc(ld, 16)
                            sp.dma_start(brow[:, k, :], d[f"b{k + 1}"]).then_inc(ld, 16)
                        sp.dma_start(b1[:], d["b1"].to_broadcast((4, F))).then_inc(ld, 16)
                        sp.dma_start(e3[:], d["e3"]).then_inc(ld, 16)
                        sp.dma_start(e3c[:], d["e3c"]).then_inc(ld, 16)
                        for k in range(4):
                            sp.dma_start(kept_w[k][:], d["L1W"][k].rearrange(halves, p=P)).then_inc(ld, 16)

                    @block.scalar
                    def _(act):
                        for k in range(3):
                            act.wait_ge(dv, 7 * k + 5)
                            nc.scalar.activation(sd[:], var[:], ACT.Sqrt).then_inc(sq, 1)

                    @block.tensor
                    def _(pe):
                        pe.wait_ge(ld, 16 * 19)
                        for k in range(3):
                            g = gk[k]
                            pe.wait_ge(dv, 7 * k + 1)
                            pe.transpose(pa[:, 0:P], g[:, 0, P:2 * P], ident[:])
                            pe.transpose(pa[0:4, P:2 * P], g[:, 0, 2 * P:XW], ident[:])
                            pe.transpose(pa[0:4, 2 * P:3 * P], g[:, 1, 2 * P:XW], ident[:])
                            pe.transpose(pb[0:1, 0:P], g[:, 0, XW - 1:XW], ident[:])
                            pe.transpose(pb[0:1, P:2 * P], g[:, 1, XW - 1:XW], ident[:])
                            pe.transpose(pb[0:1, 2 * P:XW], g[0:4, 2, XW - 1:XW], ident[0:4, 0:4]).then_inc(pt, 1)
                            pe.wait_ge(dv, 7 * k + 2)
                            for c, p in enumerate((pa, pb, pc)):
                                last = pe.matmul(p[0:hs[c], 0:XW], mrow[:, P * c:P * c + hs[c]], mrow[:], start=True, stop=True)
                            last.then_inc(pt, 1)
                            pe.wait_ge(dv, 7 * k + 3)
                            for m, p in enumerate((pa, pb, pc, pd)):
                                for c in range(3):
                                    lhsT = cov[c][:, P * m:P * m + hs[m]] if m < 3 else mbc[0:hs[c], c, :]
                                    last = pe.matmul(p[0:hs[m] if m < 3 else P, 0:F], lhsT, w[c][:], start=(c == 0), stop=(c == 2))
                            last.then_inc(pt, 1)
                            pe.wait_ge(dv, 7 * k + 4)
                            for c in range(3):
                                last = pe.matmul(pa[:, 0:F], onesf[0:hs[c], :], prod[c][:], start=(c == 0), stop=(c == 2))
                            last.then_inc(pt, 1)
                            if k < 2:
                                pe.wait_ge(dv, 7 * k + 6)
                                for c, p in enumerate((pa, pb)):
                                    for m in range(3):
                                        last = pe.transpose(p[:, P * m:P * m + hs[m]], w[m][:, P * c:P * c + P], ident[0:hs[m], 0:hs[m]])
                                last.then_inc(pt, 1)
                                pe.wait_ge(dv, 7 * k + 7)
                                for m, p in enumerate((pa, pb, pc)):
                                    for c in range(2):
                                        lhsT = hT[:, c, P * m:P * m + P] if m < 2 else hTc[:, c, :]
                                        last = pe.matmul(p[0:hs[m], 0:F], lhsT, wl[:, k + 1, c, :], start=(c == 0), stop=(c == 1 and m < 2))
                                last = pe.matmul(pc[0:4, 0:F], e3[:], brow[:, k + 1, :], start=False, stop=True)
                                last.then_inc(pt, 1)

                    @block.vector
                    def _(dve):
                        v = nc.vector
                        n = [0]

                        def link(ins):
                            n[0] += 1
                            ins.then_inc(chain, 1)
                            dve.wait_ge(chain, n[0])
                        dve.wait_ge(ld, 16 * 19)
                        for c in range(2):
                            link(v.tensor_copy(w[c][:], wl[:, 0, c, :]))
                        link(v.tensor_scalar(w[2][:], b1[:], e3c[:], None, ALU.mult))
                        for k in range(3):
                            g = gk[k]
                            dve.sem_inc(dv, 1)
                            dve.wait_ge(pt, 6 * k + 1)
                            link(v.tensor_scalar(cov[0][:], g[:, 0, :], 1.0 / N, None, ALU.mult))
                            link(v.tensor_scalar(cov[1][:, 0:P], pa[:, 0:P], 1.0 / N, None, ALU.mult))
                            link(v.tensor_scalar(cov[1][:, P:XW], g[:, 1, P:XW], 1.0 / N, None, ALU.mult))
                            link(v.tensor_scalar(cov[2][:, 0:2 * P], pa[0:4, P:3 * P], 1.0 / N, None, ALU.mult))
                            link(v.tensor_scalar(cov[2][:, 2 * P:XW], g[0:4, 2, 2 * P:XW], 1.0 / N, None, ALU.mult))
                            link(v.tensor_scalar(mrow[:], pb[0:1, 0:XW], 1.0 / N, None, ALU.mult))
                            for c in range(3):
                                link(v.tensor_copy(mbc[0:hs[c], c, :], cov[c][:, XW - 1:XW].to_broadcast((hs[c], P))))
                            dve.sem_inc(dv, 1)
                            dve.wait_ge(pt, 6 * k + 2)
                            for c, p in enumerate((pa, pb, pc)):
                                link(v.tensor_tensor(cov[c][:], cov[c][:], p[0:hs[c], 0:XW], ALU.subtract))
                            dve.sem_inc(dv, 1)
                            dve.wait_ge(pt, 6 * k + 3)
                            for c, p in enumerate((pa, pb, pc)):
                                link(v.tensor_tensor(prod[c][:], w[c][:], p[0:hs[c], 0:F], ALU.mult))
                            link(v.tensor_copy(mean[:], pd[:, 0:F]))
                            dve.sem_inc(dv, 1)
                            dve.wait_ge(pt, 6 * k + 4)
                            link(v.tensor_scalar(var[:], pa[:, 0:F], 0.0, EPS, ALU.max, ALU.add))
                            dve.sem_inc(dv, 1)
                            dve.wait_ge(sq, k + 1)
                            link(v.reciprocal(sc[:], sd[:]))
                            link(v.tensor_tensor(sc[:], sc[:], gb[:, k, 0, :], ALU.mult))
                            link(v.tensor_tensor(shift[:], mean[:], sc[:], ALU.mult))
                            link(v.tensor_tensor(shift[:], gb[:, k, 1, :], shift[:], ALU.subtract))
                            for c in range(3):
                                link(v.tensor_tensor(w[c][:], w[c][:], sc[0:hs[c], :], ALU.mult))
                            link(v.scalar_tensor_tensor(w[2][:], shift[0:4, :], e3c[:], w[2][:], ALU.mult, ALU.add))
                            dve.sem_inc(dv, 1)
                            if k < 2:
                                dve.wait_ge(pt, 6 * k + 5)
                                link(v.memset(hTc[:], 0.0))
                                for c, p in enumerate((pa, pb)):
                                    link(v.tensor_copy(hT[:, c, :], p[:, 0:XW]))
                                    link(v.tensor_copy(hTc[:, c, 0:3], p[:, F + 1:XW]))
                                dve.sem_inc(dv, 1)
                                dve.wait_ge(pt, 6 * k + 6)
                                for c, p in enumerate((pa, pb, pc)):
                                    link(v.tensor_copy(w[c][:], p[0:hs[c], 0:F]))
                            else:
                                for c in range(2):
                                    link(v.tensor_copy(hmap[c][:], w[c][:]))
                                link(v.tensor_copy(hc[:], w[2][:]))
                                link(v.memset(hsplit[:], 0.0))
                                link(v.memset(oneb[:], 1.0))
                                link(v.memset(epsc[:], EPS))
                                for part in range(3):
                                    link(v.tensor_copy(hsplit[32 * part:32 * part + 4, :], w[2][:]))
                                    if part < 2:
                                        link(v.tensor_copy(t4[:], hsplit[32 * part:32 * part + 4, :]))
                                        link(v.tensor_tensor(w[2][:], w[2][:], t4[:], ALU.subtract))

        def dense_block(name, rows, w, constant, dest):
            B = 4
            with ExitStack() as c2:
                def tmp(x, shape, dt=F32):
                    return c2.enter_context(nc.sbuf_tensor(f"{name}_{x}", shape, dt))
                xin, t, o = [tmp(x, [P, 2, 4, F]) for x in ("xin", "t", "o")]
                xT = tmp("xT", [P, B, 2, P])
                st, mv, pad = tmp("st", [P, 4, 6]), tmp("mv", [P, 4, 2]), tmp("pad", [P, 1])
                sd, rs, nm = tmp("sd", [P, 4]), tmp("rs", [P, 4]), tmp("nm", [P, 4])
                pT = [c2.enter_context(nc.psum_tensor(f"{name}_pT{x}", [P, 2, P], F32)) for x in range(B)]
                pz = [c2.enter_context(nc.psum_tensor(f"{name}_pz{x}", [P, F], F32)) for x in range(B)]
                s = lambda x: sem(f"{name}_{x}")
                t_done, xt_ready, mm_done, add_done, st_done, mv_done, sd_done, r_done, rs_done, ready = [
                    s(x) for x in ("T", "xT", "mm", "add", "stats", "mv", "sd", "r", "rs", "ready")]
                x_in, stored = sems(f"{name}_in", 2), sems(f"{name}_st", 2)
                xg = rows.rearrange("(s p q) f -> s p (q f)", p=P, q=4)
                og = dest.rearrange("(s p q) f -> s p (q f)", p=P, q=4)
                rows_of = "a p f -> (a p) f"
                free = "p q f -> p (q f)"

                def ends(eng, step):
                    step(0, True, False)
                    with eng.Fori(1, GI - 1) as i:
                        step(i, False, False)
                    step(GI - 1, False, True)

                with nc.Block() as block:
                    @block.sync
                    def _(sp):
                        def load(g, b):
                            sp.dma_start(xin[:, b].rearrange(free), xg[bass.ds(g, 1), :, :].rearrange(rows_of)).then_inc(x_in[b], 16)
                        load(0, 0)
                        load(1, 1)

                        def step(i, first, last):
                            for b in range(2):
                                g = 2 * i + b
                                if not last:
                                    sp.wait_ge(add_done, 4 * (g + 1))
                                    load(g + 2, b)
                                if not (first and b == 0):
                                    sp.wait_ge(ready, 4 * g)
                                    sp.dma_start(og[bass.ds(g - 1, 1), :, :].rearrange(rows_of), o[:, 1 - b].rearrange(free)).then_inc(stored[1 - b], 16)
                        ends(sp, step)
                        sp.wait_ge(ready, NT)
                        sp.dma_start(og[GROUPS - 1], o[:, 1].rearrange(free)).then_inc(stored[1], 16)
                        for b in range(2):
                            sp.wait_ge(stored[b], 16 * GI)

                    @block.tensor
                    def _(pe):
                        def product(n, un, waits):
                            pe.wait_ge(xt_ready, un + 1)
                            if waits:
                                pe.wait_ge(add_done, un - B + 1)
                            for c in range(2):
                                last = pe.matmul(pz[n][:], xT[:, n, c, :], w[c], start=(c == 0), stop=(c == 1 and not constant))
                            if constant:
                                last = pe.matmul(pz[n][:], oneb[:], hsplit[:], start=False, stop=True)
                            last.then_inc(mm_done, 1)

                        def step(i, first, last):
                            for b in range(2):
                                for q in range(4):
                                    un = 8 * i + 4 * b + q
                                    if q == 0:
                                        pe.wait_ge(x_in[b], 16 * i + 16)
                                    if not (first and b == 0):
                                        pe.wait_ge(xt_ready, un - B + 1)
                                    pe.transpose(pT[q][:, 0, :], xin[:, b, q, 0:P], ident[:])
                                    pe.transpose(pT[q][:, 1, :], xin[:, b, q, P:F], ident[:]).then_inc(t_done, 1)
                                    if not (first and b == 0 and q == 0):
                                        product((q - 1) % 4, un - 1, not (first and 4 * b + q <= B))
                        ends(pe, step)
                        product(3, NT - 1, True)

                    @block.scalar
                    def _(act):
                        a = nc.scalar

                        def norm(g, b, q):
                            if q == 0:
                                act.wait_ge(rs_done, g + 1)
                            a.activation(o[:, b, q, :], t[:, b, q, :], ACT.Identity, bias=nm[:, q:q + 1], scale=rs[:, q:q + 1]).then_inc(ready, 1)

                        def deviation(g):
                            act.wait_ge(mv_done, 4 * (g + 1))
                            a.activation(sd[:], mv[:, :, 1], ACT.Sqrt, bias=epsc[:]).then_inc(sd_done, 1)

                        def step(i, first, last):
                            for b in range(2):
                                g = 2 * i + b
                                lag = not (first and b == 0)
                                for q in range(4):
                                    un = 8 * i + 4 * b + q
                                    act.wait_ge(t_done, un + 1)
                                    if lag:
                                        act.wait_ge(mm_done, un - B + 1)
                                    a.activation(xT[:, q, :, :], pT[q][:], ACT.Copy).then_inc(xt_ready, 1)
                                    if lag and q == 0:
                                        deviation(g - 1)
                                    if lag and q >= 2:
                                        if q == 2 and not first:
                                            act.wait_ge(stored[1 - b], 16 * i if b == 1 else 16 * (i - 1))
                                        norm(g - 1, 1 - b, 2 * (q - 2))
                                        norm(g - 1, 1 - b, 2 * (q - 2) + 1)
                        ends(act, step)
                        deviation(GROUPS - 1)
                        act.wait_ge(stored[1], 16 * (GI - 1))
                        for q in range(4):
                            norm(GROUPS - 1, 1, q)

                    @block.vector
                    def _(dve):
                        v = nc.vector

                        def scales(g):
                            dve.wait_ge(sd_done, g + 1)
                            v.reciprocal(rs[:], sd[:]).then_inc(r_done, 1)
                            dve.wait_ge(r_done, g + 1)
                            v.scalar_tensor_tensor(nm[:], mv[:, :, 0], -1.0, rs[:], ALU.mult, ALU.mult).then_inc(rs_done, 1)

                        def step(i, first, last):
                            for b in range(2):
                                g = 2 * i + b
                                lag = not (first and b == 0)
                                for q in range(4):
                                    un = 8 * i + 4 * b + q
                                    if lag and q == 1:
                                        scales(g - 1)
                                    dve.wait_ge(mm_done, un + 1)
                                    if q == 0 and lag:
                                        dve.wait_ge(ready, 4 * (g - 1))
                                    v.tensor_tensor(t[:, b, q, :], pz[q][:], xin[:, b, q, :], ALU.add).then_inc(add_done, 1)
                                    dve.wait_ge(add_done, un + 1)
                                    v.bn_stats(st[:, q, :], t[:, b, q, :]).then_inc(st_done, 1)
                                dve.wait_ge(st_done, 4 * (g + 1))
                                if lag:
                                    dve.wait_ge(rs_done, g)
                                v.memset(pad[:], 0.0)
                                for q in range(4):
                                    v.bn_aggr(mv[:, q, :], st[:, q, :]).then_inc(mv_done, 1)
                        ends(dve, step)
                        scales(GROUPS - 1)

        class TileNorm:
            def __init__(self, c2, name):
                def tmp(x, shape):
                    return c2.enter_context(nc.sbuf_tensor(f"{name}_{x}", shape, F32))
                self.t, self.o = tmp("t", [P, RING, F]), tmp("o", [P, RING, F])
                self.st, self.mv = tmp("st", [P, RING, 6]), tmp("mv", [P, RING, 2])
                self.pad = tmp("pad", [P, 1])
                self.sd, self.rs, self.nm = tmp("sd", [P, RING]), tmp("rs", [P, RING]), tmp("nm", [P, RING])
                self.add_done, self.st_done, self.mv_done, self.sd_done, self.r_done, self.rs_done, self.ready = [
                    sem(f"{name}_{x}") for x in ("add", "stats", "mv", "sd", "r", "rs", "normed")]

            def moments(self, dve, u, r, a, b, waits):
                v = nc.vector
                if waits:
                    dve.wait_ge(self.ready, u - 3)
                v.tensor_tensor(self.t[:, r, :], a, b, ALU.add).then_inc(self.add_done, 1)
                dve.wait_ge(self.add_done, u + 1)
                v.bn_stats(self.st[:, r, :], self.t[:, r, :]).then_inc(self.st_done, 1)
                dve.wait_ge(self.st_done, u + 1)
                v.memset(self.pad[:], 0.0)
                v.bn_aggr(self.mv[:, r, :], self.st[:, r, :]).then_inc(self.mv_done, 1)

            def deviation(self, act, u, r):
                act.wait_ge(self.mv_done, u + 1)
                nc.scalar.activation(self.sd[:, r:r + 1], self.mv[:, r, 1:2], ACT.Sqrt, bias=epsc[:]).then_inc(self.sd_done, 1)

            def scales(self, dve, u, r):
                v = nc.vector
                dve.wait_ge(self.sd_done, u + 1)
                v.reciprocal(self.rs[:, r:r + 1], self.sd[:, r:r + 1]).then_inc(self.r_done, 1)
                dve.wait_ge(self.r_done, u + 1)
                v.scalar_tensor_tensor(self.nm[:, r:r + 1], self.mv[:, r, 0:1], -1.0, self.rs[:, r:r + 1], ALU.mult, ALU.mult).then_inc(self.rs_done, 1)

            def normed(self, act, u, r):
                act.wait_ge(self.rs_done, u + 1)
                nc.scalar.activation(self.o[:, r, :], self.t[:, r, :], ACT.Identity, bias=self.nm[:, r:r + 1], scale=self.rs[:, r:r + 1]).then_inc(self.ready, 1)

        class NodeTiles:
            def __init__(self, c2, name, base):
                def tmp(x, shape):
                    return c2.enter_context(nc.sbuf_tensor(f"{name}_{x}", shape, F32))
                self.base = base
                self.zin, self.zT = tmp("zin", [P, RING, F]), tmp("zT", [P, RING, 2, P])
                self.ln = TileNorm(c2, name)
                self.pT = [c2.enter_context(nc.psum_tensor(f"{name}_pT{x}", [P, 2, P], F32)) for x in range(2)]
                self.pz = [c2.enter_context(nc.psum_tensor(f"{name}_pz{x}", [P, F], F32)) for x in range(2)]
                self.t_done, self.zt_ready, self.mm_done = [sem(f"{name}_{x}") for x in ("T", "zT", "mm")]
                self.z_in, self.stored = sems(f"{name}_in"), sems(f"{name}_st")
                self.src = zrow.rearrange("(u p) f -> u p f", p=P)
                self.dst = d["out"].rearrange("(u p) f -> u p f", p=P)

            def load(self, sp, u, r, at):
                if at != 0:
                    sp.wait_ge(self.ln.add_done, u - 3)
                sp.dma_start(self.zin[:, r, :], self.src[bass.ds(u + self.base, 1), :, :].rearrange("a p f -> (a p) f")).then_inc(self.z_in[r], 16)

            def store(self, sp, u, r):
                sp.wait_ge(self.ln.ready, u + 1)
                sp.dma_start(self.dst[bass.ds(u + self.base, 1), :, :].rearrange("a p f -> (a p) f"), self.ln.o[:, r, :]).then_inc(self.stored[r], 16)

            def all_stored(self, sp):
                for r in range(RING):
                    sp.wait_ge(self.stored[r], 16 * EI)

            def turn(self, pe, u, r, i, at):
                pe.wait_ge(self.z_in[r], 16 * i + 16)
                if not (at == 0 and r < 2):
                    pe.wait_ge(self.zt_ready, u - 1)
                for c in range(2):
                    last = pe.transpose(self.pT[r % 2][:, c, :], self.zin[:, r, P * c:P * c + P], ident[:])
                last.then_inc(self.t_done, 1)

            def product(self, pe, u, r, waits):
                pe.wait_ge(self.zt_ready, u + 1)
                if waits:
                    pe.wait_ge(self.ln.add_done, u - 1)
                for c in range(2):
                    last = pe.matmul(self.pz[r % 2][:], self.zT[:, r, c, :], kept_w[0][:, c, :], start=(c == 0), stop=(c == 1))
                last.then_inc(self.mm_done, 1)

            def turned(self, act, u, r, at):
                act.wait_ge(self.t_done, u + 1)
                if at != 0:
                    act.wait_ge(self.mm_done, u - 3)
                nc.scalar.activation(self.zT[:, r, :, :], self.pT[r % 2][:], ACT.Copy).then_inc(self.zt_ready, 1)

            def sums(self, dve, u, r, waits):
                dve.wait_ge(self.mm_done, u + 1)
                self.ln.moments(dve, u, r, self.pz[r % 2][:], self.zin[:, r, :], waits)

            def norm(self, act, u, r, waits):
                if waits is not None:
                    act.wait_ge(self.stored[r], waits)
                self.ln.normed(act, u, r)

        def slots_block():
            with ExitStack() as c2:
                def tmp(name, shape, dt=F32):
                    return c2.enter_context(nc.sbuf_tensor(f"s_{name}", shape, dt))
                yin, xd = tmp("yin", [P, RING, XW]), tmp("xd", [P, RING, F])
                xT, xTc = tmp("xT", [P, 2, F]), tmp("xTc", [4, 2, P])
                jring, kring = tmp("jring", [P, RING], I32), tmp("kring", [P, RING], I32)
                k_ready = sem("s_k")
                ln = TileNorm(c2, "s_ln")
                begun = sem("s_begun")
                pT = [c2.enter_context(nc.psum_tensor(f"s_pT{x}", [P, 512], F32)) for x in range(2)]
                pz = [c2.enter_context(nc.psum_tensor(f"s_pz{x}", [P, F], F32)) for x in range(2)]
                idx_ready, t_done, xt_ready, mm_done = [sem(f"s_{x}") for x in ("idx", "T", "xT", "mm")]
                got, y_in, stored = sems("s_got"), sems("s_in"), sems("s_st")
                cv = cube.rearrange("(u p) f -> u p f", p=P)
                xv = xown.rearrange("(u p) f -> u p f", p=P)
                flat_ = "a p f -> (a p) f"
                with nc.Block() as block:
                    @block.sync
                    def _(sp):
                        def step(i, at):
                            for r in range(RING):
                                u = 4 * i + r
                                if at != 0:
                                    sp.wait_ge(t_done, u - 3)
                                sp.dma_start(yin[:, r, :], cv[bass.ds(u, 1), :, :].rearrange(flat_)).then_inc(y_in[r], 16)
                                if at != 0:
                                    sp.wait_ge(ln.add_done, u - 3)
                                sp.dma_start(xd[:, r, :], xv[bass.ds(u, 1), :, :].rearrange(flat_)).then_inc(got[r], 16)
                        loop(sp, step)

                    @block.gpsimd
                    def _(pool):
                        top = pool.to_reg(NPAD - 1)

                        def scatter(u, r):
                            pool.wait_ge(ln.ready, u + 1)
                            pool.wait_ge(k_ready, u + 1)
                            pool.sem_inc(begun, 1)
                            pool.indirect_dma_start(zrow, bass.IndirectOffsetOnAxis(ap=kring[:, r:r + 1], axis=0), ln.o[:, r, :], None,
                                                    bounds_check=top, oob_is_err=False).then_inc(stored[r], 16)

                        def step(i, at):
                            for r in range(RING):
                                u = 4 * i + r
                                scatter(u, r)
                        loop(pool, step)
                        for r in range(RING):
                            pool.wait_ge(stored[r], 16 * EI)

                    @block.tensor
                    def _(pe):
                        def product(u, r, waits):
                            pe.wait_ge(xt_ready, 2 * (u + 1))
                            if waits:
                                pe.wait_ge(ln.add_done, u - 1)
                            p = pz[r % 2]
                            for c in range(2):
                                pe.matmul(p[:], xT[:, r % 2, P * c:P * c + P], hmap[c][:], start=(c == 0), stop=False)
                            pe.matmul(p[:], xTc[:, r % 2, :], hc[:], start=False, stop=True).then_inc(mm_done, 1)

                        def step(i, at):
                            for r in range(RING):
                                u = 4 * i + r
                                pe.wait_ge(y_in[r], 16 * i + 16)
                                if not (at == 0 and r < 2):
                                    pe.wait_ge(xt_ready, 2 * (u - 1))
                                p = pT[r % 2]
                                pe.transpose(p[:, 0:P], yin[:, r, 0:P], ident[:])
                                pe.transpose(p[:, P:F], yin[:, r, P:F], ident[:])
                                pe.transpose(p[0:4, F:F + P], yin[:, r, F:XW], ident[:]).then_inc(t_done, 1)
                                if not (at == 0 and r == 0):
                                    product(u - 1, (r - 1) % 4, not (at == 0 and r < 3))
                        loop(pe, step)
                        product(ET - 1, 3, True)

                    @block.scalar
                    def _(act):
                        def norm(u, r, waits):
                            if waits is not None:
                                act.wait_ge(stored[r], waits)
                            ln.normed(act, u, r)

                        def step(i, at):
                            for r in range(RING):
                                u = 4 * i + r
                                act.wait_ge(t_done, u + 1)
                                if not (at == 0 and r < 2):
                                    act.wait_ge(mm_done, u - 1)
                                nc.scalar.activation(xT[:, r % 2, :], pT[r % 2][:, 0:F], ACT.Copy).then_inc(xt_ready, 1)
                                nc.scalar.activation(xTc[:, r % 2, :], pT[r % 2][0:4, F:F + P], ACT.Copy).then_inc(xt_ready, 1)
                                if not (at == 0 and r < 2):
                                    ln.deviation(act, u - 2, (r - 2) % 4)
                                if not (at == 0 and r < 3):
                                    norm(u - 3, (r - 3) % 4, None if at == 0 else (16 * i if r == 3 else 16 * (i - 1)))
                        loop(act, step)
                        for u in (ET - 2, ET - 1):
                            ln.deviation(act, u, u % 4)
                        for u in range(ET - 3, ET):
                            norm(u, u % 4, 16 * (EI - 1))

                    @block.vector
                    def _(dve):
                        v = nc.vector
                        def finish(i, r, waits):
                            u = 4 * i + r
                            dve.wait_ge(mm_done, u + 1)
                            dve.wait_ge(got[r], 16 * i + 16)
                            ln.moments(dve, u, r, pz[r % 2][:], xd[:, r, :], waits)
                            if waits:
                                dve.wait_ge(stored[r], 16 * i)
                            copy(kring[:, r:r + 1], sidx[:, bass.ds(u, 1)]).then_inc(k_ready, 1)

                        def step(i, at):
                            for r in range(RING):
                                finish(i, r, at != 0)
                                if not (at == 0 and r < 2):
                                    ln.scales(dve, 4 * i + r - 2, (r - 2) % 4)
                        loop(dve, step)
                        for u in (ET - 2, ET - 1):
                            ln.scales(dve, u, u % 4)

        def hop_pass(k):
            table_of, rows = {1: (zrow, NPAD), 2: (hop1, NSLOT), 3: (hop2, NSLOT)}[k]
            idx, weight = (other, wK) if k == 1 else (idxh, w23)
            dest = None if k == 3 else (hop1, hop2)[k - 1].rearrange("(u p) f -> u p f", p=P)
            with ExitStack() as c2:
                def tmp(name, shape, dt=F32):
                    return c2.enter_context(nc.sbuf_tensor(f"h{k}_{name}", shape, dt))
                xs, h = tmp("xs", [P, RING, F]), tmp("h", [P, RING, F])
                mw, wcol = tmp("mw", [P, RING, P]), tmp("wcol", [P, ET])
                ps = [c2.enter_context(nc.psum_tensor(f"h{k}_ps{b}", [P, F], F32)) for b in range(RING)]
                s = lambda x: sem(f"h{k}_{x}")
                begun = s("begun")
                init, idx_ready, mw_ready, ps_ready, h_ready = s("init"), s("idx"), s("mw"), s("ps"), s("h")
                head_ready, carried, chain = s("head"), s("carried"), s("chain")
                got, stored = sems(f"h{k}_got"), sems(f"h{k}_st")
                flat_ = "a p f -> (a p) f"
                if k < 3:
                    nodes = NodeTiles(c2, f"n{k}", (k - 1) * ET)
                else:
                    ins = tmp("ins", [P, RING, 3, F])
                    jring = tmp("jring", [P, RING], I32)
                    z_in, j_ready = sems("h3_zin"), s("j")
                    xT = tmp("xT", [P, RING, 8, P])
                    kring = tmp("kring", [P, RING], I32)
                    ln = TileNorm(c2, "o_ln")
                    pT = [c2.enter_context(nc.psum_tensor(f"h3_pT{b}", [P, 4, P], F32)) for b in range(2)]
                    pz = [c2.enter_context(nc.psum_tensor(f"h3_pz{b}", [P, F], F32)) for b in range(2)]
                    ta_done, tb_done, xa_ready, xb_ready, mm_done, k_ready = s("Ta"), s("Tb"), s("xa"), s("xb"), s("mm"), s("k")
                    in3 = sems("h3_in")
                    hops = [x.rearrange("(u p) f -> u p f", p=P) for x in (hop1, hop2)]
                with nc.Block() as block:
                    @block.gpsimd
                    def _(pool):
                        top = pool.to_reg(rows - 1)
                        out_top = pool.to_reg(NPAD - 1)
                        pool.wait_ge(init, 1)

                        def scatter(u, r):
                            pool.wait_ge(ln.ready, u + 1)
                            pool.wait_ge(k_ready, u + 1)
                            pool.sem_inc(begun, 1)
                            pool.indirect_dma_start(d["out"], bass.IndirectOffsetOnAxis(ap=kring[:, r:r + 1], axis=0), ln.o[:, r, :], None,
                                                    bounds_check=out_top, oob_is_err=False).then_inc(stored[r], 16)

                        def step(i, at):
                            for r in range(RING):
                                u = 4 * i + r
                                if at != 0:
                                    pool.wait_ge(ps_ready, u - 3)
                                pool.wait_ge(idx_ready, u + 1)
                                pool.sem_inc(begun, 1)
                                pool.indirect_dma_start(xs[:, r, :], None, table_of, bass.IndirectOffsetOnAxis(ap=iring[:, r:r + 1], axis=0),
                                                        bounds_check=top, oob_is_err=False).then_inc(got[r], 16)
                                if k == 3:
                                    if at != 0:
                                        pool.wait_ge(ln.add_done, u - 3)
                                    pool.wait_ge(j_ready, u + 1)
                                    pool.sem_inc(begun, 1)
                                    pool.indirect_dma_start(ins[:, r, 0, :], None, zrow, bass.IndirectOffsetOnAxis(ap=jring[:, r:r + 1], axis=0),
                                                            bounds_check=out_top, oob_is_err=False).then_inc(z_in[r], 16)
                                if k == 3 and not (at == 0 or (at == 1 and r < 3)):
                                    scatter(u - 7, (r - 7) % 4)
                        loop(pool, step, 2 if k == 3 else 1)
                        if k == 3:
                            for u in range(ET - 7, ET):
                                scatter(u, u % 4)
                            for r in range(RING):
                                pool.wait_ge(stored[r], 16 * EI)

                    @block.sync
                    def _(sp):
                        if k < 3:
                            def step(i, at):
                                for r in range(RING):
                                    u = 4 * i + r
                                    nodes.load(sp, u, r, at)
                                    if not (at == 0 and r < 3):
                                        v = u - 3
                                        sp.wait_ge(h_ready, v + 1)
                                        sp.dma_start(dest[bass.ds(v, 1), :, :].rearrange(flat_), h[:, (r - 3) % 4, :]).then_inc(stored[(r - 3) % 4], 16)
                                    if at != 0 and not (at == 1 and r < 3):
                                        nodes.store(sp, u - 7, (r - 7) % 4)
                            loop(sp, step, 2)
                            for u in range(ET - 3, ET):
                                sp.wait_ge(h_ready, u + 1)
                                sp.dma_start(dest[u], h[:, u % 4, :]).then_inc(stored[u % 4], 16)
                            for u in range(ET - 7, ET):
                                nodes.store(sp, u, u % 4)
                            for r in range(RING):
                                sp.wait_ge(stored[r], 16 * EI)
                            nodes.all_stored(sp)
                        else:
                            def step(i, at):
                                for r in range(RING):
                                    u = 4 * i + r
                                    if at != 0:
                                        sp.wait_ge(tb_done, u - 3)
                                    for x in range(2):
                                        sp.dma_start(ins[:, r, 1 + x, :], hops[x][bass.ds(u, 1), :, :].rearrange(flat_)).then_inc(in3[r], 16)
                            loop(sp, step)

                    @block.scalar
                    def _(act):
                        def head(u, r, i):
                            act.wait_ge(got[r], 16 * i + 16)
                            nc.scalar.activation(xs[0:1, r, :], xs[0:1, r, :], ACT.Copy, scale=weight[0:1, bass.ds(u, 1)]).then_inc(head_ready, 1)

                        act.wait_ge(init, 1)
                        head(0, 0, 0)

                        def evacuate(u, r, i):
                            act.wait_ge(ps_ready, u + 1)
                            if i is not None:
                                if k == 3:
                                    act.wait_ge(tb_done, u - 3)
                                else:
                                    act.wait_ge(stored[r], 16 * i)
                            nc.scalar.activation(h[:, r, :], ps[r][:], ACT.Copy).then_inc(h_ready, 1)

                        def turned(u, r, waits):
                            act.wait_ge(tb_done, u + 1)
                            if waits:
                                act.wait_ge(mm_done, u - 3)
                            nc.scalar.activation(xT[:, r, 4:8, :], pT[1][:], ACT.Copy).then_inc(xb_ready, 1)

                        def norm(u, r, waits):
                            if waits is not None:
                                act.wait_ge(stored[r], waits)
                            ln.normed(act, u, r)

                        def step(i, at):
                            for r in range(RING):
                                u = 4 * i + r
                                if not (at == EI - 1 and r == 3):
                                    head(u + 1, (r + 1) % 4, i + (1 if r == 3 else 0))
                                if not (at == 0 and r == 0):
                                    act.wait_ge(carried, u)
                                    evacuate(u - 1, (r - 1) % 4, None if at == 0 or (at == 1 and r == 0) else i - (1 if r == 0 else 0))
                                if k < 3:
                                    nodes.turned(act, u, r, at)
                                    if not (at == 0 and r < 3):
                                        nodes.ln.deviation(act, u - 3, (r - 3) % 4)
                                    if at != 0:
                                        nodes.norm(act, u - 4, r, 16 * (i - 1) if at != 1 else None)
                                if k == 3:
                                    if not (at == 0 and r < 3):
                                        ln.deviation(act, u - 3, (r - 3) % 4)
                                    if at != 0:
                                        norm(u - 4, r, 16 * (i - 1) if at != 1 else None)
                                    if not (at == 0 and r == 0):
                                        turned(u - 1, (r - 1) % 4, not (at == 0 or (at == 1 and r == 0)))
                        loop(act, step, 2)
                        evacuate(ET - 1, 3, EI - 1)
                        if k < 3:
                            for u in range(ET - 3, ET):
                                nodes.ln.deviation(act, u, u % 4)
                            for u in range(ET - 4, ET):
                                nodes.norm(act, u, u % 4, 16 * (EI - 1))
                        if k == 3:
                            turned(ET - 1, 3, True)
                            for u in range(ET - 3, ET):
                                ln.deviation(act, u, u % 4)
                            for u in range(ET - 4, ET):
                                norm(u, u % 4, 16 * (EI - 1))

                    @block.tensor
                    def _(pe):
                        pe.wait_ge(init, 1)

                        def product(u, r, waits):
                            pe.wait_ge(xa_ready, u + 1)
                            pe.wait_ge(xb_ready, u + 1)
                            if waits:
                                pe.wait_ge(ln.add_done, u - 1)
                            for c in range(8):
                                last = pe.matmul(pz[r % 2][:], xT[:, r, c, :], kept_w[c // 2][:, c % 2, :], start=(c == 0), stop=(c == 7))
                            last.then_inc(mm_done, 1)

                        def turn_hop(u, r, waits):
                            if waits:
                                pe.wait_ge(xb_ready, u)
                            for c in range(2):
                                pe.transpose(pT[1][:, c, :], ins[:, r, 2, P * c:P * c + P], ident[:])
                            pe.wait_ge(h_ready, u + 1)
                            for c in range(2):
                                last = pe.transpose(pT[1][:, 2 + c, :], h[:, r, P * c:P * c + P], ident[:])
                            last.then_inc(tb_done, 1)

                        def step(i, at):
                            for r in range(RING):
                                u = 4 * i + r
                                pe.wait_ge(mw_ready, u + 1)
                                if at != 0:
                                    pe.wait_ge(h_ready, u - 3)
                                if at == 0 and r == 0:
                                    pe.wait_ge(head_ready, 1)
                                else:
                                    pe.wait_ge(carried, u)
                                pe.matmul(ps[r][:], mw[:, r, :], xs[:, r, :], start=True, stop=True).then_inc(ps_ready, 1)
                                if k < 3:
                                    nodes.turn(pe, u, r, i, at)
                                    if not (at == 0 and r == 0):
                                        nodes.product(pe, u - 1, (r - 1) % 4, not (at == 0 and r < 3))
                                if k == 3:
                                    pe.wait_ge(in3[r], 32 * i + 32)
                                    pe.wait_ge(z_in[r], 16 * i + 16)
                                    if not (at == 0 and r == 0):
                                        pe.wait_ge(xa_ready, u)
                                    for c in range(4):
                                        last = pe.transpose(pT[0][:, c, :], ins[:, r, c // 2, P * (c % 2):P * (c % 2) + P], ident[:])
                                    last.then_inc(ta_done, 1)
                                    if not (at == 0 and r < 2):
                                        product(u - 2, (r - 2) % 4, at != 0)
                                    if not (at == 0 and r == 0):
                                        turn_hop(u - 1, (r - 1) % 4, not (at == 0 and r == 1))
                        loop(pe, step)
                        if k < 3:
                            nodes.product(pe, ET - 1, 3, True)
                        if k == 3:
                            product(ET - 2, 2, True)
                            turn_hop(ET - 1, 3, True)
                            product(ET - 1, 3, True)

                    @block.vector
                    def _(dve):
                        v = nc.vector
                        v.memset(xs[:], 0.0).then_inc(init, 1)
                        carrying_weights(v, linker(dve, chain), wcol, weight[:])

                        def prepare(u, r, first):
                            if not first:
                                dve.wait_ge(ps_ready, u - 3)
                            v.tensor_scalar(mw[:, r, :], same[:, bass.ds(u, 1), :].rearrange("p a j -> p (a j)"), wcol[:, bass.ds(u, 1)], None, ALU.mult).then_inc(mw_ready, 1)

                        def carry(u, r):
                            dve.wait_ge(head_ready, u + 1)
                            dve.wait_ge(ps_ready, u)
                            v.scalar_tensor_tensor(xs[0:1, r, :], ps[(r - 1) % 4][0:1, :], cflag[:, bass.ds(u - 1, 1)], xs[0:1, r, :],
                                                   ALU.mult, ALU.add).then_inc(carried, 1)

                        def sums(u, r, waits, stored_at):
                            dve.wait_ge(mm_done, u + 1)
                            ln.moments(dve, u, r, pz[r % 2][:], ins[:, r, 0, :], waits)
                            if stored_at is not None:
                                dve.wait_ge(stored[r], stored_at)
                            copy(kring[:, r:r + 1], sidx[:, bass.ds(u, 1)]).then_inc(k_ready, 1)

                        for r in range(RING):
                            copy(iring[:, r:r + 1], idx[:, r:r + 1]).then_inc(idx_ready, 1)
                            if k == 3:
                                copy(jring[:, r:r + 1], dstJ[:, r:r + 1]).then_inc(j_ready, 1)
                        for r in range(2):
                            prepare(r, r, True)

                        def step(i, at):
                            for r in range(RING):
                                u = 4 * i + r
                                if not (at == 0 and r == 0):
                                    carry(u, r)
                                if not (at == EI - 1 and r >= 2):
                                    prepare(u + 2, (r + 2) % 4, at == 0 and r < 2)
                                dve.wait_ge(got[r], 16 * i + 16)
                                copy(iring[:, r:r + 1], idx[:, bass.ds(u + RING, 1)]).then_inc(idx_ready, 1)
                                if k < 3:
                                    if not (at == 0 and r < 2):
                                        nodes.sums(dve, u - 2, (r - 2) % 4, not (at == 0 or (at == 1 and r < 2)))
                                    if at != 0:
                                        nodes.ln.scales(dve, u - 4, r)
                                if k == 3:
                                    dve.wait_ge(z_in[r], 16 * i + 16)
                                    copy(jring[:, r:r + 1], dstJ[:, bass.ds(u + RING, 1)]).then_inc(j_ready, 1)
                                    if not (at == 0 and r < 3):
                                        sums(u - 3, (r - 3) % 4, not (at == 0 or (at == 1 and r < 3)),
                                             None if at == 0 or (at == 1 and r < 3) else (16 * (i - 1) if r < 3 else 16 * i))
                                    if at != 0:
                                        ln.scales(dve, u - 4, r)
                                    dve.wait_ge(ta_done, u + 1)
                                    if at != 0:
                                        dve.wait_ge(mm_done, u - 3)
                                    v.tensor_copy(xT[:, r, 0:4, :], pT[0][:]).then_inc(xa_ready, 1)
                        loop(dve, step, 2)
                        if k < 3:
                            for u in (ET - 2, ET - 1):
                                nodes.sums(dve, u, u % 4, True)
                            for u in range(ET - 4, ET):
                                nodes.ln.scales(dve, u, u % 4)
                        if k == 3:
                            for r in (1, 2, 3):
                                sums(ET - 4 + r, r, True, 16 * (EI - 1))
                            for u in range(ET - 4, ET):
                                ln.scales(dve, u, u % 4)

        load_block()
        end_of_block()
        out_of_order = nc.values_load(unsorted[0:1, 0:1], min_val=0, max_val=NSLOT)
        with nc.If(out_of_order > 0):
            sort_block("ds", d["dstK"], d["dstrow"], d["srcK"], d["wK"])
            end_of_block()
        structure_block("dt", table, True)
        end_of_block()
        node_gram_block()
        end_of_block()
        for k in (1, 2, 3):
            a_pass(k, gk[k - 1])
            end_of_block()
        norm_block()
        end_of_block()
        dense_block("z", d["x"], [hmap[0][:], hmap[1][:]], True, zrow)
        end_of_block()
        slots_block()
        end_of_block()
        sort_block("ss", d["skey"], d["skeyrow"], d["sother"], d["wK"])
        end_of_block()
        structure_block("st", table2, False)
        end_of_block()
        for k in (1, 2, 3):
            hop_pass(k)
            end_of_block()


def kernel(x, src, dst, edge_weight, L0_gnn_W1, L0_gnn_b1, L0_gnn_g1, L0_gnn_be1, L0_gnn_W2, L0_gnn_b2, L0_gnn_g2, L0_gnn_be2,
           L0_gnn_W3, L0_gnn_b3, L0_gnn_g3, L0_gnn_be3, L1_gnn_weight):
    import concourse.bacc as bacc
    from concourse.bass_utils import run_bass_kernel_spmd

    def padded(a, n, fill):
        return np.concatenate([a, np.full((n - a.shape[0],) + a.shape[1:], fill, a.dtype)])

    def tiles(a):
        return np.ascontiguousarray(a.reshape(ET, P)[::-1])

    x, src, dst, edge_weight = (np.asarray(a) for a in (x, src, dst, edge_weight))
    s, t, w = padded(src, NSLOT, 0), padded(dst, NSLOT, N), padded(edge_weight, NSLOT, 0)
    skey, sother = padded(src, NSLOT, N), padded(dst, NSLOT, 0)
    before = np.concatenate([np.full((1,), -1, t.dtype), t[:-1]])
    table0 = np.zeros((NPAD, 2), np.float32)
    table0[:, 0] = np.where(np.arange(NPAD) < N, np.arange(NPAD), 2 * NPAD)
    table0[:, 1] = 1.0

    def rows(a):
        return np.ascontiguousarray(tiles(a)[:, ::-1])

    def columns(a):
        return np.ascontiguousarray(rows(a).T)

    k, m = np.arange(P)[:, None], np.arange(P)[None, :]
    arrays = {
        "x": padded(x, NPAD, 0),
        "srcK": columns(s), "dstK": columns(t), "wK": columns(w), "dstrow": rows(t),
        "skey": columns(skey), "skeyrow": rows(skey), "sother": columns(sother),
        "dstJ": np.ascontiguousarray(tiles(t).T), "dprev": np.ascontiguousarray(tiles(before).T),
        "iota": np.ascontiguousarray(np.broadcast_to(np.arange(NPAD // P, dtype=np.float32), (P, NPAD // P))),
        "tri": (m < k).astype(np.float32), "triu": (k < m).astype(np.float32), "rev": (k + m == P - 1).astype(np.float32),
        "slots": np.ascontiguousarray((NPAD + np.arange(NSLOT, dtype=np.float32)).reshape(ET, P).T),
        "table0": table0, "ident": np.eye(P, dtype=np.float32), "ones": np.ones((P, P), np.float32),
        "e3": np.array([[0, 0, 0, 1]], np.float32), "e3c": np.array([[0], [0], [0], [1]], np.float32),
        "L1W": np.ascontiguousarray(np.asarray(L1_gnn_weight).transpose(2, 0, 1)),
    }
    for k, (W, b, g, be) in enumerate(((L0_gnn_W1, L0_gnn_b1, L0_gnn_g1, L0_gnn_be1), (L0_gnn_W2, L0_gnn_b2, L0_gnn_g2, L0_gnn_be2),
                                       (L0_gnn_W3, L0_gnn_b3, L0_gnn_g3, L0_gnn_be3)), 1):
        arrays[f"W{k}"] = np.asarray(W)
        for n, a in (("b", b), ("g", g), ("be", be)):
            arrays[f"{n}{k}"] = np.asarray(a)[None]
    nc = bacc.Bacc("TRN2", target_bir_lowering=False, num_devices=1)
    d = {n: nc.dram_tensor(f"in_{n}", a.shape, mybir.dt.from_np(a.dtype), kind="ExternalInput").ap() for n, a in arrays.items()}
    d["out"] = nc.dram_tensor("out_rows", (NPAD, F), F32, kind="ExternalOutput").ap()
    build_program(nc, d)
    r = run_bass_kernel_spmd(nc, [{f"in_{n}": a for n, a in arrays.items()}], core_ids=[0])
    return r.results[0]["out_rows"][:N]
```

```python
from contextlib import ExitStack

import numpy as np

import concourse.bass as bass
from concourse import mybir

ALU = mybir.AluOpType
ACT = mybir.ActivationFunctionType
AX = mybir.AxisListType
F32 = mybir.dt.float32
BF16 = mybir.dt.bfloat16
I32 = mybir.dt.int32

P = 128
N = 50000
E = 25000
F = 256
XW = F + 4
RING = 4
ET = 196
NSLOT = ET * P
EI = ET // RING
GROUPS = 98
NPAD = GROUPS * 4 * P
GI = GROUPS // 2
FAR = 1000000.0
EPS = 1e-5
NT = GROUPS * 4


def build_program(nc, d):
    with ExitStack() as ctx:
        def sb(name, shape, dt=F32):
            return ctx.enter_context(nc.sbuf_tensor(name, shape, dt))

        in_use = []

        def sem(name):
            in_use.append(nc.alloc_semaphore(name=name))
            return in_use[-1]

        def end_of_block():
            nc.clear_and_free_semaphores(in_use)
            in_use.clear()
            nc.all_engine_barrier()

        def sems(name, n=RING):
            return [sem(f"{name}{k}") for k in range(n)]

        def copy(out, a):
            return nc.vector.tensor_scalar(out, a, 1.0, None, ALU.mult)

        def dram(name, shape, dt=F32):
            return nc.dram_tensor(name, shape, dt, kind="Internal").ap()
        table = dram("node_table", (NPAD, 2))
        hist = dram("l0_rows", (NPAD + 2 * NSLOT, XW))
        cube = dram("l0_cube", (NSLOT, XW))
        zrow = dram("z_rows", (NPAD, F))
        xown = dram("own_rows", (NSLOT, F))
        hop1 = dram("hop1", (NSLOT, F))
        hop2 = dram("hop2", (NSLOT, F))

        srows = dram("sorted_rows", (NSLOT, 4))
        flat = dram("key_rows", (ET, P))
        table2 = dram("hop_table", (NPAD, 2))

        ident = sb("ident", [P, P])
        identb = sb("identb", [P, P], BF16)
        onesf = sb("onesf", [P, P])
        same = sb("same", [P, ET, P], BF16)
        keyJ = sb("keyJ", [P, ET])
        keyK = sb("keyK", [P, ET])
        other = sb("other", [P, ET + RING], I32)
        dstJ = sb("dstJ", [P, ET + RING], I32)
        wK = sb("wK", [P, ET])
        w23 = sb("w23", [P, ET])
        edge = sb("edge", [P, ET, 2])
        idx2 = sb("idx2", [P, ET + RING], I32)
        idx3 = sb("idx3", [P, ET + RING], I32)
        idxh = sb("idxh", [P, ET + RING], I32)
        sidx = sb("sidx", [P, ET + RING], I32)
        rep = sb("rep", [P, ET])
        dinvrep = sb("dinvrep", [P, ET])
        dinv2rep = sb("dinv2rep", [P, ET])
        cflag = sb("cflag", [1, ET])
        side = sb("side", [P, ET, 3])
        nonU = sb("nonU", [P, NT])
        gram = sb("gram", [P, 3, XW])
        hidx = sb("hidx", [P, ET + RING], I32)
        tabv = sb("tabv", [P, ET, 2])
        rec = sb("rec", [P, ET, 4])
        place = sb("place", [P, ET], I32)
        iring = sb("iring", [P, RING], I32)
        unsorted = sb("unsorted", [1, 1], I32)

        def loop(eng, step, peel=1):
            for i in range(peel):
                step(i, i)
            with eng.Fori(peel, EI - 1) as i:
                step(i, None)
            step(EI - 1, EI - 1)

        def linker(dve, chain):
            n = [0]

            def link(ins):
                n[0] += 1
                ins.then_inc(chain, 1)
                dve.wait_ge(chain, n[0])
            return link

        class Scatter:
            def __init__(self, c2, name, dest, rows, values, width, index):
                self.vals = c2.enter_context(nc.sbuf_tensor(f"{name}_vals", [P, RING, width], F32))
                self.ring = c2.enter_context(nc.sbuf_tensor(f"{name}_ring", [P, RING], I32))
                self.dest, self.rows, self.values, self.index = dest, rows, values, index
                self.put_ready, self.begun, self.put = sem(f"{name}_ready"), sem(f"{name}_begun"), sems(f"{name}_put")

            def dve(self, u, r, i, at):
                if at != 0:
                    nc.vector.wait_ge(self.put[r], 16 * i)
                copy(self.vals[:, r, :], self.values[:, bass.ds(u, 1), :].rearrange("p a c -> p (a c)")).then_inc(self.put_ready, 1)
                copy(self.ring[:, r:r + 1], self.index[:, bass.ds(u, 1)]).then_inc(self.put_ready, 1)

            def begin(self, pool):
                self.top = pool.to_reg(self.rows - 1)

            def pool(self, pool, u, r, at):
                pool.wait_ge(self.put_ready, 2 * u + 2)
                pool.sem_inc(self.begun, 1)
                pool.indirect_dma_start(self.dest, bass.IndirectOffsetOnAxis(ap=self.ring[:, r:r + 1], axis=0), self.vals[:, r, :], None,
                                        bounds_check=self.top, oob_is_err=False).then_inc(self.put[r], 16)

            def end(self, pool):
                for r in range(RING):
                    pool.wait_ge(self.put[r], 16 * EI)

        class LookUp:
            def __init__(self, c2, name, table_):
                self.vals = c2.enter_context(nc.sbuf_tensor(f"{name}_vals", [P, RING, 2], F32))
                self.ring = c2.enter_context(nc.sbuf_tensor(f"{name}_ring", [P, RING], I32))
                self.table = table_
                self.look_idx, self.looked, self.begun, self.look = sem(f"{name}_idx"), sem(f"{name}_looked"), sem(f"{name}_begun"), sems(f"{name}_in")

            def dve_begin(self):
                for r in range(RING):
                    copy(self.ring[:, r:r + 1], other[:, r:r + 1]).then_inc(self.look_idx, 1)

            def dve(self, u, r, i):
                nc.vector.wait_ge(self.look[r], 16 * i + 16)
                copy(edge[:, bass.ds(u, 1), :].rearrange("p a c -> p (a c)"), self.vals[:, r, :]).then_inc(self.looked, 1)
                copy(self.ring[:, r:r + 1], other[:, bass.ds(u + RING, 1)]).then_inc(self.look_idx, 1)

            def dve_end(self, dve):
                dve.wait_ge(self.looked, ET)
                dve.wait_ge(self.look_idx, ET + RING)

            def begin(self, pool):
                self.top = pool.to_reg(NPAD - 1)

            def pool(self, pool, u, r, at):
                if at != 0:
                    pool.wait_ge(self.looked, u - 3)
                pool.wait_ge(self.look_idx, u + 1)
                pool.sem_inc(self.begun, 1)
                pool.indirect_dma_start(self.vals[:, r, :], None, self.table, bass.IndirectOffsetOnAxis(ap=self.ring[:, r:r + 1], axis=0),
                                        bounds_check=self.top, oob_is_err=False).then_inc(self.look[r], 16)

        def run_beside(pool, guest):
            guest.begin(pool)

            def step(i, at):
                for r in range(RING):
                    guest.pool(pool, 4 * i + r, r, at)
            loop(pool, step)

        def edge_scatter(c2, name):
            return Scatter(c2, name, srows, NSLOT, rec, 4, place)

        def scatter_block():
            with ExitStack() as c2:
                guest = edge_scatter(c2, "es")
                with nc.Block() as block:
                    @block.vector
                    def _(dve):
                        def step(i, at):
                            for r in range(RING):
                                guest.dve(4 * i + r, r, i, at)
                        loop(dve, step)

                    @block.gpsimd
                    def _(pool):
                        run_beside(pool, guest)
                        guest.end(pool)

        def load_block():
            with ExitStack() as c2:
                def tmp(name, shape, dt=F32):
                    return c2.enter_context(nc.sbuf_tensor(f"l_{name}", shape, dt))
                dK, dJ, dP = tmp("dK", [P, ET], I32), tmp("dJ", [P, ET], I32), tmp("dP", [P, ET], I32)
                dPf, t0, t1 = tmp("dPf", [P, ET]), tmp("t0", [P, ET]), tmp("t1", [P, 1])
                pf = c2.enter_context(nc.psum_tensor("l_pf", [1, 1], F32))
                loaded, chain, bad, summed = sem("l_loaded"), sem("l_chain"), sem("l_bad"), sem("l_sum")
                with nc.Block() as block:
                    @block.sync
                    def _(sp):
                        for t, name in ((ident, "ident"), (onesf, "ones"), (dK, "dstK"), (dJ, "dstJ"), (dP, "dprev")):
                            sp.dma_start(t[:], d[name]).then_inc(loaded, 16)
                        sp.dma_start(other[:, 0:ET], d["srcK"]).then_inc(loaded, 16)

                    @block.vector
                    def _(dve):
                        v = nc.vector
                        link = linker(dve, chain)
                        for t in (other, dstJ, idx2, idx3, idxh, sidx, hidx):
                            link(v.memset(t[:, ET:ET + RING], 0))
                        dve.wait_ge(loaded, 16 * 6)
                        link(v.tensor_copy(identb[:], ident[:]))
                        link(v.tensor_copy(keyK[:], dK[:]))
                        link(v.tensor_copy(keyJ[:], dJ[:]))
                        link(v.tensor_copy(dPf[:], dP[:]))
                        link(v.tensor_tensor(rep[:], keyJ[:], dPf[:], ALU.not_equal))
                        link(v.tensor_tensor(t0[:], dPf[:], keyJ[:], ALU.is_gt))
                        v.tensor_reduce(t1[:], t0[:], AX.X, ALU.add).then_inc(bad, 1)
                        dve.wait_ge(summed, 1)
                        link(v.tensor_copy(unsorted[:], pf[:]))

                    @block.tensor
                    def _(pe):
                        pe.wait_ge(bad, 1)
                        pe.matmul(pf[:], t1[:], onesf[:, 0:1], start=True, stop=True).then_inc(summed, 1)

        def rank_block(name, keys, key_rows, others, weights, guest_of):
            LO = NPAD // P
            with ExitStack() as c2:
                def tmp(x, shape, dt=F32):
                    return c2.enter_context(nc.sbuf_tensor(f"{name}_{x}", shape, dt))
                key, oth, wt = tmp("key", [P, ET], I32), tmp("oth", [P, ET], I32), tmp("wt", [P, ET])
                hi, lo, ti = tmp("hi", [P, ET]), tmp("lo", [P, ET]), tmp("ti", [P, ET], I32)
                keyf, rank, pos = tmp("keyf", [P, ET]), tmp("rank", [P, ET]), tmp("pos", [P, ET])
                tf = tmp("tf", [P, ET])
                iota, tri = tmp("iota", [P, LO]), tmp("tri", [P, P])
                triu = tmp("triu", [P, P])
                rowb = tmp("rowb", [P, RING, P], I32)
                ohl, ohh = tmp("ohl", [P, RING, LO], BF16), tmp("ohh", [P, RING, P], BF16)
                ohT = tmp("ohT", [P, 2, P])
                state = tmp("state", [P, 2, LO])
                base, incl, zrow_ = tmp("base", [P, LO]), tmp("incl", [P, LO]), tmp("zrow", [P, LO])
                junk, junk2 = tmp("junk", [P, RING, LO], BF16), tmp("junk2", [P, RING, P], BF16)
                guest = guest_of(c2) if guest_of else None
                ph = c2.enter_context(nc.psum_tensor(f"{name}_ph", [P, LO], F32))
                pl = [c2.enter_context(nc.psum_tensor(f"{name}_pl{x}", [P, LO], F32)) for x in range(2)]
                pt = [c2.enter_context(nc.psum_tensor(f"{name}_pt{x}", [P, P], BF16)) for x in range(2)]
                po = c2.enter_context(nc.psum_tensor(f"{name}_po", [P, 1], F32))
                s = lambda x: sem(f"{name}_{x}")
                loaded, chain = s("loaded"), s("chain")
                hot1, counted, based, offset = s("hot1"), s("counted"), s("based"), s("offset")
                hot2, turned, turnedc, looked, kept, updated, chosen, inrank = [s(x) for x in ("hot2", "turn", "turnc", "look", "kept", "upd", "chosen", "inrank")]
                row_in = sems(f"{name}_row")
                with nc.Block() as block:
                    @block.sync
                    def _(sp):
                        for t, a in ((key, keys), (oth, others), (wt, weights), (iota, d["iota"]), (tri, d["tri"]), (triu, d["triu"])):
                            sp.dma_start(t[:], a).then_inc(loaded, 16)

                        def step(i, first):
                            for r in range(RING):
                                if not first:
                                    sp.wait_ge(inrank, 4 * i + r - 3)
                                sp.dma_start(rowb[:, r, :], key_rows[bass.ds(i * RING + r, 1), :].to_broadcast((P, P))).then_inc(row_in[r], 16)
                        step(0, True)
                        with sp.Fori(1, EI) as i:
                            step(i, False)

                    @block.tensor
                    def _(pe):
                        pe.wait_ge(based, 1)
                        pe.matmul(ph[:], zrow_[:, 0:P], zrow_[:], start=True, stop=False)
                        with pe.Fori(0, EI) as i:
                            for r in range(RING):
                                pe.wait_ge(hot1, 8 * i + 2 * r + 2)
                                pe.matmul(ph[:], ohh[:, r, :], ohl[:, r, :], start=False, stop=False).then_inc(counted, 1)
                        pe.matmul(ph[:], zrow_[:, 0:P], zrow_[:], start=False, stop=True).then_inc(counted, 1)
                        pe.wait_ge(based, 2)
                        pe.matmul(po[:], triu[:], incl[:, LO - 1:LO], start=True, stop=True).then_inc(offset, 1)
                        pe.wait_ge(based, 3)
                        pe.matmul(ph[:], ident[:], base[:], start=True, stop=True).then_inc(updated, 1)

                        def step(i, first):
                            for r in range(RING):
                                u = 4 * i + r
                                pe.wait_ge(hot2, 2 * (u + 1))
                                if not (first and r < 2):
                                    pe.wait_ge(turnedc, u - 1)
                                pe.transpose(pt[r % 2][:], ohh[:, r, :], identb[:]).then_inc(turned, 1)
                                pe.wait_ge(turnedc, u + 1)
                                pe.wait_ge(kept, u + 1)
                                if not (first and r < 2):
                                    pe.wait_ge(chosen, u - 1)
                                pe.matmul(ph[:], ohh[:, r, :], ohl[:, r, :], start=False, stop=True, skip_group_check=True).then_inc(updated, 1)
                                pe.matmul(pl[r % 2][:], ohT[:, r % 2, :], state[:, r % 2, :], start=True, stop=True).then_inc(looked, 1)
                        step(0, True)
                        with pe.Fori(1, EI) as i:
                            step(i, False)

                    @block.scalar
                    def _(act):
                        def step(i, first):
                            for r in range(RING):
                                u = 4 * i + r
                                act.wait_ge(updated, u + 1)
                                if not (first and r < 2):
                                    act.wait_ge(looked, u - 1)
                                nc.scalar.activation(state[:, r % 2, :], ph[:], ACT.Copy).then_inc(kept, 1)
                                act.wait_ge(turned, u + 1)
                                nc.scalar.activation(ohT[:, r % 2, :], pt[r % 2][:], ACT.Copy).then_inc(turnedc, 1)
                        step(0, True)
                        with act.Fori(1, EI) as i:
                            step(i, False)

                    @block.vector
                    def _(dve):
                        v = nc.vector
                        link = linker(dve, chain)
                        link(v.memset(zrow_[:], 0.0))
                        dve.wait_ge(loaded, 16 * 6)
                        link(v.tensor_copy(keyf[:], key[:]))
                        link(v.tensor_scalar(ti[:], key[:], 127, None, ALU.bitwise_and))
                        link(v.tensor_copy(hi[:], ti[:]))
                        link(v.tensor_scalar(ti[:], key[:], 7, None, ALU.arith_shift_right))
                        link(v.tensor_copy(lo[:], ti[:]))
                        dve.sem_inc(based, 1)

                        def hot(u, r, ready):
                            v.tensor_scalar(ohl[:, r, :], iota[:], lo[:, bass.ds(u, 1)], None, ALU.is_equal).then_inc(ready, 1)
                            v.tensor_scalar(ohh[:, r, :], iota[:, 0:P], hi[:, bass.ds(u, 1)], None, ALU.is_equal).then_inc(ready, 1)

                        def count(i, first):
                            for r in range(RING):
                                if not first:
                                    dve.wait_ge(counted, 4 * i + r - 3)
                                hot(4 * i + r, r, hot1)
                        count(0, True)
                        with dve.Fori(1, EI) as i:
                            count(i, False)
                        dve.wait_ge(counted, ET + 1)
                        link(v.tensor_copy(base[:], ph[:]))
                        link(v.tensor_tensor_scan(incl[:], zrow_[:], base[:], 0.0, ALU.add, ALU.add))
                        dve.sem_inc(based, 1)
                        link(v.tensor_tensor(base[:], incl[:], base[:], ALU.subtract))
                        dve.wait_ge(offset, 1)
                        link(v.tensor_scalar(base[:], base[:], po[:, 0:1], None, ALU.add))
                        dve.sem_inc(based, 1)

                        def select(u, r):
                            dve.wait_ge(looked, u + 1)
                            v.scalar_tensor_tensor(junk[:, r, :], pl[r % 2][:], 1.0, ohl[:, r, :], ALU.mult, ALU.mult, accum_out=pos[:, bass.ds(u, 1)]).then_inc(chosen, 1)

                        def step(i, at):
                            for r in range(RING):
                                u = 4 * i + r
                                if at != 0:
                                    dve.wait_ge(chosen, u - 3)
                                    dve.wait_ge(looked, u - 3)
                                    dve.wait_ge(inrank, u - 3)
                                hot(u, r, hot2)
                                dve.wait_ge(row_in[r], 16 * i + 16)
                                v.scalar_tensor_tensor(junk2[:, r, :], rowb[:, r, :], keyf[:, bass.ds(u, 1)], tri[:], ALU.is_equal, ALU.mult, accum_out=rank[:, bass.ds(u, 1)]).then_inc(inrank, 1)
                                if not (at == 0 and r == 0):
                                    select(u - 1, (r - 1) % 4)
                                if guest:
                                    guest.dve(u, r, i, at)
                        loop(dve, step)
                        select(ET - 1, 3)
                        dve.wait_ge(inrank, ET)
                        dve.wait_ge(chosen, ET)
                        link(v.tensor_tensor(pos[:], pos[:], rank[:], ALU.add))
                        link(v.tensor_copy(ti[:], pos[:]))
                        link(v.tensor_scalar(ti[:], ti[:], 127, None, ALU.bitwise_and))
                        link(v.tensor_copy(rank[:], ti[:]))
                        link(v.tensor_tensor(tf[:], pos[:], rank[:], ALU.subtract))
                        link(v.tensor_scalar(tf[:], tf[:], -1.0 / P, ET - 1.0, ALU.mult, ALU.add))
                        link(v.scalar_tensor_tensor(pos[:], rank[:], float(ET), tf[:], ALU.mult, ALU.add))
                        link(v.tensor_copy(place[:], pos[:]))
                        link(v.tensor_copy(rec[:, :, 0], keyf[:]))
                        link(v.tensor_copy(rec[:, :, 1], oth[:]))
                        link(v.tensor_copy(rec[:, :, 2], wt[:]))
                        link(v.memset(rec[:, :, 3], 0.0))

                    @block.gpsimd
                    def _(pool):
                        if guest:
                            run_beside(pool, guest)
                            guest.end(pool)

        def sorted_block(name):
            LO = ET * 2
            with ExitStack() as c2:
                def tmp(x, shape, dt=F32):
                    return c2.enter_context(nc.sbuf_tensor(f"{name}_{x}", shape, dt))
                sj, tf, rev = tmp("sj", [P, ET, 4]), tmp("tf", [P, ET]), tmp("rev", [P, P])
                pr = [c2.enter_context(nc.psum_tensor(f"{name}_pr{x}", [P, LO], F32)) for x in range(2)]
                loaded, chain, back, reved, kdone, placed = [sem(f"{name}_{x}") for x in ("loaded", "chain", "back", "rev", "kdone", "placed")]
                with nc.Block() as block:
                    @block.sync
                    def _(sp):
                        sp.dma_start(rev[:], d["rev"]).then_inc(loaded, 16)
                        sp.dma_start(sj[:].rearrange("p u c -> p (u c)"), srows.rearrange("(p u) c -> p (u c)", p=P)).then_inc(back, 16)
                        sp.wait_ge(placed, 2)
                        sp.dma_start(tf[1:P, :], keyJ[0:P - 1, :]).then_inc(kdone, 16)
                        sp.dma_start(tf[0:1, 0:ET - 1], keyJ[P - 1:P, 1:ET]).then_inc(kdone, 16)

                    @block.tensor
                    def _(pe):
                        pe.wait_ge(loaded, 16)
                        pe.wait_ge(back, 16)
                        sjf = sj[:].rearrange("p u c -> p (u c)")
                        for x in range(2):
                            last = pe.matmul(pr[x][:], rev[:], sjf[:, LO * x:LO * x + LO], start=True, stop=True)
                        last.then_inc(reved, 1)

                    @block.vector
                    def _(dve):
                        v = nc.vector
                        link = linker(dve, chain)
                        v.memset(tf[:], -1.0).then_inc(placed, 1)
                        dve.wait_ge(back, 16)
                        v.tensor_copy(keyJ[:], sj[:, :, 0]).then_inc(placed, 1)
                        dve.wait_ge(reved, 1)
                        H = ET // 2
                        for x in range(2):
                            g = pr[x][:].rearrange("p (u c) -> p u c", c=4)
                            link(v.tensor_copy(keyK[:, H * x:H * x + H], g[:, :, 0]))
                            link(v.tensor_copy(other[:, H * x:H * x + H], g[:, :, 1]))
                            link(v.tensor_copy(wK[:, H * x:H * x + H], g[:, :, 2]))
                        dve.wait_ge(placed, 2)
                        dve.wait_ge(kdone, 32)
                        link(v.tensor_tensor(rep[:], keyJ[:], tf[:], ALU.not_equal))

        def structure_block(name, out_table, with_degree, sidx):
            with ExitStack() as c2:
                def tmp(x, shape, dt=F32):
                    return c2.enter_context(nc.sbuf_tensor(f"{name}_{x}", shape, dt))
                C = 7
                CI = ET // (2 * C)
                rowb = tmp("rowb", [P, 2, C, P])
                onesb = tmp("onesb", [P, 1], BF16)
                turned = tmp("turned", [ET // 2, 2, P])
                cnt, cont, t0 = tmp("cnt", [P, ET]), tmp("cont", [P, ET]), tmp("t0", [P, ET])
                srow, crow = tmp("srow", [1, ET]), tmp("crow", [1, ET])
                slots = tmp("slots", [P, ET])
                ptr = c2.enter_context(nc.psum_tensor(f"{name}_ptr", [ET // 2, 2, P], F32))
                pcnt = c2.enter_context(nc.psum_tensor(f"{name}_pcnt", [P, 512], F32))
                pbc = c2.enter_context(nc.psum_tensor(f"{name}_pbc", [P, 2, 256], F32))
                s = lambda x: sem(f"{name}_{x}")
                loaded, tinit, chain, flat_out = s("loaded"), s("tinit"), s("chain"), s("flat")
                turn, turnc, row_free, cnt_done, rows_ready, bc_done = [s(x) for x in ("turn", "turnc", "built", "cnt", "rows", "bc")]
                sq_in, sq_out = s("sqin"), s("sqout")
                row_in = sems(f"{name}_row", 2)
                chunks = flat.rearrange("(c u) p -> c (u p)", u=C)
                H = ET // 2
                with nc.Block() as block:
                    @block.sync
                    def _(sp):
                        sp.dma_start(slots[:], d["slots"]).then_inc(loaded, 16)
                        sp.wait_ge(turnc, 1)
                        sp.dma_start(flat.rearrange("(x u) p -> u x p", x=2), turned[:]).then_inc(flat_out, 16)
                        sp.wait_ge(flat_out, 16)

                        def step(i, first):
                            for b in range(2):
                                if not first:
                                    sp.wait_ge(row_free, 2 * i + b - 1)
                                sp.dma_start(rowb[:, b].rearrange("p u j -> p (u j)"), chunks[bass.ds(2 * i + b, 1), :].to_broadcast((P, C * P))).then_inc(row_in[b], 16)
                        step(0, True)
                        with sp.Fori(1, CI) as i:
                            step(i, False)

                    @block.tensor
                    def _(pe):
                        for x in range(2):
                            last = pe.transpose(ptr[:, x, :], keyJ[:, H * x:H * x + H], ident[:])
                        last.then_inc(turn, 1)
                        if with_degree:
                            with pe.Fori(0, CI) as i:
                                for b in range(2):
                                    pe.wait_ge(row_free, 2 * i + b + 1)
                                    for c in range(C):
                                        u = 2 * C * i + C * b + c
                                        pe.matmul(pcnt[:, bass.ds(u, 1)], same[:, bass.ds(u, 1), :].rearrange("p a j -> p (a j)"),
                                                  onesb[:], start=True, stop=True).then_inc(cnt_done, 1)
                            pe.wait_ge(rows_ready, 1)
                            pe.matmul(pbc[:, 0, 0:ET], onesf[0:1, :], crow[:], start=True, stop=True).then_inc(bc_done, 1)
                            pe.matmul(pbc[:, 1, 0:ET], onesf[0:1, :], keyJ[0:1, :], start=True, stop=True).then_inc(bc_done, 1)

                    @block.scalar
                    def _(act):
                        if with_degree:
                            act.wait_ge(sq_in, 1)
                            nc.scalar.activation(t0[:], cnt[:], ACT.Sqrt).then_inc(sq_out, 1)

                    @block.vector
                    def _(dve):
                        v = nc.vector
                        link = linker(dve, chain)
                        link(v.memset(onesb[:], 1.0))
                        dve.wait_ge(turn, 1)
                        v.tensor_copy(turned[:], ptr[:]).then_inc(turnc, 1)
                        link(v.tensor_scalar(t0[:], keyJ[:], float(N), None, ALU.is_lt))
                        link(v.tensor_tensor(rep[:], rep[:], t0[:], ALU.mult))
                        link(v.tensor_scalar(t0[:], rep[:], -FAR, FAR, ALU.mult, ALU.add))
                        link(v.tensor_tensor(t0[:], t0[:], keyJ[:], ALU.add))
                        link(v.tensor_copy(sidx[:, 0:ET], t0[:]))
                        link(v.tensor_copy(dstJ[:, 0:ET], keyJ[:]))
                        link(v.memset(cflag[:], 0.0))
                        link(v.tensor_tensor(cflag[:, 0:ET - 1], keyK[0:1, 1:ET], keyJ[0:1, 0:ET - 1], ALU.is_equal))
                        dve.wait_ge(loaded, 16)
                        link(v.tensor_copy(tabv[:, :, 0], slots[:]))
                        with dve.Fori(0, CI) as i:
                            for b in range(2):
                                dve.wait_ge(row_in[b], 16 * i + 16)
                                u = 2 * C * i + C * b
                                v.tensor_tensor(same[:, bass.ds(u, C), :], rowb[:, b], keyK[:, bass.ds(u, C), None].to_broadcast((P, C, P)),
                                                ALU.is_equal).then_inc(row_free, 1)
                        if with_degree:
                            link(v.tensor_copy(side[:], rep[:, :, None].to_broadcast((P, ET, 3))))
                            link(v.memset(srow[:], 0.0))
                            link(v.tensor_tensor(srow[:, 1:ET], keyJ[0:1, 1:ET], keyJ[0:1, 0:ET - 1], ALU.is_equal))
                            dve.wait_ge(cnt_done, ET)
                            link(v.tensor_copy(cnt[:], pcnt[:, 0:ET]))
                            link(v.tensor_tensor_scan(crow[:], srow[:], cnt[0:1, :], 0.0, ALU.mult, ALU.add))
                            dve.sem_inc(rows_ready, 1)
                            dve.wait_ge(bc_done, 2)
                            link(v.tensor_tensor(cont[:, 1:ET], keyJ[:, 1:ET], pbc[:, 1, 0:ET - 1], ALU.is_equal))
                            link(v.tensor_tensor(cont[:, 1:ET], cont[:, 1:ET], pbc[:, 0, 0:ET - 1], ALU.mult))
                            link(v.tensor_tensor(cnt[:, 1:ET], cnt[:, 1:ET], cont[:, 1:ET], ALU.add))
                            link(v.tensor_scalar(cnt[:], cnt[:], 1.0, None, ALU.add))
                            dve.sem_inc(sq_in, 1)
                            dve.wait_ge(sq_out, 1)
                            link(v.reciprocal(tabv[:, :, 1], t0[:]))
                            link(v.tensor_tensor(dinvrep[:], tabv[:, :, 1], rep[:], ALU.mult))
                            link(v.tensor_tensor(dinv2rep[:], tabv[:, :, 1], dinvrep[:], ALU.mult))
                        else:
                            link(v.memset(tabv[:, :, 1], 0.0))

                    @block.gpsimd
                    def _(pool):
                        pool.dma_start(out_table, d["table0"]).then_inc(tinit, 16)
                        pool.wait_ge(tinit, 16)

        def table_scatter(name, out_table, sidx):
            return lambda c2: Scatter(c2, name, out_table, NPAD, tabv, 2, sidx)

        def node_gram_block():
            with ExitStack() as c2:
                xin = c2.enter_context(nc.sbuf_tensor("g_xin", [P, 2, 4, F], F32))
                xm = c2.enter_context(nc.sbuf_tensor("g_xm", [P, 2, 4, XW], F32))
                zero = c2.enter_context(nc.sbuf_tensor("g_zero", [P, XW], F32))
                pg = [c2.enter_context(nc.psum_tensor(f"g_p{k}", [P, XW], F32)) for k in range(3)]
                x_in = sems("g_in", 2)
                masked = sem("g_masked")
                sided = sem("g_side")
                used = sem("g_used")
                stored = sems("g_st", 2)
                zr = sem("g_zr")
                out = sem("g_out")
                guest = LookUp(c2, "lk", table)
                tfull = c2.enter_context(nc.sbuf_tensor("g_tfull", [P, NT, 2], F32))
                t0, t1 = [c2.enter_context(nc.sbuf_tensor(f"g_t{x}", [P, ET], F32)) for x in range(2)]
                tfl, known, chain = sem("g_tfl"), sem("g_known"), sem("g_chain")
                xg = d["x"].rearrange("(s p q) f -> s p (q f)", p=P, q=4)
                hg = hist[0:NPAD, :].rearrange("(s p q) f -> s p (q f)", p=P, q=4)
                with nc.Block() as block:
                    @block.sync
                    def _(sp):
                        sp.dma_start(tfull[:].rearrange("p (s q) c -> p s (q c)", q=4),
                                     table.rearrange("(s p q) c -> p s (q c)", p=P, q=4)).then_inc(tfl, 16)

                        def step(i, at):
                            for b in range(2):
                                g = 2 * i + b
                                if at != 0:
                                    sp.wait_ge(masked, 4 * (g - 1))
                                sp.dma_start(xin[:, b].rearrange("p q f -> p (q f)"), xg[bass.ds(g, 1), :, :].rearrange("a p f -> (a p) f")).then_inc(x_in[b], 16)
                                if not (at == 0 and b == 0):
                                    store(g - 1, 1 - b)

                        def store(g, b):
                            sp.wait_ge(masked, 4 * (g + 1))
                            sp.wait_ge(sided, g + 1)
                            sp.dma_start(hg[bass.ds(g, 1), :, :].rearrange("a p f -> (a p) f"), xm[:, b].rearrange("p q f -> p (q f)")).then_inc(stored[b], 16)
                        loop(sp, step)
                        store(GROUPS - 1, 1)
                        for b in range(2):
                            sp.wait_ge(stored[b], 16 * GI)

                    @block.gpsimd
                    def _(pool):
                        run_beside(pool, guest)

                    @block.scalar
                    def _(act):
                        act.wait_ge(known, 1)

                        def step(i, first):
                            for b in range(2):
                                act.wait_ge(x_in[b], 16 * i + 16)
                                if not first:
                                    act.wait_ge(used, 2 * i + b - 1)
                                    act.wait_ge(stored[b], 16 * i)
                                for q in range(4):
                                    nc.scalar.activation(xm[:, b, q, 0:F], xin[:, b, q, :], ACT.Copy, scale=nonU[:, bass.ds((2 * i + b) * 4 + q, 1)]).then_inc(masked, 1)
                        step(0, True)
                        with act.Fori(1, GI) as i:
                            step(i, False)

                    @block.vector
                    def _(dve):
                        nc.vector.memset(zero[:], 0.0).then_inc(zr, 1)
                        guest.dve_begin()
                        dve.wait_ge(tfl, 16)
                        nc.vector.tensor_scalar(nonU[:], tfull[:, :, 0], float(NPAD), None, ALU.is_lt).then_inc(known, 1)
                        dve.wait_ge(known, 1)

                        def step(i, first):
                            for b in range(2):
                                if not first:
                                    dve.wait_ge(used, 2 * i + b - 1)
                                    dve.wait_ge(stored[b], 16 * i)
                                copy(xm[:, b, :, F:XW], nonU[:, bass.ds((2 * i + b) * 4, 4), None].to_broadcast((P, 4, 4))).then_inc(sided, 1)
                                for r in (2 * b, 2 * b + 1):
                                    guest.dve(4 * i + r, r, i)
                        step(0, True)
                        with dve.Fori(1, GI) as i:
                            step(i, False)
                        guest.dve_end(dve)
                        v = nc.vector
                        link = linker(dve, chain)
                        link(v.tensor_scalar(t0[:], edge[:, :, 0], float(NPAD), None, ALU.is_ge))
                        link(v.tensor_copy(idx2[:, 0:ET], edge[:, :, 0]))
                        link(v.tensor_scalar(t1[:], t0[:], float(NSLOT), None, ALU.mult))
                        link(v.tensor_tensor(t1[:], t1[:], edge[:, :, 0], ALU.add))
                        link(v.tensor_copy(idx3[:, 0:ET], t1[:]))
                        dve.wait_ge(used, GROUPS + 1)
                        for k in range(3):
                            nc.vector.tensor_copy(gram[0:P if k < 2 else 4, k, 128 * k:XW], pg[k][0:P if k < 2 else 4, 128 * k:XW]).then_inc(out, 1)

                    @block.tensor
                    def _(pe):
                        pe.wait_ge(zr, 1)
                        open_gram(pe, pg, zero)
                        with pe.Fori(0, GI) as i:
                            for b in range(2):
                                pe.wait_ge(masked, 4 * (2 * i + b + 1))
                                pe.wait_ge(sided, 2 * i + b + 1)
                                for q in range(4):
                                    last = add_gram(pe, pg, xm[:, b, q, :])
                                last.then_inc(used, 1)
                        close_gram(pe, pg, zero).then_inc(used, 1)

        def open_gram(pe, pg, zero):
            for k in range(3):
                m = P if k < 2 else 4
                pe.matmul(pg[k][0:m, 128 * k:XW], zero[:, 0:m], zero[:, 128 * k:XW], start=True, stop=False)

        def add_gram(pe, pg, y):
            for k in range(3):
                m = P if k < 2 else 4
                last = pe.matmul(pg[k][0:m, 128 * k:XW], y[:, 128 * k:128 * k + m], y[:, 128 * k:XW], start=False, stop=False)
            return last

        def close_gram(pe, pg, zero):
            for k in range(3):
                m = P if k < 2 else 4
                last = pe.matmul(pg[k][0:m, 128 * k:XW], zero[:, 0:m], zero[:, 128 * k:XW], start=False, stop=True)
            return last

        def carrying_weights(v, link, wcol, weight):
            link(v.tensor_copy(wcol[:], weight))
            link(v.memset(wcol[0:1, :], 1.0))

        def a_pass(k, gout):
            table_of = d["x"] if k == 1 else hist[0:NPAD + (k - 1) * NSLOT, :]
            width = F if k == 1 else XW
            idx = {1: other, 2: idx2, 3: idx3}[k]
            rows = NPAD + (k - 1) * NSLOT
            prev = None if k == 1 else hist[NPAD + (k - 2) * NSLOT:NPAD + (k - 1) * NSLOT, :].rearrange("(u p) f -> u p f", p=P)
            dest = (hist[NPAD + (k - 1) * NSLOT:NPAD + k * NSLOT, :] if k < 3 else cube).rearrange("(u p) f -> u p f", p=P)
            own = xown.rearrange("(u p) f -> u p f", p=P)
            W1 = F + 1
            heads = 2 if k == 1 else 1
            with ExitStack() as c2:
                def tmp(name, shape, dt=F32):
                    return c2.enter_context(nc.sbuf_tensor(f"a{k}_{name}", shape, dt))
                xs = tmp("xs", [P, RING, XW])
                xd = tmp("xd", [P, RING, XW])
                mw = tmp("mw", [P, RING, P])
                yt = tmp("yt", [P, RING, W1])
                y = tmp("y", [P, RING, XW])
                jring = tmp("jring", [P, RING], I32)
                zero = tmp("zero", [P, XW])
                wcol = tmp("wcol", [P, ET])
                ps = [c2.enter_context(nc.psum_tensor(f"a{k}_ps{b}", [P, 512], F32)) for b in range(RING)]
                pg = [c2.enter_context(nc.psum_tensor(f"a{k}_pg{b}", [P, XW], F32)) for b in range(3)]
                s = lambda x: sem(f"a{k}_{x}")
                begun = s("begun")
                chain = s("chain")
                init, idx_ready, mw_ready, head_ready, carried, ps_ready = s("init"), s("idx"), s("mw"), s("head"), s("carried"), s("ps")
                yt_ready, y_ready, gram_done, out = s("yt"), s("y"), s("gram"), s("out")
                got, self_in, stored = sems(f"a{k}_got"), sems(f"a{k}_self"), sems(f"a{k}_st")
                kept = sems(f"a{k}_kept")
                rows_of = "a p f -> (a p) f"
                with nc.Block() as block:
                    @block.gpsimd
                    def _(pool):
                        top = pool.to_reg(rows - 1)
                        pool.wait_ge(init, 3)

                        def step(i, at):
                            for r in range(RING):
                                u = 4 * i + r
                                if at != 0:
                                    pool.wait_ge(ps_ready, u - 3)
                                pool.wait_ge(idx_ready, (2 if k == 1 else 1) * (u + 1))
                                pool.sem_inc(begun, 1)
                                pool.indirect_dma_start(xs[:, r, 0:width], None, table_of, bass.IndirectOffsetOnAxis(ap=iring[:, r:r + 1], axis=0),
                                                        bounds_check=top, oob_is_err=False).then_inc(got[r], 16)
                                if k == 1:
                                    if at != 0:
                                        pool.wait_ge(y_ready, 2 * (u - 3))
                                        pool.wait_ge(kept[r], 16 * i)
                                    pool.sem_inc(begun, 1)
                                    pool.indirect_dma_start(xd[:, r, 0:F], None, table_of, bass.IndirectOffsetOnAxis(ap=jring[:, r:r + 1], axis=0),
                                                            bounds_check=top, oob_is_err=False).then_inc(self_in[r], 16)
                        loop(pool, step)

                    @block.sync
                    def _(sp):
                        sp.wait_ge(init, 3)

                        def step(i, at):
                            for r in range(RING):
                                u = 4 * i + r
                                if k > 1:
                                    if at != 0:
                                        sp.wait_ge(y_ready, 2 * (u - 3))
                                    sp.dma_start(xd[:, r, :], prev[bass.ds(u, 1), :, :].rearrange(rows_of)).then_inc(self_in[r], 16)
                                else:
                                    sp.wait_ge(self_in[r], 16 * i + 16)
                                    sp.dma_start(own[bass.ds(u, 1), :, :].rearrange(rows_of), xd[:, r, 0:F]).then_inc(kept[r], 16)
                        loop(sp, step)
                        if k == 1:
                            for r in range(RING):
                                sp.wait_ge(kept[r], 16 * EI)

                    @block.scalar
                    def _(act):
                        def head(u, r, i):
                            act.wait_ge(got[r], 16 * i + 16)
                            nc.scalar.activation(xs[0:1, r, 0:width], xs[0:1, r, 0:width], ACT.Copy, scale=edge[0:1, bass.ds(u, 1), 1]).then_inc(head_ready, 1)
                            if k == 1:
                                nc.scalar.activation(xs[0:1, r, F:W1], edge[0:1, bass.ds(u, 1), 1], ACT.Copy).then_inc(head_ready, 1)

                        def scaled(u, r, waits):
                            act.wait_ge(ps_ready, u + 1)
                            if waits:
                                act.wait_ge(y_ready, 2 * (u - 3))
                            nc.scalar.activation(yt[:, r, :], ps[r][:, 0:W1], ACT.Copy, scale=dinvrep[:, bass.ds(u, 1)]).then_inc(yt_ready, 1)

                        def store(u, r):
                            act.wait_ge(y_ready, 2 * (u + 1))
                            act.dma_start(dest[bass.ds(u, 1), :, :].rearrange(rows_of), y[:, r, :]).then_inc(stored[r], 16)

                        act.wait_ge(init, 3)
                        head(0, 0, 0)

                        def step(i, at):
                            for r in range(RING):
                                u = 4 * i + r
                                if not (at == EI - 1 and r == 3):
                                    head(u + 1, (r + 1) % 4, i + (1 if r == 3 else 0))
                                if not (at == 0 and r == 0):
                                    act.wait_ge(carried, u)
                                    scaled(u - 1, (r - 1) % 4, not (at == 0 or (at == 1 and r == 0)))
                                if not (at == 0 and r < 3):
                                    store(u - 3, (r - 3) % 4)
                        loop(act, step, 2)
                        scaled(ET - 1, 3, True)
                        for u in range(ET - 3, ET):
                            store(u, u % 4)
                        for r in range(RING):
                            act.wait_ge(stored[r], 16 * EI)

                    @block.vector
                    def _(dve):
                        v = nc.vector
                        v.memset(zero[:], 0.0).then_inc(init, 1)
                        v.memset(xs[:], 1.0).then_inc(init, 1)
                        v.memset(xd[:], 1.0).then_inc(init, 1)
                        carrying_weights(v, linker(dve, chain), wcol, edge[:, :, 1])

                        def idx_copy(u, r):
                            copy(iring[:, r:r + 1], idx[:, bass.ds(u, 1)]).then_inc(idx_ready, 1)
                            if k == 1:
                                copy(jring[:, r:r + 1], dstJ[:, bass.ds(u, 1)]).then_inc(idx_ready, 1)

                        def prepare(u, r, waits):
                            if waits:
                                dve.wait_ge(ps_ready, u - 3)
                            v.tensor_scalar(mw[:, r, :], same[:, bass.ds(u, 1), :].rearrange("p a j -> p (a j)"), wcol[:, bass.ds(u, 1)], None, ALU.mult).then_inc(mw_ready, 1)

                        def carry(u, r):
                            dve.wait_ge(head_ready, heads * (u + 1))
                            dve.wait_ge(ps_ready, u)
                            v.scalar_tensor_tensor(xs[0:1, r, 0:W1], ps[(r - 1) % 4][0:1, 0:W1], cflag[:, bass.ds(u - 1, 1)], xs[0:1, r, 0:W1],
                                                   ALU.mult, ALU.add).then_inc(carried, 1)

                        def finish(u, r, waits, i):
                            dve.wait_ge(self_in[r], 16 * i + 16)
                            dve.wait_ge(yt_ready, u + 1)
                            if waits:
                                dve.wait_ge(gram_done, u - 3)
                                dve.wait_ge(stored[r], 16 * i)
                            v.scalar_tensor_tensor(y[:, r, 0:W1], xd[:, r, 0:W1], dinv2rep[:, bass.ds(u, 1)], yt[:, r, :], ALU.mult, ALU.add).then_inc(y_ready, 1)
                            copy(y[:, r, W1:XW], side[:, bass.ds(u, 1), :].rearrange("p a c -> p (a c)")).then_inc(y_ready, 1)

                        def keep_side(u, r):
                            if k < 3:
                                dve.wait_ge(y_ready, 2 * (u + 1))
                                copy(side[:, bass.ds(u, 1), 2 - k], y[:, r, F:W1]).then_inc(out, 1)

                        for r in range(RING):
                            idx_copy(r, r)
                        for r in range(2):
                            prepare(r, r, False)

                        def step(i, at):
                            for r in range(RING):
                                u = 4 * i + r
                                if not (at == 0 and r == 0):
                                    carry(u, r)
                                if not (at == EI - 1 and r >= 2):
                                    prepare(u + 2, (r + 2) % 4, not (at == 0 and r < 2))
                                if not (at == 0 and r < 3):
                                    keep_side(u - 3, (r - 3) % 4)
                                if not (at == 0 and r < 2):
                                    finish(u - 2, (r - 2) % 4, not (at == 0 or (at == 1 and r < 2)), i - (1 if r < 2 else 0))
                                dve.wait_ge(got[r], 16 * i + 16)
                                if k == 1:
                                    dve.wait_ge(self_in[r], 16 * i + 16)
                                idx_copy(u + RING, r)
                        loop(dve, step, 2)
                        keep_side(ET - 3, 1)
                        for r in (2, 3):
                            finish(ET - 4 + r, r, True, EI - 1)
                            keep_side(ET - 4 + r, r)
                        dve.wait_ge(gram_done, ET + 1)
                        for b in range(3):
                            m = P if b < 2 else 4
                            v.tensor_tensor(gout[0:m, b, 128 * b:XW], gram[0:m, b, 128 * b:XW], pg[b][0:m, 128 * b:XW], ALU.add).then_inc(out, 1)

                    @block.tensor
                    def _(pe):
                        pe.wait_ge(init, 3)
                        open_gram(pe, pg, zero)

                        def step(i, at):
                            for r in range(RING):
                                u = 4 * i + r
                                pe.wait_ge(mw_ready, u + 1)
                                if at != 0:
                                    pe.wait_ge(yt_ready, u - 3)
                                if at == 0 and r == 0:
                                    pe.wait_ge(head_ready, heads)
                                else:
                                    pe.wait_ge(carried, u)
                                pe.matmul(ps[r][:, 0:W1], mw[:, r, :], xs[:, r, 0:W1], start=True, stop=True).then_inc(ps_ready, 1)
                                if not (at == 0 and r < 3):
                                    pe.wait_ge(y_ready, 2 * (u - 2))
                                    add_gram(pe, pg, y[:, (r - 3) % 4, :]).then_inc(gram_done, 1)
                        loop(pe, step)
                        for u in range(ET - 3, ET):
                            pe.wait_ge(y_ready, 2 * (u + 1))
                            add_gram(pe, pg, y[:, u % 4, :]).then_inc(gram_done, 1)
                        close_gram(pe, pg, zero).then_inc(gram_done, 1)

        hc = sb("hc", [4, F])
        hmap = [sb(f"hmap{c}", [P, F]) for c in range(2)]
        gk = [sb(f"gram{k}", [P, 3, XW]) for k in (1, 2, 3)]

        kept_w = [sb(f"l1w{k}", [P, 2, F]) for k in range(4)]
        hsplit = sb("hsplit", [68, F], BF16)
        oneb = sb("oneb", [68, P], BF16)
        epsc = sb("epsc", [P, 1])

        def norm_block():
            with ExitStack() as c2:
                def tmp(name, shape, dt=F32):
                    return c2.enter_context(nc.sbuf_tensor(f"n_{name}", shape, dt))
                gb = tmp("gb", [P, 3, 2, F])
                wl = tmp("wl", [P, 3, 2, F])
                b1 = tmp("b1", [4, F])
                brow = tmp("brow", [1, 3, F])
                e3 = tmp("e3", [1, 4])
                e3c = tmp("e3c", [4, 1])
                w = [tmp(f"w{c}", [P if c < 2 else 4, F]) for c in range(3)]
                cov = [tmp(f"cov{c}", [P if c < 2 else 4, XW]) for c in range(3)]
                mbc = tmp("mbc", [P, 3, P])
                mrow = tmp("mrow", [1, XW])
                prod = [tmp(f"prod{c}", [P if c < 2 else 4, F]) for c in range(3)]
                mean = tmp("mean", [P, F])
                var = tmp("var", [P, F])
                sd = tmp("sd", [P, F])
                sc = tmp("sc", [P, F])
                shift = tmp("shift", [P, F])
                hT = tmp("hT", [P, 2, XW])
                hTc = tmp("hTc", [P, 2, 4])
                t4 = tmp("t4", [4, F])
                pa, pb, pc, pd = [c2.enter_context(nc.psum_tensor(f"n_p{x}", [P, 512], F32)) for x in "abcd"]
                ld, dv, pt, sq = sem("n_loaded"), sem("n_dve"), sem("n_pe"), sem("n_sqrt")
                chain = sem("n_chain")
                halves = "(c p) f -> p c f"
                hs = (P, P, 4)
                with nc.Block() as block:
                    @block.sync
                    def _(sp):
                        for k in range(3):
                            sp.dma_start(gb[:, k, 0, :], d[f"g{k + 1}"].to_broadcast((P, F))).then_inc(ld, 16)
                            sp.dma_start(gb[:, k, 1, :], d[f"be{k + 1}"].to_broadcast((P, F))).then_inc(ld, 16)
                            sp.dma_start(wl[:, k, :, :], d[f"W{k + 1}"].rearrange(halves, p=P)).then_inc(ld, 16)
                            sp.dma_start(brow[:, k, :], d[f"b{k + 1}"]).then_inc(ld, 16)
                        sp.dma_start(b1[:], d["b1"].to_broadcast((4, F))).then_inc(ld, 16)
                        sp.dma_start(e3[:], d["e3"]).then_inc(ld, 16)
                        sp.dma_start(e3c[:], d["e3c"]).then_inc(ld, 16)
                        for k in range(4):
                            sp.dma_start(kept_w[k][:], d["L1W"][k].rearrange(halves, p=P)).then_inc(ld, 16)

                    @block.scalar
                    def _(act):
                        for k in range(3):
                            act.wait_ge(dv, 7 * k + 5)
                            nc.scalar.activation(sd[:], var[:], ACT.Sqrt).then_inc(sq, 1)

                    @block.tensor
                    def _(pe):
                        pe.wait_ge(ld, 16 * 19)
                        for k in range(3):
                            g = gk[k]
                            pe.wait_ge(dv, 7 * k + 1)
                            pe.transpose(pa[:, 0:P], g[:, 0, P:2 * P], ident[:])
                            pe.transpose(pa[0:4, P:2 * P], g[:, 0, 2 * P:XW], ident[:])
                            pe.transpose(pa[0:4, 2 * P:3 * P], g[:, 1, 2 * P:XW], ident[:])
                            pe.transpose(pb[0:1, 0:P], g[:, 0, XW - 1:XW], ident[:])
                            pe.transpose(pb[0:1, P:2 * P], g[:, 1, XW - 1:XW], ident[:])
                            pe.transpose(pb[0:1, 2 * P:XW], g[0:4, 2, XW - 1:XW], ident[0:4, 0:4]).then_inc(pt, 1)
                            pe.wait_ge(dv, 7 * k + 2)
                            for c, p in enumerate((pa, pb, pc)):
                                last = pe.matmul(p[0:hs[c], 0:XW], mrow[:, P * c:P * c + hs[c]], mrow[:], start=True, stop=True)
                            last.then_inc(pt, 1)
                            pe.wait_ge(dv, 7 * k + 3)
                            for m, p in enumerate((pa, pb, pc, pd)):
                                for c in range(3):
                                    lhsT = cov[c][:, P * m:P * m + hs[m]] if m < 3 else mbc[0:hs[c], c, :]
                                    last = pe.matmul(p[0:hs[m] if m < 3 else P, 0:F], lhsT, w[c][:], start=(c == 0), stop=(c == 2))
                            last.then_inc(pt, 1)
                            pe.wait_ge(dv, 7 * k + 4)
                            for c in range(3):
                                last = pe.matmul(pa[:, 0:F], onesf[0:hs[c], :], prod[c][:], start=(c == 0), stop=(c == 2))
                            last.then_inc(pt, 1)
                            if k < 2:
                                pe.wait_ge(dv, 7 * k + 6)
                                for c, p in enumerate((pa, pb)):
                                    for m in range(3):
                                        last = pe.transpose(p[:, P * m:P * m + hs[m]], w[m][:, P * c:P * c + P], ident[0:hs[m], 0:hs[m]])
                                last.then_inc(pt, 1)
                                pe.wait_ge(dv, 7 * k + 7)
                                for m, p in enumerate((pa, pb, pc)):
                                    for c in range(2):
                                        lhsT = hT[:, c, P * m:P * m + P] if m < 2 else hTc[:, c, :]
                                        last = pe.matmul(p[0:hs[m], 0:F], lhsT, wl[:, k + 1, c, :], start=(c == 0), stop=(c == 1 and m < 2))
                                last = pe.matmul(pc[0:4, 0:F], e3[:], brow[:, k + 1, :], start=False, stop=True)
                                last.then_inc(pt, 1)

                    @block.vector
                    def _(dve):
                        v = nc.vector
                        n = [0]

                        def link(ins):
                            n[0] += 1
                            ins.then_inc(chain, 1)
                            dve.wait_ge(chain, n[0])
                        dve.wait_ge(ld, 16 * 19)
                        for c in range(2):
                            link(v.tensor_copy(w[c][:], wl[:, 0, c, :]))
                        link(v.tensor_scalar(w[2][:], b1[:], e3c[:], None, ALU.mult))
                        for k in range(3):
                            g = gk[k]
                            dve.sem_inc(dv, 1)
                            dve.wait_ge(pt, 6 * k + 1)
                            link(v.tensor_scalar(cov[0][:], g[:, 0, :], 1.0 / N, None, ALU.mult))
                            link(v.tensor_scalar(cov[1][:, 0:P], pa[:, 0:P], 1.0 / N, None, ALU.mult))
                            link(v.tensor_scalar(cov[1][:, P:XW], g[:, 1, P:XW], 1.0 / N, None, ALU.mult))
                            link(v.tensor_scalar(cov[2][:, 0:2 * P], pa[0:4, P:3 * P], 1.0 / N, None, ALU.mult))
                            link(v.tensor_scalar(cov[2][:, 2 * P:XW], g[0:4, 2, 2 * P:XW], 1.0 / N, None, ALU.mult))
                            link(v.tensor_scalar(mrow[:], pb[0:1, 0:XW], 1.0 / N, None, ALU.mult))
                            for c in range(3):
                                link(v.tensor_copy(mbc[0:hs[c], c, :], cov[c][:, XW - 1:XW].to_broadcast((hs[c], P))))
                            dve.sem_inc(dv, 1)
                            dve.wait_ge(pt, 6 * k + 2)
                            for c, p in enumerate((pa, pb, pc)):
                                link(v.tensor_tensor(cov[c][:], cov[c][:], p[0:hs[c], 0:XW], ALU.subtract))
                            dve.sem_inc(dv, 1)
                            dve.wait_ge(pt, 6 * k + 3)
                            for c, p in enumerate((pa, pb, pc)):
                                link(v.tensor_tensor(prod[c][:], w[c][:], p[0:hs[c], 0:F], ALU.mult))
                            link(v.tensor_copy(mean[:], pd[:, 0:F]))
                            dve.sem_inc(dv, 1)
                            dve.wait_ge(pt, 6 * k + 4)
                            link(v.tensor_scalar(var[:], pa[:, 0:F], 0.0, EPS, ALU.max, ALU.add))
                            dve.sem_inc(dv, 1)
                            dve.wait_ge(sq, k + 1)
                            link(v.reciprocal(sc[:], sd[:]))
                            link(v.tensor_tensor(sc[:], sc[:], gb[:, k, 0, :], ALU.mult))
                            link(v.tensor_tensor(shift[:], mean[:], sc[:], ALU.mult))
                            link(v.tensor_tensor(shift[:], gb[:, k, 1, :], shift[:], ALU.subtract))
                            for c in range(3):
                                link(v.tensor_tensor(w[c][:], w[c][:], sc[0:hs[c], :], ALU.mult))
                            link(v.scalar_tensor_tensor(w[2][:], shift[0:4, :], e3c[:], w[2][:], ALU.mult, ALU.add))
                            dve.sem_inc(dv, 1)
                            if k < 2:
                                dve.wait_ge(pt, 6 * k + 5)
                                link(v.memset(hTc[:], 0.0))
                                for c, p in enumerate((pa, pb)):
                                    link(v.tensor_copy(hT[:, c, :], p[:, 0:XW]))
                                    link(v.tensor_copy(hTc[:, c, 0:3], p[:, F + 1:XW]))
                                dve.sem_inc(dv, 1)
                                dve.wait_ge(pt, 6 * k + 6)
                                for c, p in enumerate((pa, pb, pc)):
                                    link(v.tensor_copy(w[c][:], p[0:hs[c], 0:F]))
                            else:
                                for c in range(2):
                                    link(v.tensor_copy(hmap[c][:], w[c][:]))
                                link(v.tensor_copy(hc[:], w[2][:]))
                                link(v.memset(hsplit[:], 0.0))
                                link(v.memset(oneb[:], 1.0))
                                link(v.memset(epsc[:], EPS))
                                for part in range(3):
                                    link(v.tensor_copy(hsplit[32 * part:32 * part + 4, :], w[2][:]))
                                    if part < 2:
                                        link(v.tensor_copy(t4[:], hsplit[32 * part:32 * part + 4, :]))
                                        link(v.tensor_tensor(w[2][:], w[2][:], t4[:], ALU.subtract))

        def dense_block(name, rows, w, constant, dest):
            B = 4
            with ExitStack() as c2:
                def tmp(x, shape, dt=F32):
                    return c2.enter_context(nc.sbuf_tensor(f"{name}_{x}", shape, dt))
                guest = edge_scatter(c2, "zs")
                xin, t, o = [tmp(x, [P, 2, 4, F]) for x in ("xin", "t", "o")]
                xT = tmp("xT", [P, B, 2, P])
                st, mv, pad = tmp("st", [P, 4, 6]), tmp("mv", [P, 4, 2]), tmp("pad", [P, 1])
                sd, rs, nm = tmp("sd", [P, 4]), tmp("rs", [P, 2, 4]), tmp("nm", [P, 2, 4])
                pT = [c2.enter_context(nc.psum_tensor(f"{name}_pT{x}", [P, 2, P], F32)) for x in range(B)]
                pz = [c2.enter_context(nc.psum_tensor(f"{name}_pz{x}", [P, F], F32)) for x in range(B)]
                s = lambda x: sem(f"{name}_{x}")
                t_done, xt_ready, mm_done, add_done, st_done, mv_done, sd_done, r_done, rs_done, ready = [
                    s(x) for x in ("T", "xT", "mm", "add", "stats", "mv", "sd", "r", "rs", "ready")]
                x_in, stored = sems(f"{name}_in", 2), sems(f"{name}_st", 2)
                xg = rows.rearrange("(s p q) f -> s p (q f)", p=P, q=4)
                og = dest.rearrange("(s p q) f -> s p (q f)", p=P, q=4)
                rows_of = "a p f -> (a p) f"
                free = "p q f -> p (q f)"

                def ends(eng, step):
                    step(0, True, False)
                    with eng.Fori(1, GI - 1) as i:
                        step(i, False, False)
                    step(GI - 1, False, True)

                with nc.Block() as block:
                    @block.sync
                    def _(sp):
                        def load(g, b):
                            sp.dma_start(xin[:, b].rearrange(free), xg[bass.ds(g, 1), :, :].rearrange(rows_of)).then_inc(x_in[b], 16)

                        def store(g, b):
                            sp.wait_ge(ready, 4 * (g + 1))
                            sp.dma_start(og[bass.ds(g, 1), :, :].rearrange(rows_of), o[:, b].rearrange(free)).then_inc(stored[b], 16)
                        load(0, 0)
                        load(1, 1)

                        def step(i, first, last):
                            for b in range(2):
                                g = 2 * i + b
                                if not first:
                                    store(g - 2, b)
                                if not last:
                                    sp.wait_ge(add_done, 4 * (g + 1))
                                    load(g + 2, b)
                        ends(sp, step)
                        store(GROUPS - 2, 0)
                        store(GROUPS - 1, 1)
                        for b in range(2):
                            sp.wait_ge(stored[b], 16 * GI)

                    @block.gpsimd
                    def _(pool):
                        run_beside(pool, guest)
                        guest.end(pool)

                    @block.tensor
                    def _(pe):
                        def product(n, un, waits):
                            pe.wait_ge(xt_ready, un + 1)
                            if waits:
                                pe.wait_ge(add_done, un - B + 1)
                            for c in range(2):
                                last = pe.matmul(pz[n][:], xT[:, n, c, :], w[c], start=(c == 0), stop=(c == 1 and not constant))
                            if constant:
                                last = pe.matmul(pz[n][:], oneb[:], hsplit[:], start=False, stop=True)
                            last.then_inc(mm_done, 1)

                        def step(i, first, last):
                            for b in range(2):
                                for q in range(4):
                                    un = 8 * i + 4 * b + q
                                    if q == 0:
                                        pe.wait_ge(x_in[b], 16 * i + 16)
                                    if not (first and b == 0):
                                        pe.wait_ge(xt_ready, un - B + 1)
                                    pe.transpose(pT[q][:, 0, :], xin[:, b, q, 0:P], ident[:])
                                    pe.transpose(pT[q][:, 1, :], xin[:, b, q, P:F], ident[:]).then_inc(t_done, 1)
                                    if not (first and b == 0 and q == 0):
                                        product((q - 1) % 4, un - 1, not (first and 4 * b + q <= B))
                        ends(pe, step)
                        product(3, NT - 1, True)

                    @block.scalar
                    def _(act):
                        a = nc.scalar

                        def norm(g, b, q):
                            if q == 0:
                                act.wait_ge(rs_done, g + 1)
                            a.activation(o[:, b, q, :], t[:, b, q, :], ACT.Identity, bias=nm[:, b, q:q + 1], scale=rs[:, b, q:q + 1]).then_inc(ready, 1)

                        def deviation(g):
                            act.wait_ge(mv_done, 4 * (g + 1))
                            a.activation(sd[:], mv[:, :, 1], ACT.Sqrt, bias=epsc[:]).then_inc(sd_done, 1)

                        def step(i, at):
                            for b in range(2):
                                g = 2 * i + b
                                lag = not (at == 0 and b == 0)
                                for q in range(4):
                                    un = 8 * i + 4 * b + q
                                    act.wait_ge(t_done, un + 1)
                                    if lag:
                                        act.wait_ge(mm_done, un - B + 1)
                                    a.activation(xT[:, q, :, :], pT[q][:], ACT.Copy).then_inc(xt_ready, 1)
                                    if at != 0 and q < 2:
                                        norm(g - 2, b, q + 2)
                                    if lag and q == 1:
                                        deviation(g - 1)
                                    if lag and q >= 2:
                                        if q == 2 and at != 0 and not (at == 1 and b == 0):
                                            act.wait_ge(stored[1 - b], 16 * i if b == 1 else 16 * (i - 1))
                                        norm(g - 1, 1 - b, q - 2)
                        loop(act, step, 2)
                        norm(GROUPS - 2, 0, 2)
                        norm(GROUPS - 2, 0, 3)
                        deviation(GROUPS - 1)
                        act.wait_ge(stored[1], 16 * (GI - 1))
                        for q in range(4):
                            norm(GROUPS - 1, 1, q)

                    @block.vector
                    def _(dve):
                        v = nc.vector

                        def scales(g, b):
                            dve.wait_ge(sd_done, g + 1)
                            v.reciprocal(rs[:, b, :], sd[:]).then_inc(r_done, 1)
                            dve.wait_ge(r_done, g + 1)
                            v.scalar_tensor_tensor(nm[:, b, :], mv[:, :, 0], -1.0, rs[:, b, :], ALU.mult, ALU.mult).then_inc(rs_done, 1)

                        def step(i, first, last):
                            for b in range(2):
                                g = 2 * i + b
                                lag = not (first and b == 0)
                                for q in range(4):
                                    un = 8 * i + 4 * b + q
                                    if lag and q == 1:
                                        scales(g - 1, 1 - b)
                                    dve.wait_ge(mm_done, un + 1)
                                    if not first:
                                        dve.wait_ge(ready, un - 7)
                                    v.tensor_tensor(t[:, b, q, :], pz[q][:], xin[:, b, q, :], ALU.add).then_inc(add_done, 1)
                                    dve.wait_ge(add_done, un + 1)
                                    v.bn_stats(st[:, q, :], t[:, b, q, :]).then_inc(st_done, 1)
                                    if q >= 2:
                                        r = 2 * b + q - 2
                                        guest.dve(4 * i + r, r, i, 0 if first else None)
                                dve.wait_ge(st_done, 4 * (g + 1))
                                if lag:
                                    dve.wait_ge(rs_done, g)
                                v.memset(pad[:], 0.0)
                                for q in range(4):
                                    v.bn_aggr(mv[:, q, :], st[:, q, :]).then_inc(mv_done, 1)
                        ends(dve, step)
                        scales(GROUPS - 1, 1)

        class TileNorm:
            def __init__(self, c2, name):
                def tmp(x, shape):
                    return c2.enter_context(nc.sbuf_tensor(f"{name}_{x}", shape, F32))
                self.t, self.o = tmp("t", [P, RING, F]), tmp("o", [P, RING, F])
                self.st, self.mv = tmp("st", [P, RING, 6]), tmp("mv", [P, RING, 2])
                self.pad = tmp("pad", [P, 1])
                self.sd, self.rs, self.nm = tmp("sd", [P, RING]), tmp("rs", [P, RING]), tmp("nm", [P, RING])
                self.add_done, self.st_done, self.mv_done, self.sd_done, self.r_done, self.rs_done, self.ready = [
                    sem(f"{name}_{x}") for x in ("add", "stats", "mv", "sd", "r", "rs", "normed")]

            def add(self, dve, u, r, a, b, waits):
                if waits:
                    dve.wait_ge(self.ready, u - 3)
                nc.vector.tensor_tensor(self.t[:, r, :], a, b, ALU.add).then_inc(self.add_done, 1)

            def stats(self, dve, u, r):
                dve.wait_ge(self.add_done, u + 1)
                nc.vector.bn_stats(self.st[:, r, :], self.t[:, r, :]).then_inc(self.st_done, 1)

            def aggregate(self, dve, u, r):
                dve.wait_ge(self.st_done, u + 1)
                nc.vector.memset(self.pad[:], 0.0)
                nc.vector.bn_aggr(self.mv[:, r, :], self.st[:, r, :]).then_inc(self.mv_done, 1)

            def moments(self, dve, u, r, a, b, waits):
                self.add(dve, u, r, a, b, waits)
                self.stats(dve, u, r)
                self.aggregate(dve, u, r)

            def deviation(self, act, u, r):
                act.wait_ge(self.mv_done, u + 1)
                nc.scalar.activation(self.sd[:, r:r + 1], self.mv[:, r, 1:2], ACT.Sqrt, bias=epsc[:]).then_inc(self.sd_done, 1)

            def inverse(self, dve, u, r):
                dve.wait_ge(self.sd_done, u + 1)
                nc.vector.reciprocal(self.rs[:, r:r + 1], self.sd[:, r:r + 1]).then_inc(self.r_done, 1)

            def shift(self, dve, u, r):
                dve.wait_ge(self.r_done, u + 1)
                nc.vector.scalar_tensor_tensor(self.nm[:, r:r + 1], self.mv[:, r, 0:1], -1.0, self.rs[:, r:r + 1], ALU.mult, ALU.mult).then_inc(self.rs_done, 1)

            def scales(self, dve, u, r):
                self.inverse(dve, u, r)
                self.shift(dve, u, r)

            def normed(self, act, u, r):
                act.wait_ge(self.rs_done, u + 1)
                nc.scalar.activation(self.o[:, r, :], self.t[:, r, :], ACT.Identity, bias=self.nm[:, r:r + 1], scale=self.rs[:, r:r + 1]).then_inc(self.ready, 1)

        class NodeTiles:
            def __init__(self, c2, name, base):
                def tmp(x, shape):
                    return c2.enter_context(nc.sbuf_tensor(f"{name}_{x}", shape, F32))
                self.base = base
                self.zin, self.zT = tmp("zin", [P, RING, F]), tmp("zT", [P, RING, 2, P])
                self.ln = TileNorm(c2, name)
                self.pT = [c2.enter_context(nc.psum_tensor(f"{name}_pT{x}", [P, 2, P], F32)) for x in range(2)]
                self.pz = [c2.enter_context(nc.psum_tensor(f"{name}_pz{x}", [P, F], F32)) for x in range(2)]
                self.t_done, self.zt_ready, self.mm_done = [sem(f"{name}_{x}") for x in ("T", "zT", "mm")]
                self.z_in, self.stored = sems(f"{name}_in"), sems(f"{name}_st")
                self.src = zrow.rearrange("(u p) f -> u p f", p=P)
                self.dst = d["out"].rearrange("(u p) f -> u p f", p=P)

            def load(self, sp, u, r, at):
                if at != 0:
                    sp.wait_ge(self.ln.add_done, u - 3)
                sp.dma_start(self.zin[:, r, :], self.src[bass.ds(u + self.base, 1), :, :].rearrange("a p f -> (a p) f")).then_inc(self.z_in[r], 16)

            def store(self, sp, u, r):
                sp.wait_ge(self.ln.ready, u + 1)
                sp.dma_start(self.dst[bass.ds(u + self.base, 1), :, :].rearrange("a p f -> (a p) f"), self.ln.o[:, r, :]).then_inc(self.stored[r], 16)

            def all_stored(self, sp):
                for r in range(RING):
                    sp.wait_ge(self.stored[r], 16 * EI)

            def turn(self, pe, u, r, i, at):
                pe.wait_ge(self.z_in[r], 16 * i + 16)
                if not (at == 0 and r < 2):
                    pe.wait_ge(self.zt_ready, u - 1)
                for c in range(2):
                    last = pe.transpose(self.pT[r % 2][:, c, :], self.zin[:, r, P * c:P * c + P], ident[:])
                last.then_inc(self.t_done, 1)

            def product(self, pe, u, r, waits):
                pe.wait_ge(self.zt_ready, u + 1)
                if waits:
                    pe.wait_ge(self.ln.add_done, u - 1)
                for c in range(2):
                    last = pe.matmul(self.pz[r % 2][:], self.zT[:, r, c, :], kept_w[0][:, c, :], start=(c == 0), stop=(c == 1))
                last.then_inc(self.mm_done, 1)

            def turned(self, act, u, r, at):
                act.wait_ge(self.t_done, u + 1)
                if at != 0:
                    act.wait_ge(self.mm_done, u - 3)
                nc.scalar.activation(self.zT[:, r, :, :], self.pT[r % 2][:], ACT.Copy).then_inc(self.zt_ready, 1)

            def add(self, dve, u, r, waits):
                dve.wait_ge(self.mm_done, u + 1)
                self.ln.add(dve, u, r, self.pz[r % 2][:], self.zin[:, r, :], waits)

            def norm(self, act, u, r, waits):
                if waits is not None:
                    act.wait_ge(self.stored[r], waits)
                self.ln.normed(act, u, r)

        def slots_block():
            with ExitStack() as c2:
                def tmp(name, shape, dt=F32):
                    return c2.enter_context(nc.sbuf_tensor(f"s_{name}", shape, dt))
                yin, xd = tmp("yin", [P, RING, XW]), tmp("xd", [P, RING, F])
                xT, xTc = tmp("xT", [P, 2, F]), tmp("xTc", [4, 2, P])
                jring, kring = tmp("jring", [P, RING], I32), tmp("kring", [P, RING], I32)
                k_ready = sem("s_k")
                guest = table_scatter("sp", table2, hidx)(c2)
                ln = TileNorm(c2, "s_ln")
                begun = sem("s_begun")
                pT = [c2.enter_context(nc.psum_tensor(f"s_pT{x}", [P, 512], F32)) for x in range(2)]
                pz = [c2.enter_context(nc.psum_tensor(f"s_pz{x}", [P, F], F32)) for x in range(2)]
                idx_ready, t_done, xt_ready, mm_done = [sem(f"s_{x}") for x in ("idx", "T", "xT", "mm")]
                got, y_in, stored = sems("s_got"), sems("s_in"), sems("s_st")
                cv = cube.rearrange("(u p) f -> u p f", p=P)
                xv = xown.rearrange("(u p) f -> u p f", p=P)
                flat_ = "a p f -> (a p) f"
                with nc.Block() as block:
                    @block.sync
                    def _(sp):
                        def step(i, at):
                            for r in range(RING):
                                u = 4 * i + r
                                if at != 0:
                                    sp.wait_ge(t_done, u - 3)
                                sp.dma_start(yin[:, r, :], cv[bass.ds(u, 1), :, :].rearrange(flat_)).then_inc(y_in[r], 16)
                                if at != 0:
                                    sp.wait_ge(ln.add_done, u - 3)
                                sp.dma_start(xd[:, r, :], xv[bass.ds(u, 1), :, :].rearrange(flat_)).then_inc(got[r], 16)
                        loop(sp, step)

                    @block.gpsimd
                    def _(pool):
                        top = pool.to_reg(NPAD - 1)
                        guest.begin(pool)

                        def scatter(u, r):
                            pool.wait_ge(ln.ready, u + 1)
                            pool.wait_ge(k_ready, u + 1)
                            pool.sem_inc(begun, 1)
                            pool.indirect_dma_start(zrow, bass.IndirectOffsetOnAxis(ap=kring[:, r:r + 1], axis=0), ln.o[:, r, :], None,
                                                    bounds_check=top, oob_is_err=False).then_inc(stored[r], 16)

                        def step(i, at):
                            for r in range(RING):
                                u = 4 * i + r
                                if at != 0:
                                    scatter(u - 4, r)
                                guest.pool(pool, u, r, at)
                        loop(pool, step)
                        for u in range(ET - 4, ET):
                            scatter(u, u % 4)
                        for r in range(RING):
                            pool.wait_ge(stored[r], 16 * EI)
                        guest.end(pool)

                    @block.tensor
                    def _(pe):
                        def product(u, r, waits):
                            pe.wait_ge(xt_ready, 2 * (u + 1))
                            if waits:
                                pe.wait_ge(ln.add_done, u - 1)
                            p = pz[r % 2]
                            for c in range(2):
                                pe.matmul(p[:], xT[:, r % 2, P * c:P * c + P], hmap[c][:], start=(c == 0), stop=False)
                            pe.matmul(p[:], xTc[:, r % 2, :], hc[:], start=False, stop=True).then_inc(mm_done, 1)

                        def step(i, at):
                            for r in range(RING):
                                u = 4 * i + r
                                pe.wait_ge(y_in[r], 16 * i + 16)
                                if not (at == 0 and r < 2):
                                    pe.wait_ge(xt_ready, 2 * (u - 1))
                                p = pT[r % 2]
                                pe.transpose(p[:, 0:P], yin[:, r, 0:P], ident[:])
                                pe.transpose(p[:, P:F], yin[:, r, P:F], ident[:])
                                pe.transpose(p[0:4, F:F + P], yin[:, r, F:XW], ident[:]).then_inc(t_done, 1)
                                if not (at == 0 and r == 0):
                                    product(u - 1, (r - 1) % 4, not (at == 0 and r < 3))
                        loop(pe, step)
                        product(ET - 1, 3, True)

                    @block.scalar
                    def _(act):
                        def norm(u, r, waits):
                            if waits is not None:
                                act.wait_ge(stored[r], waits)
                            ln.normed(act, u, r)

                        def step(i, at):
                            for r in range(RING):
                                u = 4 * i + r
                                act.wait_ge(t_done, u + 1)
                                if not (at == 0 and r < 2):
                                    act.wait_ge(mm_done, u - 1)
                                nc.scalar.activation(xT[:, r % 2, :], pT[r % 2][:, 0:F], ACT.Copy).then_inc(xt_ready, 1)
                                nc.scalar.activation(xTc[:, r % 2, :], pT[r % 2][0:4, F:F + P], ACT.Copy).then_inc(xt_ready, 1)
                                if not (at == 0 and r < 3):
                                    ln.deviation(act, u - 3, (r - 3) % 4)
                                if at != 0:
                                    norm(u - 4, r, None if at == 1 else 16 * (i - 1))
                        loop(act, step, 2)
                        for u in range(ET - 3, ET):
                            ln.deviation(act, u, u % 4)
                        for u in range(ET - 4, ET):
                            norm(u, u % 4, 16 * (EI - 1))

                    @block.vector
                    def _(dve):
                        v = nc.vector
                        def finish(i, r, waits):
                            u = 4 * i + r
                            dve.wait_ge(mm_done, u + 1)
                            dve.wait_ge(got[r], 16 * i + 16)
                            ln.moments(dve, u, r, pz[r % 2][:], xd[:, r, :], waits)

                        def scales(u, r, waits):
                            ln.scales(dve, u, r)
                            if waits is not None:
                                dve.wait_ge(stored[r], waits)
                            copy(kring[:, r:r + 1], sidx[:, bass.ds(u, 1)]).then_inc(k_ready, 1)

                        def step(i, at):
                            for r in range(RING):
                                if not (at == 0 and r < 3):
                                    early = at == 0 or (at == 1 and r < 3)
                                    scales(4 * i + r - 3, (r - 3) % 4, None if early else (16 * (i - 1) if r < 3 else 16 * i))
                                finish(i, r, at != 0)
                                guest.dve(4 * i + r, r, i, at)
                        loop(dve, step, 2)
                        for u in range(ET - 3, ET):
                            scales(u, u % 4, 16 * (EI - 1))

        def hop_pass(k):
            table_of, rows = {1: (zrow, NPAD), 2: (hop1, NSLOT), 3: (hop2, NSLOT)}[k]
            idx, weight = (other, wK) if k == 1 else (idxh, w23)
            dest = None if k == 3 else (hop1, hop2)[k - 1].rearrange("(u p) f -> u p f", p=P)
            with ExitStack() as c2:
                def tmp(name, shape, dt=F32):
                    return c2.enter_context(nc.sbuf_tensor(f"h{k}_{name}", shape, dt))
                xs, h = tmp("xs", [P, RING, F]), tmp("h", [P, RING, F])
                mw, wcol = tmp("mw", [P, RING, P]), tmp("wcol", [P, ET])
                ps = [c2.enter_context(nc.psum_tensor(f"h{k}_ps{b}", [P, F], F32)) for b in range(RING)]
                s = lambda x: sem(f"h{k}_{x}")
                begun = s("begun")
                init, idx_ready, mw_ready, ps_ready, h_ready = s("init"), s("idx"), s("mw"), s("ps"), s("h")
                head_ready, carried, chain = s("head"), s("carried"), s("chain")
                got, stored = sems(f"h{k}_got"), sems(f"h{k}_st")
                flat_ = "a p f -> (a p) f"
                if k == 1:
                    guest = LookUp(c2, "lk2", table2)
                    far = tmp("far", [P, ET])
                if k < 3:
                    nodes = NodeTiles(c2, f"n{k}", (k - 1) * ET)
                else:
                    ins = tmp("ins", [P, RING, 3, F])
                    jring = tmp("jring", [P, RING], I32)
                    z_in, j_ready = sems("h3_zin"), s("j")
                    xT = tmp("xT", [P, RING, 8, P])
                    kring = tmp("kring", [P, RING], I32)
                    ln = TileNorm(c2, "o_ln")
                    pT = [c2.enter_context(nc.psum_tensor(f"h3_pT{b}", [P, 4, P], F32)) for b in range(2)]
                    pz = [c2.enter_context(nc.psum_tensor(f"h3_pz{b}", [P, F], F32)) for b in range(2)]
                    ta_done, tb_done, xa_ready, xb_ready, mm_done, k_ready = s("Ta"), s("Tb"), s("xa"), s("xb"), s("mm"), s("k")
                    in3 = sems("h3_in")
                    hops = [x.rearrange("(u p) f -> u p f", p=P) for x in (hop1, hop2)]
                with nc.Block() as block:
                    @block.gpsimd
                    def _(pool):
                        top = pool.to_reg(rows - 1)
                        out_top = pool.to_reg(NPAD - 1)
                        pool.wait_ge(init, 1)
                        if k == 1:
                            guest.begin(pool)

                        def scatter(u, r):
                            pool.wait_ge(ln.ready, u + 1)
                            pool.wait_ge(k_ready, u + 1)
                            pool.sem_inc(begun, 1)
                            pool.indirect_dma_start(d["out"], bass.IndirectOffsetOnAxis(ap=kring[:, r:r + 1], axis=0), ln.o[:, r, :], None,
                                                    bounds_check=out_top, oob_is_err=False).then_inc(stored[r], 16)

                        def step(i, at):
                            for r in range(RING):
                                u = 4 * i + r
                                if at != 0:
                                    pool.wait_ge(ps_ready, u - 3)
                                pool.wait_ge(idx_ready, u + 1)
                                pool.sem_inc(begun, 1)
                                pool.indirect_dma_start(xs[:, r, :], None, table_of, bass.IndirectOffsetOnAxis(ap=iring[:, r:r + 1], axis=0),
                                                        bounds_check=top, oob_is_err=False).then_inc(got[r], 16)
                                if k == 1:
                                    guest.pool(pool, u, r, at)
                                if k == 3:
                                    if at != 0:
                                        pool.wait_ge(ln.add_done, u - 3)
                                    pool.wait_ge(j_ready, u + 1)
                                    pool.sem_inc(begun, 1)
                                    pool.indirect_dma_start(ins[:, r, 0, :], None, zrow, bass.IndirectOffsetOnAxis(ap=jring[:, r:r + 1], axis=0),
                                                            bounds_check=out_top, oob_is_err=False).then_inc(z_in[r], 16)
                                if k == 3 and not (at == 0 or (at == 1 and r < 3)):
                                    scatter(u - 7, (r - 7) % 4)
                        loop(pool, step, 2 if k == 3 else 1)
                        if k == 3:
                            for u in range(ET - 7, ET):
                                scatter(u, u % 4)
                            for r in range(RING):
                                pool.wait_ge(stored[r], 16 * EI)

                    @block.sync
                    def _(sp):
                        if k < 3:
                            def step(i, at):
                                for r in range(RING):
                                    u = 4 * i + r
                                    nodes.load(sp, u, r, at)
                                    if not (at == 0 and r < 3):
                                        v = u - 3
                                        sp.wait_ge(h_ready, v + 1)
                                        sp.dma_start(dest[bass.ds(v, 1), :, :].rearrange(flat_), h[:, (r - 3) % 4, :]).then_inc(stored[(r - 3) % 4], 16)
                                    if at != 0 and not (at == 1 and r < 3):
                                        nodes.store(sp, u - 7, (r - 7) % 4)
                            loop(sp, step, 2)
                            for u in range(ET - 3, ET):
                                sp.wait_ge(h_ready, u + 1)
                                sp.dma_start(dest[u], h[:, u % 4, :]).then_inc(stored[u % 4], 16)
                            for u in range(ET - 7, ET):
                                nodes.store(sp, u, u % 4)
                            for r in range(RING):
                                sp.wait_ge(stored[r], 16 * EI)
                            nodes.all_stored(sp)
                        else:
                            def step(i, at):
                                for r in range(RING):
                                    u = 4 * i + r
                                    if at != 0:
                                        sp.wait_ge(tb_done, u - 3)
                                    for x in range(2):
                                        sp.dma_start(ins[:, r, 1 + x, :], hops[x][bass.ds(u, 1), :, :].rearrange(flat_)).then_inc(in3[r], 16)
                            loop(sp, step)

                    @block.scalar
                    def _(act):
                        def head(u, r, i):
                            act.wait_ge(got[r], 16 * i + 16)
                            nc.scalar.activation(xs[0:1, r, :], xs[0:1, r, :], ACT.Copy, scale=weight[0:1, bass.ds(u, 1)]).then_inc(head_ready, 1)

                        act.wait_ge(init, 1)
                        head(0, 0, 0)

                        def evacuate(u, r, i):
                            act.wait_ge(ps_ready, u + 1)
                            if i is not None:
                                if k == 3:
                                    act.wait_ge(tb_done, u - 3)
                                else:
                                    act.wait_ge(stored[r], 16 * i)
                            nc.scalar.activation(h[:, r, :], ps[r][:], ACT.Copy).then_inc(h_ready, 1)

                        def turned(u, r, waits):
                            act.wait_ge(tb_done, u + 1)
                            if waits:
                                act.wait_ge(mm_done, u - 3)
                            nc.scalar.activation(xT[:, r, 4:8, :], pT[1][:], ACT.Copy).then_inc(xb_ready, 1)

                        def norm(u, r, waits):
                            if waits is not None:
                                act.wait_ge(stored[r], waits)
                            ln.normed(act, u, r)

                        def step(i, at):
                            for r in range(RING):
                                u = 4 * i + r
                                if not (at == EI - 1 and r == 3):
                                    head(u + 1, (r + 1) % 4, i + (1 if r == 3 else 0))
                                if not (at == 0 and r == 0):
                                    act.wait_ge(carried, u)
                                    evacuate(u - 1, (r - 1) % 4, None if at == 0 or (at == 1 and r == 0) else i - (1 if r == 0 else 0))
                                if k < 3:
                                    nodes.turned(act, u, r, at)
                                    if not (at == 0 and r < 3):
                                        nodes.ln.deviation(act, u - 3, (r - 3) % 4)
                                    if at != 0:
                                        nodes.norm(act, u - 4, r, 16 * (i - 1) if at != 1 else None)
                                if k == 3:
                                    if not (at == 0 and r < 3):
                                        ln.deviation(act, u - 3, (r - 3) % 4)
                                    if at != 0:
                                        norm(u - 4, r, 16 * (i - 1) if at != 1 else None)
                                    if not (at == 0 and r == 0):
                                        turned(u - 1, (r - 1) % 4, not (at == 0 or (at == 1 and r == 0)))
                        loop(act, step, 2)
                        evacuate(ET - 1, 3, EI - 1)
                        if k < 3:
                            for u in range(ET - 3, ET):
                                nodes.ln.deviation(act, u, u % 4)
                            for u in range(ET - 4, ET):
                                nodes.norm(act, u, u % 4, 16 * (EI - 1))
                        if k == 3:
                            turned(ET - 1, 3, True)
                            for u in range(ET - 3, ET):
                                ln.deviation(act, u, u % 4)
                            for u in range(ET - 4, ET):
                                norm(u, u % 4, 16 * (EI - 1))

                    @block.tensor
                    def _(pe):
                        pe.wait_ge(init, 1)

                        def product(u, r, waits):
                            pe.wait_ge(xa_ready, u + 1)
                            pe.wait_ge(xb_ready, u + 1)
                            if waits:
                                pe.wait_ge(ln.add_done, u - 1)
                            for c in range(8):
                                last = pe.matmul(pz[r % 2][:], xT[:, r, c, :], kept_w[c // 2][:, c % 2, :], start=(c == 0), stop=(c == 7))
                            last.then_inc(mm_done, 1)

                        def turn_hop(u, r, waits):
                            if waits:
                                pe.wait_ge(xb_ready, u)
                            for c in range(2):
                                pe.transpose(pT[1][:, c, :], ins[:, r, 2, P * c:P * c + P], ident[:])
                            pe.wait_ge(h_ready, u + 1)
                            for c in range(2):
                                last = pe.transpose(pT[1][:, 2 + c, :], h[:, r, P * c:P * c + P], ident[:])
                            last.then_inc(tb_done, 1)

                        def step(i, at):
                            for r in range(RING):
                                u = 4 * i + r
                                pe.wait_ge(mw_ready, u + 1)
                                if at != 0:
                                    pe.wait_ge(h_ready, u - 3)
                                if at == 0 and r == 0:
                                    pe.wait_ge(head_ready, 1)
                                else:
                                    pe.wait_ge(carried, u)
                                pe.matmul(ps[r][:], mw[:, r, :], xs[:, r, :], start=True, stop=True).then_inc(ps_ready, 1)
                                if k < 3:
                                    nodes.turn(pe, u, r, i, at)
                                    if not (at == 0 and r == 0):
                                        nodes.product(pe, u - 1, (r - 1) % 4, not (at == 0 and r < 3))
                                if k == 3:
                                    pe.wait_ge(in3[r], 32 * i + 32)
                                    pe.wait_ge(z_in[r], 16 * i + 16)
                                    if not (at == 0 and r == 0):
                                        pe.wait_ge(xa_ready, u)
                                    for c in range(4):
                                        last = pe.transpose(pT[0][:, c, :], ins[:, r, c // 2, P * (c % 2):P * (c % 2) + P], ident[:])
                                    last.then_inc(ta_done, 1)
                                    if not (at == 0 and r < 2):
                                        product(u - 2, (r - 2) % 4, at != 0)
                                    if not (at == 0 and r == 0):
                                        turn_hop(u - 1, (r - 1) % 4, not (at == 0 and r == 1))
                        loop(pe, step)
                        if k < 3:
                            nodes.product(pe, ET - 1, 3, True)
                        if k == 3:
                            product(ET - 2, 2, True)
                            turn_hop(ET - 1, 3, True)
                            product(ET - 1, 3, True)

                    @block.vector
                    def _(dve):
                        v = nc.vector
                        v.memset(xs[:], 0.0).then_inc(init, 1)
                        link = linker(dve, chain)
                        carrying_weights(v, link, wcol, weight[:])

                        def prepare(u, r, first):
                            if not first:
                                dve.wait_ge(ps_ready, u - 3)
                            v.tensor_scalar(mw[:, r, :], same[:, bass.ds(u, 1), :].rearrange("p a j -> p (a j)"), wcol[:, bass.ds(u, 1)], None, ALU.mult).then_inc(mw_ready, 1)

                        def carry(u, r):
                            dve.wait_ge(head_ready, u + 1)
                            dve.wait_ge(ps_ready, u)
                            v.scalar_tensor_tensor(xs[0:1, r, :], ps[(r - 1) % 4][0:1, :], cflag[:, bass.ds(u - 1, 1)], xs[0:1, r, :],
                                                   ALU.mult, ALU.add).then_inc(carried, 1)

                        def add(u, r, waits):
                            dve.wait_ge(mm_done, u + 1)
                            ln.add(dve, u, r, pz[r % 2][:], ins[:, r, 0, :], waits)

                        def sums(u, r, stored_at):
                            ln.stats(dve, u, r)
                            ln.aggregate(dve, u, r)
                            if stored_at is not None:
                                dve.wait_ge(stored[r], stored_at)
                            copy(kring[:, r:r + 1], hidx[:, bass.ds(u, 1)]).then_inc(k_ready, 1)

                        for r in range(RING):
                            copy(iring[:, r:r + 1], idx[:, r:r + 1]).then_inc(idx_ready, 1)
                            if k == 3:
                                copy(jring[:, r:r + 1], dstJ[:, r:r + 1]).then_inc(j_ready, 1)
                        if k == 1:
                            guest.dve_begin()
                        for r in range(2):
                            prepare(r, r, True)

                        def step(i, at):
                            for r in range(RING):
                                u = 4 * i + r
                                if not (at == 0 and r == 0):
                                    carry(u, r)
                                if k < 3 and not (at == 0 and r < 2):
                                    nodes.add(dve, u - 2, (r - 2) % 4, not (at == 0 or (at == 1 and r < 2)))
                                if k == 3 and not (at == 0 and r < 3):
                                    add(u - 3, (r - 3) % 4, not (at == 0 or (at == 1 and r < 3)))
                                if not (at == EI - 1 and r >= 2):
                                    prepare(u + 2, (r + 2) % 4, at == 0 and r < 2)
                                if k < 3 and not (at == 0 and r < 2):
                                    nodes.ln.stats(dve, u - 2, (r - 2) % 4)
                                if k < 3 and at != 0:
                                    nodes.ln.inverse(dve, u - 4, r)
                                dve.wait_ge(got[r], 16 * i + 16)
                                copy(iring[:, r:r + 1], idx[:, bass.ds(u + RING, 1)]).then_inc(idx_ready, 1)
                                if k == 1:
                                    guest.dve(u, r, i)
                                if k < 3:
                                    if at != 0:
                                        nodes.ln.shift(dve, u - 4, r)
                                    if not (at == 0 and r < 2):
                                        nodes.ln.aggregate(dve, u - 2, (r - 2) % 4)
                                if k == 3:
                                    dve.wait_ge(z_in[r], 16 * i + 16)
                                    copy(jring[:, r:r + 1], dstJ[:, bass.ds(u + RING, 1)]).then_inc(j_ready, 1)
                                    if at != 0:
                                        ln.scales(dve, u - 4, r)
                                    if not (at == 0 and r < 3):
                                        sums(u - 3, (r - 3) % 4,
                                             None if at == 0 or (at == 1 and r < 3) else (16 * (i - 1) if r < 3 else 16 * i))
                                    dve.wait_ge(ta_done, u + 1)
                                    if at != 0:
                                        dve.wait_ge(mm_done, u - 3)
                                    v.tensor_copy(xT[:, r, 0:4, :], pT[0][:]).then_inc(xa_ready, 1)
                        loop(dve, step, 2)
                        if k < 3:
                            for u in (ET - 2, ET - 1):
                                nodes.add(dve, u, u % 4, True)
                                nodes.ln.stats(dve, u, u % 4)
                                nodes.ln.aggregate(dve, u, u % 4)
                            for u in range(ET - 4, ET):
                                nodes.ln.scales(dve, u, u % 4)
                        if k == 1:
                            guest.dve_end(dve)
                            link(v.tensor_scalar(far[:], edge[:, :, 0], float(NPAD), None, ALU.is_ge))
                            link(v.tensor_tensor(w23[:], wK[:], far[:], ALU.mult))
                            link(v.tensor_scalar(far[:], far[:], -FAR, FAR - NPAD, ALU.mult, ALU.add))
                            link(v.tensor_tensor(far[:], far[:], edge[:, :, 0], ALU.add))
                            link(v.tensor_copy(idxh[:, 0:ET], far[:]))
                        if k == 3:
                            for r in (1, 2, 3):
                                add(ET - 4 + r, r, True)
                                sums(ET - 4 + r, r, 16 * (EI - 1))
                            for u in range(ET - 4, ET):
                                ln.scales(dve, u, u % 4)

        load_block()
        end_of_block()
        out_of_order = nc.values_load(unsorted[0:1, 0:1], min_val=0, max_val=NSLOT)
        with nc.If(out_of_order > 0):
            rank_block("ds", d["dstK"], d["dstrow"], d["srcK"], d["wK"], None)
            end_of_block()
            scatter_block()
            end_of_block()
            sorted_block("db")
            end_of_block()
        structure_block("dt", table, True, sidx)
        end_of_block()
        rank_block("ss", d["skey"], d["skeyrow"], d["sother"], d["wK"], table_scatter("dp", table, sidx))
        end_of_block()
        node_gram_block()
        end_of_block()
        for k in (1, 2, 3):
            a_pass(k, gk[k - 1])
            end_of_block()
        norm_block()
        end_of_block()
        dense_block("z", d["x"], [hmap[0][:], hmap[1][:]], True, zrow)
        end_of_block()
        sorted_block("sb")
        end_of_block()
        structure_block("st", table2, False, hidx)
        end_of_block()
        slots_block()
        end_of_block()
        for k in (1, 2, 3):
            hop_pass(k)
            end_of_block()


def kernel(x, src, dst, edge_weight, L0_gnn_W1, L0_gnn_b1, L0_gnn_g1, L0_gnn_be1, L0_gnn_W2, L0_gnn_b2, L0_gnn_g2, L0_gnn_be2,
           L0_gnn_W3, L0_gnn_b3, L0_gnn_g3, L0_gnn_be3, L1_gnn_weight):
    import concourse.bacc as bacc
    from concourse.bass_utils import run_bass_kernel_spmd

    def padded(a, n, fill):
        return np.concatenate([a, np.full((n - a.shape[0],) + a.shape[1:], fill, a.dtype)])

    def tiles(a):
        return np.ascontiguousarray(a.reshape(ET, P)[::-1])

    x, src, dst, edge_weight = (np.asarray(a) for a in (x, src, dst, edge_weight))
    s, t, w = padded(src, NSLOT, 0), padded(dst, NSLOT, N), padded(edge_weight, NSLOT, 0)
    skey, sother = padded(src, NSLOT, N), padded(dst, NSLOT, 0)
    before = np.concatenate([np.full((1,), -1, t.dtype), t[:-1]])
    table0 = np.zeros((NPAD, 2), np.float32)
    table0[:, 0] = np.where(np.arange(NPAD) < N, np.arange(NPAD), 2 * NPAD)
    table0[:, 1] = 1.0

    def rows(a):
        return np.ascontiguousarray(tiles(a)[:, ::-1])

    def columns(a):
        return np.ascontiguousarray(rows(a).T)

    k, m = np.arange(P)[:, None], np.arange(P)[None, :]
    arrays = {
        "x": padded(x, NPAD, 0),
        "srcK": columns(s), "dstK": columns(t), "wK": columns(w), "dstrow": rows(t),
        "skey": columns(skey), "skeyrow": rows(skey), "sother": columns(sother),
        "dstJ": np.ascontiguousarray(tiles(t).T), "dprev": np.ascontiguousarray(tiles(before).T),
        "iota": np.ascontiguousarray(np.broadcast_to(np.arange(NPAD // P, dtype=np.float32), (P, NPAD // P))),
        "tri": (m < k).astype(np.float32), "triu": (k < m).astype(np.float32), "rev": (k + m == P - 1).astype(np.float32),
        "slots": np.ascontiguousarray((NPAD + np.arange(NSLOT, dtype=np.float32)).reshape(ET, P).T),
        "table0": table0, "ident": np.eye(P, dtype=np.float32), "ones": np.ones((P, P), np.float32),
        "e3": np.array([[0, 0, 0, 1]], np.float32), "e3c": np.array([[0], [0], [0], [1]], np.float32),
        "L1W": np.ascontiguousarray(np.asarray(L1_gnn_weight).transpose(2, 0, 1)),
    }
    for k, (W, b, g, be) in enumerate(((L0_gnn_W1, L0_gnn_b1, L0_gnn_g1, L0_gnn_be1), (L0_gnn_W2, L0_gnn_b2, L0_gnn_g2, L0_gnn_be2),
                                       (L0_gnn_W3, L0_gnn_b3, L0_gnn_g3, L0_gnn_be3)), 1):
        arrays[f"W{k}"] = np.asarray(W)
        for n, a in (("b", b), ("g", g), ("be", be)):
            arrays[f"{n}{k}"] = np.asarray(a)[None]
    nc = bacc.Bacc("TRN2", target_bir_lowering=False, num_devices=1)
    d = {n: nc.dram_tensor(f"in_{n}", a.shape, mybir.dt.from_np(a.dtype), kind="ExternalInput").ap() for n, a in arrays.items()}
    d["out"] = nc.dram_tensor("out_rows", (NPAD, F), F32, kind="ExternalOutput").ap()
    build_program(nc, d)
    r = run_bass_kernel_spmd(nc, [{f"in_{n}": a for n, a in arrays.items()}], core_ids=[0])
    return r.results[0]["out_rows"][:N]
```
